# Optimizing a Trainium2 kernel written in Bass

```python
import numpy as np
import jax
import jax.numpy as jnp

def _softmax(x, axis=-1):
    return jax.nn.softmax(x, axis=axis)

def _gelu(x):
    return jax.nn.gelu(x, approximate=True)

def _silu(x):
    return jax.nn.silu(x)

def _sigmoid(x):
    return jax.nn.sigmoid(x)

def _layernorm(x, axis=-1, eps=1e-05):
    m = jnp.mean(x, axis=axis, keepdims=True)
    v = jnp.var(x, axis=axis, keepdims=True)
    return (x - m) / jnp.sqrt(v + eps)

def _scatter_add(tgt, idx, src, axis=0):
    return tgt.at[idx].add(src)

def _segment_sum(src, seg, n):
    return jax.ops.segment_sum(src, seg, n)
kernel_name = 'mk_adaln_ffn_d4_seqx_r4_380158'

def setup_inputs(seed: int=0):
    np.random.seed(seed)
    _w = jnp.asarray

    def _rec_inputs():
        import jax
        import jax.numpy as jnp
        _rk = jax.random.key(seed)
        x = -0.0003929 + 0.9999 * jax.random.normal(jax.random.fold_in(_rk, 1), (32, 64, 1024), jnp.float32)
        _lenS = 64 - jax.random.randint(jax.random.fold_in(_rk, 7), (32,), 0, max(1, 64 // 4) + 1, jnp.int32)
        _lenS2 = 64 - jax.random.randint(jax.random.fold_in(_rk, 8), (32,), 0, max(1, 64 // 4) + 1, jnp.int32)
        cond_512 = 0.00782532 + 1.00527 * jax.random.normal(jax.random.fold_in(_rk, 11), (32, 128), jnp.float32)
        return (x, cond_512)
    x, cond_512 = _rec_inputs()

    def _L0_cond_setup():
        import jax, jax.numpy as jnp
        from jax import lax
        import numpy as np
        CIN, COUT, K, STYLE_DIM = (64, 64, 3, 128)
        N_LAYERS = 4
        TYPES = ('same', 'upsample', 'same', 'downsample')
        SCALE = 1.0 / float(np.sqrt(CIN * K ** 2))
        EPS = 1e-08
        _BK = np.array([1.0, 3.0, 3.0, 1.0], dtype=np.float32)
        BLUR_K = _BK / _BK.sum()

        def _blur(x, kern, pad):
            B, C, _ = x.shape
            xp = jnp.pad(x, ((0, 0), (0, 0), (pad[0], pad[1])))
            w = jnp.broadcast_to(kern.astype(x.dtype)[None, None, :], (C, 1, kern.shape[0]))
            return lax.conv_general_dilated(xp, w, (1,), 'VALID', feature_group_count=C, dimension_numbers=('NCH', 'OIH', 'NCH'))

        def _conv_same(x, w):
            p = (K - 1) // 2
            return lax.conv_general_dilated(x[None], w, (1,), [(p, p)], dimension_numbers=('NCH', 'OIH', 'NCH'))[0]

        def _conv_down(x, w):
            return lax.conv_general_dilated(x[None], w, (2,), 'VALID', dimension_numbers=('NCH', 'OIH', 'NCH'))[0]

        def _conv_up(x, w_t):
            return lax.conv_transpose(x[None], w_t, (2,), 'VALID', dimension_numbers=('NCH', 'IOH', 'NCH'), transpose_kernel=True)[0]

        def _layer(x, style, w, b, mw, mb, typ):
            s = style @ mw.T + mb
            weight = SCALE * w * s[:, None, :, None]
            demod = lax.rsqrt(jnp.sum(weight * weight, axis=(2, 3)) + EPS)
            weight = weight * demod[:, :, None, None]
            blur_k = jnp.asarray(BLUR_K)
            if typ == 'same':
                out = jax.vmap(_conv_same)(x, weight) + b[None, :, None]
            elif typ == 'upsample':
                out = jax.vmap(_conv_up)(x, weight.transpose(0, 2, 1, 3)) + b[None, :, None]
                out = _blur(out, 2.0 * blur_k, (1, 1))
            elif typ == 'downsample':
                xb = _blur(x, blur_k, (2, 2))
                out = jax.vmap(_conv_down)(xb, weight) + b[None, :, None]
            else:
                raise NotImplementedError(typ)
            return out
        key = jax.random.key(seed)
        ks = jax.random.split(key, 6)
        B, L = (16, 1024)
        return {'x': jax.random.normal(ks[0], (B, CIN, L), dtype=jnp.float32), 'style': jax.random.normal(ks[1], (B, STYLE_DIM), dtype=jnp.float32), 'weights': jax.random.normal(ks[2], (N_LAYERS, COUT, CIN, K), dtype=jnp.float32), 'biases': jax.random.normal(ks[3], (N_LAYERS, COUT), dtype=jnp.float32) * 0.1, 'mod_w': jax.random.normal(ks[4], (N_LAYERS, CIN, STYLE_DIM), dtype=jnp.float32) / np.sqrt(STYLE_DIM), 'mod_b': 1.0 + 0.1 * jax.random.normal(ks[5], (N_LAYERS, CIN), dtype=jnp.float32)}
    _L0_cond_all = _L0_cond_setup()
    _L0_cond_in = {k: v for k, v in _L0_cond_all.items() if k in ('weights', 'biases', 'mod_w', 'mod_b')}
    del _L0_cond_all

    def _L0_ffn_setup():
        import jax, jax.numpy as jnp
        import numpy as np
        ALPHA = 32
        R = 16
        SCALING = ALPHA / R
        key = jax.random.key(seed)
        k1, k2, k3, k4 = jax.random.split(key, 4)
        B_, S, D = (4, 512, 1024)
        H, r, O = (8, R, 1024)
        x = jax.random.normal(k1, (B_, S, D), dtype=jnp.float32)
        A = jax.random.normal(k2, (H, r, D), dtype=jnp.float32) * 0.02
        Bm = jax.random.normal(k3, (H, O, r), dtype=jnp.float32) * 0.02
        Wr = jax.random.normal(k4, (H, D), dtype=jnp.float32) * 0.02
        br = jnp.zeros((H,), dtype=jnp.float32)
        return {'x': x, 'A': A, 'B': Bm, 'Wr': Wr, 'br': br}
    _L0_ffn_all = _L0_ffn_setup()
    _L0_ffn_in = {k: v for k, v in _L0_ffn_all.items() if k in ('A', 'B', 'Wr', 'br')}
    del _L0_ffn_all

    def _L1_cond_setup():
        import jax, jax.numpy as jnp
        from jax import lax
        import numpy as np
        CIN, COUT, K, STYLE_DIM = (64, 64, 3, 128)
        N_LAYERS = 4
        TYPES = ('same', 'upsample', 'same', 'downsample')
        SCALE = 1.0 / float(np.sqrt(CIN * K ** 2))
        EPS = 1e-08
        _BK = np.array([1.0, 3.0, 3.0, 1.0], dtype=np.float32)
        BLUR_K = _BK / _BK.sum()

        def _blur(x, kern, pad):
            B, C, _ = x.shape
            xp = jnp.pad(x, ((0, 0), (0, 0), (pad[0], pad[1])))
            w = jnp.broadcast_to(kern.astype(x.dtype)[None, None, :], (C, 1, kern.shape[0]))
            return lax.conv_general_dilated(xp, w, (1,), 'VALID', feature_group_count=C, dimension_numbers=('NCH', 'OIH', 'NCH'))

        def _conv_same(x, w):
            p = (K - 1) // 2
            return lax.conv_general_dilated(x[None], w, (1,), [(p, p)], dimension_numbers=('NCH', 'OIH', 'NCH'))[0]

        def _conv_down(x, w):
            return lax.conv_general_dilated(x[None], w, (2,), 'VALID', dimension_numbers=('NCH', 'OIH', 'NCH'))[0]

        def _conv_up(x, w_t):
            return lax.conv_transpose(x[None], w_t, (2,), 'VALID', dimension_numbers=('NCH', 'IOH', 'NCH'), transpose_kernel=True)[0]

        def _layer(x, style, w, b, mw, mb, typ):
            s = style @ mw.T + mb
            weight = SCALE * w * s[:, None, :, None]
            demod = lax.rsqrt(jnp.sum(weight * weight, axis=(2, 3)) + EPS)
            weight = weight * demod[:, :, None, None]
            blur_k = jnp.asarray(BLUR_K)
            if typ == 'same':
                out = jax.vmap(_conv_same)(x, weight) + b[None, :, None]
            elif typ == 'upsample':
                out = jax.vmap(_conv_up)(x, weight.transpose(0, 2, 1, 3)) + b[None, :, None]
                out = _blur(out, 2.0 * blur_k, (1, 1))
            elif typ == 'downsample':
                xb = _blur(x, blur_k, (2, 2))
                out = jax.vmap(_conv_down)(xb, weight) + b[None, :, None]
            else:
                raise NotImplementedError(typ)
            return out
        key = jax.random.key(seed)
        ks = jax.random.split(key, 6)
        B, L = (16, 1024)
        return {'x': jax.random.normal(ks[0], (B, CIN, L), dtype=jnp.float32), 'style': jax.random.normal(ks[1], (B, STYLE_DIM), dtype=jnp.float32), 'weights': jax.random.normal(ks[2], (N_LAYERS, COUT, CIN, K), dtype=jnp.float32), 'biases': jax.random.normal(ks[3], (N_LAYERS, COUT), dtype=jnp.float32) * 0.1, 'mod_w': jax.random.normal(ks[4], (N_LAYERS, CIN, STYLE_DIM), dtype=jnp.float32) / np.sqrt(STYLE_DIM), 'mod_b': 1.0 + 0.1 * jax.random.normal(ks[5], (N_LAYERS, CIN), dtype=jnp.float32)}
    _L1_cond_all = _L1_cond_setup()
    _L1_cond_in = {k: v for k, v in _L1_cond_all.items() if k in ('weights', 'biases', 'mod_w', 'mod_b')}
    del _L1_cond_all

    def _L1_ffn_setup():
        import jax, jax.numpy as jnp
        import numpy as np
        B, T, D_IN, D_OUT = (8, 512, 1024, 1024)
        N_LORAS, RANK = (16, 32)
        SCALING = 1.0
        key = jax.random.key(seed)
        ks = jax.random.split(key, 8)
        std = 1.0 / D_IN ** 0.5
        x = jax.random.normal(ks[0], (B, T, D_IN), dtype=jnp.float32)
        idx = jax.random.randint(ks[1], (B,), 0, N_LORAS)
        gate = jax.nn.one_hot(idx, N_LORAS, dtype=jnp.float32)
        kernel = jax.random.normal(ks[2], (D_IN, D_OUT), dtype=jnp.float32) * std
        bias = jnp.zeros((D_OUT,), dtype=jnp.float32)
        lora_A = jax.random.normal(ks[3], (N_LORAS, RANK, D_IN), dtype=jnp.float32) * std
        lora_B = jax.random.normal(ks[4], (N_LORAS, D_OUT, RANK), dtype=jnp.float32) * 0.01
        lora_A_shared = jax.random.normal(ks[5], (RANK, D_IN), dtype=jnp.float32) * std
        lora_B_shared = jax.random.normal(ks[6], (D_OUT, RANK), dtype=jnp.float32) * 0.01
        return {'x': x, 'gate': gate, 'kernel': kernel, 'bias': bias, 'lora_A': lora_A, 'lora_B': lora_B, 'lora_A_shared': lora_A_shared, 'lora_B_shared': lora_B_shared}
    _L1_ffn_all = _L1_ffn_setup()
    _L1_ffn_in = {k: v for k, v in _L1_ffn_all.items() if k in ('gate', 'kernel', 'bias', 'lora_A', 'lora_B', 'lora_A_shared', 'lora_B_shared')}
    del _L1_ffn_all

    def _L2_cond_setup():
        import jax, jax.numpy as jnp
        from jax import lax
        import numpy as np
        CIN, COUT, K, STYLE_DIM = (64, 64, 3, 128)
        N_LAYERS = 4
        TYPES = ('same', 'upsample', 'same', 'downsample')
        SCALE = 1.0 / float(np.sqrt(CIN * K ** 2))
        EPS = 1e-08
        _BK = np.array([1.0, 3.0, 3.0, 1.0], dtype=np.float32)
        BLUR_K = _BK / _BK.sum()

        def _blur(x, kern, pad):
            B, C, _ = x.shape
            xp = jnp.pad(x, ((0, 0), (0, 0), (pad[0], pad[1])))
            w = jnp.broadcast_to(kern.astype(x.dtype)[None, None, :], (C, 1, kern.shape[0]))
            return lax.conv_general_dilated(xp, w, (1,), 'VALID', feature_group_count=C, dimension_numbers=('NCH', 'OIH', 'NCH'))

        def _conv_same(x, w):
            p = (K - 1) // 2
            return lax.conv_general_dilated(x[None], w, (1,), [(p, p)], dimension_numbers=('NCH', 'OIH', 'NCH'))[0]

        def _conv_down(x, w):
            return lax.conv_general_dilated(x[None], w, (2,), 'VALID', dimension_numbers=('NCH', 'OIH', 'NCH'))[0]

        def _conv_up(x, w_t):
            return lax.conv_transpose(x[None], w_t, (2,), 'VALID', dimension_numbers=('NCH', 'IOH', 'NCH'), transpose_kernel=True)[0]

        def _layer(x, style, w, b, mw, mb, typ):
            s = style @ mw.T + mb
            weight = SCALE * w * s[:, None, :, None]
            demod = lax.rsqrt(jnp.sum(weight * weight, axis=(2, 3)) + EPS)
            weight = weight * demod[:, :, None, None]
            blur_k = jnp.asarray(BLUR_K)
            if typ == 'same':
                out = jax.vmap(_conv_same)(x, weight) + b[None, :, None]
            elif typ == 'upsample':
                out = jax.vmap(_conv_up)(x, weight.transpose(0, 2, 1, 3)) + b[None, :, None]
                out = _blur(out, 2.0 * blur_k, (1, 1))
            elif typ == 'downsample':
                xb = _blur(x, blur_k, (2, 2))
                out = jax.vmap(_conv_down)(xb, weight) + b[None, :, None]
            else:
                raise NotImplementedError(typ)
            return out
        key = jax.random.key(seed)
        ks = jax.random.split(key, 6)
        B, L = (16, 1024)
        return {'x': jax.random.normal(ks[0], (B, CIN, L), dtype=jnp.float32), 'style': jax.random.normal(ks[1], (B, STYLE_DIM), dtype=jnp.float32), 'weights': jax.random.normal(ks[2], (N_LAYERS, COUT, CIN, K), dtype=jnp.float32), 'biases': jax.random.normal(ks[3], (N_LAYERS, COUT), dtype=jnp.float32) * 0.1, 'mod_w': jax.random.normal(ks[4], (N_LAYERS, CIN, STYLE_DIM), dtype=jnp.float32) / np.sqrt(STYLE_DIM), 'mod_b': 1.0 + 0.1 * jax.random.normal(ks[5], (N_LAYERS, CIN), dtype=jnp.float32)}
    _L2_cond_all = _L2_cond_setup()
    _L2_cond_in = {k: v for k, v in _L2_cond_all.items() if k in ('weights', 'biases', 'mod_w', 'mod_b')}
    del _L2_cond_all

    def _L2_ffn_setup():
        import jax, jax.numpy as jnp
        import numpy as np
        N_EXPERTS = 28
        TOP_K = 2
        RANK = 8
        LORA_ALPHA = 16
        SCALING = LORA_ALPHA / RANK
        TEMP = 1.0
        key = jax.random.key(seed)
        ks = jax.random.split(key, 5)
        B, S, D_IN, D_OUT = (4, 512, 1024, 1024)
        x = jax.random.normal(ks[0], (B, S, D_IN), dtype=jnp.float32)
        base_W = jax.random.normal(ks[1], (D_OUT, D_IN), dtype=jnp.float32) * (1.0 / np.sqrt(D_IN))
        gate_W = jax.random.normal(ks[2], (N_EXPERTS, D_IN), dtype=jnp.float32) * (1.0 / np.sqrt(D_IN))
        lora_A = jax.random.normal(ks[3], (N_EXPERTS, RANK, D_IN), dtype=jnp.float32) * (1.0 / np.sqrt(D_IN))
        lora_B = jax.random.normal(ks[4], (N_EXPERTS, D_OUT, RANK), dtype=jnp.float32) * 0.01
        return {'x': x, 'base_W': base_W, 'gate_W': gate_W, 'lora_A': lora_A, 'lora_B': lora_B}
    _L2_ffn_all = _L2_ffn_setup()
    _L2_ffn_in = {k: v for k, v in _L2_ffn_all.items() if k in ('base_W', 'gate_W', 'lora_A', 'lora_B')}
    del _L2_ffn_all

    def _L3_cond_setup():
        import jax, jax.numpy as jnp
        from jax import lax
        import numpy as np
        CIN, COUT, K, STYLE_DIM = (64, 64, 3, 128)
        N_LAYERS = 4
        TYPES = ('same', 'upsample', 'same', 'downsample')
        SCALE = 1.0 / float(np.sqrt(CIN * K ** 2))
        EPS = 1e-08
        _BK = np.array([1.0, 3.0, 3.0, 1.0], dtype=np.float32)
        BLUR_K = _BK / _BK.sum()

        def _blur(x, kern, pad):
            B, C, _ = x.shape
            xp = jnp.pad(x, ((0, 0), (0, 0), (pad[0], pad[1])))
            w = jnp.broadcast_to(kern.astype(x.dtype)[None, None, :], (C, 1, kern.shape[0]))
            return lax.conv_general_dilated(xp, w, (1,), 'VALID', feature_group_count=C, dimension_numbers=('NCH', 'OIH', 'NCH'))

        def _conv_same(x, w):
            p = (K - 1) // 2
            return lax.conv_general_dilated(x[None], w, (1,), [(p, p)], dimension_numbers=('NCH', 'OIH', 'NCH'))[0]

        def _conv_down(x, w):
            return lax.conv_general_dilated(x[None], w, (2,), 'VALID', dimension_numbers=('NCH', 'OIH', 'NCH'))[0]

        def _conv_up(x, w_t):
            return lax.conv_transpose(x[None], w_t, (2,), 'VALID', dimension_numbers=('NCH', 'IOH', 'NCH'), transpose_kernel=True)[0]

        def _layer(x, style, w, b, mw, mb, typ):
            s = style @ mw.T + mb
            weight = SCALE * w * s[:, None, :, None]
            demod = lax.rsqrt(jnp.sum(weight * weight, axis=(2, 3)) + EPS)
            weight = weight * demod[:, :, None, None]
            blur_k = jnp.asarray(BLUR_K)
            if typ == 'same':
                out = jax.vmap(_conv_same)(x, weight) + b[None, :, None]
            elif typ == 'upsample':
                out = jax.vmap(_conv_up)(x, weight.transpose(0, 2, 1, 3)) + b[None, :, None]
                out = _blur(out, 2.0 * blur_k, (1, 1))
            elif typ == 'downsample':
                xb = _blur(x, blur_k, (2, 2))
                out = jax.vmap(_conv_down)(xb, weight) + b[None, :, None]
            else:
                raise NotImplementedError(typ)
            return out
        key = jax.random.key(seed)
        ks = jax.random.split(key, 6)
        B, L = (16, 1024)
        return {'x': jax.random.normal(ks[0], (B, CIN, L), dtype=jnp.float32), 'style': jax.random.normal(ks[1], (B, STYLE_DIM), dtype=jnp.float32), 'weights': jax.random.normal(ks[2], (N_LAYERS, COUT, CIN, K), dtype=jnp.float32), 'biases': jax.random.normal(ks[3], (N_LAYERS, COUT), dtype=jnp.float32) * 0.1, 'mod_w': jax.random.normal(ks[4], (N_LAYERS, CIN, STYLE_DIM), dtype=jnp.float32) / np.sqrt(STYLE_DIM), 'mod_b': 1.0 + 0.1 * jax.random.normal(ks[5], (N_LAYERS, CIN), dtype=jnp.float32)}
    _L3_cond_all = _L3_cond_setup()
    _L3_cond_in = {k: v for k, v in _L3_cond_all.items() if k in ('weights', 'biases', 'mod_w', 'mod_b')}
    del _L3_cond_all

    def _L3_ffn_setup():
        import jax, jax.numpy as jnp
        import numpy as np
        NUM_EXPERTS = 8
        RANK = 32
        ALPHA = 16.0
        TOP_K = 2
        TEMPERATURE = 1.0
        GAMMA = 0.5
        SOFT_TOPK_TEMP = 0.5
        N_GRAM = 2
        EPS = 1e-06
        key = jax.random.key(seed)
        ks = jax.random.split(key, 6)
        d_in, d_out = (1024, 1024)
        Bsz, T = (4, 512)
        x = jax.random.normal(ks[0], (Bsz, T, d_in), dtype=jnp.float32)
        W = jax.random.normal(ks[1], (d_out, d_in), dtype=jnp.float32) / np.sqrt(d_in)
        b = jax.random.normal(ks[2], (d_out,), dtype=jnp.float32) * 0.01
        A = jax.random.normal(ks[3], (d_in, RANK), dtype=jnp.float32) / np.sqrt(d_in)
        Bmat = jax.random.normal(ks[4], (RANK, d_out), dtype=jnp.float32) * 0.01
        LiMEs = jax.random.normal(ks[5], (NUM_EXPERTS, RANK), dtype=jnp.float32) * 0.1
        return {'x': x, 'W': W, 'b': b, 'A': A, 'Bmat': Bmat, 'LiMEs': LiMEs}
    _L3_ffn_all = _L3_ffn_setup()
    _L3_ffn_in = {k: v for k, v in _L3_ffn_all.items() if k in ('W', 'b', 'A', 'Bmat', 'LiMEs')}
    del _L3_ffn_all
    return {'x': x, 'cond_512': cond_512, 'L0_cond_weights': _L0_cond_in['weights'], 'L0_cond_biases': _L0_cond_in['biases'], 'L0_cond_mod_w': _L0_cond_in['mod_w'], 'L0_cond_mod_b': _L0_cond_in['mod_b'], 'L0_ffn_A': _L0_ffn_in['A'], 'L0_ffn_B': _L0_ffn_in['B'], 'L0_ffn_Wr': _L0_ffn_in['Wr'], 'L0_ffn_br': _L0_ffn_in['br'], 'L1_cond_weights': _L1_cond_in['weights'], 'L1_cond_biases': _L1_cond_in['biases'], 'L1_cond_mod_w': _L1_cond_in['mod_w'], 'L1_cond_mod_b': _L1_cond_in['mod_b'], 'L1_ffn_gate': _L1_ffn_in['gate'], 'L1_ffn_kernel': _L1_ffn_in['kernel'], 'L1_ffn_bias': _L1_ffn_in['bias'], 'L1_ffn_lora_A': _L1_ffn_in['lora_A'], 'L1_ffn_lora_B': _L1_ffn_in['lora_B'], 'L1_ffn_lora_A_shared': _L1_ffn_in['lora_A_shared'], 'L1_ffn_lora_B_shared': _L1_ffn_in['lora_B_shared'], 'L2_cond_weights': _L2_cond_in['weights'], 'L2_cond_biases': _L2_cond_in['biases'], 'L2_cond_mod_w': _L2_cond_in['mod_w'], 'L2_cond_mod_b': _L2_cond_in['mod_b'], 'L2_ffn_base_W': _L2_ffn_in['base_W'], 'L2_ffn_gate_W': _L2_ffn_in['gate_W'], 'L2_ffn_lora_A': _L2_ffn_in['lora_A'], 'L2_ffn_lora_B': _L2_ffn_in['lora_B'], 'L3_cond_weights': _L3_cond_in['weights'], 'L3_cond_biases': _L3_cond_in['biases'], 'L3_cond_mod_w': _L3_cond_in['mod_w'], 'L3_cond_mod_b': _L3_cond_in['mod_b'], 'L3_ffn_W': _L3_ffn_in['W'], 'L3_ffn_b': _L3_ffn_in['b'], 'L3_ffn_A': _L3_ffn_in['A'], 'L3_ffn_Bmat': _L3_ffn_in['Bmat'], 'L3_ffn_LiMEs': _L3_ffn_in['LiMEs']}

def reference(x, cond_512, L0_cond_weights, L0_cond_biases, L0_cond_mod_w, L0_cond_mod_b, L0_ffn_A, L0_ffn_B, L0_ffn_Wr, L0_ffn_br, L1_cond_weights, L1_cond_biases, L1_cond_mod_w, L1_cond_mod_b, L1_ffn_gate, L1_ffn_kernel, L1_ffn_bias, L1_ffn_lora_A, L1_ffn_lora_B, L1_ffn_lora_A_shared, L1_ffn_lora_B_shared, L2_cond_weights, L2_cond_biases, L2_cond_mod_w, L2_cond_mod_b, L2_ffn_base_W, L2_ffn_gate_W, L2_ffn_lora_A, L2_ffn_lora_B, L3_cond_weights, L3_cond_biases, L3_cond_mod_w, L3_cond_mod_b, L3_ffn_W, L3_ffn_b, L3_ffn_A, L3_ffn_Bmat, L3_ffn_LiMEs):
    import jax
    import jax.numpy as jnp

    def _L0_cond_ref(x, style, weights, biases, mod_w, mod_b):
        import jax, jax.numpy as jnp
        from jax import lax
        import numpy as np
        CIN, COUT, K, STYLE_DIM = (64, 64, 3, 128)
        N_LAYERS = 4
        TYPES = ('same', 'upsample', 'same', 'downsample')
        SCALE = 1.0 / float(np.sqrt(CIN * K ** 2))
        EPS = 1e-08
        _BK = np.array([1.0, 3.0, 3.0, 1.0], dtype=np.float32)
        BLUR_K = _BK / _BK.sum()

        def _blur(x, kern, pad):
            B, C, _ = x.shape
            xp = jnp.pad(x, ((0, 0), (0, 0), (pad[0], pad[1])))
            w = jnp.broadcast_to(kern.astype(x.dtype)[None, None, :], (C, 1, kern.shape[0]))
            return lax.conv_general_dilated(xp, w, (1,), 'VALID', feature_group_count=C, dimension_numbers=('NCH', 'OIH', 'NCH'))

        def _conv_same(x, w):
            p = (K - 1) // 2
            return lax.conv_general_dilated(x[None], w, (1,), [(p, p)], dimension_numbers=('NCH', 'OIH', 'NCH'))[0]

        def _conv_down(x, w):
            return lax.conv_general_dilated(x[None], w, (2,), 'VALID', dimension_numbers=('NCH', 'OIH', 'NCH'))[0]

        def _conv_up(x, w_t):
            return lax.conv_transpose(x[None], w_t, (2,), 'VALID', dimension_numbers=('NCH', 'IOH', 'NCH'), transpose_kernel=True)[0]

        def _layer(x, style, w, b, mw, mb, typ):
            s = style @ mw.T + mb
            weight = SCALE * w * s[:, None, :, None]
            demod = lax.rsqrt(jnp.sum(weight * weight, axis=(2, 3)) + EPS)
            weight = weight * demod[:, :, None, None]
            blur_k = jnp.asarray(BLUR_K)
            if typ == 'same':
                out = jax.vmap(_conv_same)(x, weight) + b[None, :, None]
            elif typ == 'upsample':
                out = jax.vmap(_conv_up)(x, weight.transpose(0, 2, 1, 3)) + b[None, :, None]
                out = _blur(out, 2.0 * blur_k, (1, 1))
            elif typ == 'downsample':
                xb = _blur(x, blur_k, (2, 2))
                out = jax.vmap(_conv_down)(xb, weight) + b[None, :, None]
            else:
                raise NotImplementedError(typ)
            return out
        out = x
        for i, typ in enumerate(TYPES):
            out = _layer(out, style, weights[i], biases[i], mod_w[i], mod_b[i], typ)
        return out

    def _L0_ffn_ref(x, A, B, Wr, br):
        import jax, jax.numpy as jnp
        import numpy as np
        ALPHA = 32
        R = 16
        SCALING = ALPHA / R
        H = A.shape[0]
        router_logits = jnp.einsum('bsd,hd->bsh', x, Wr) + br
        scores = H * jax.nn.softmax(router_logits, axis=-1)
        low = jnp.einsum('bsd,hrd->bshr', x, A)
        out = jnp.einsum('bshr,hor,bsh->bso', low, B, scores)
        return SCALING * out

    def _L1_cond_ref(x, style, weights, biases, mod_w, mod_b):
        import jax, jax.numpy as jnp
        from jax import lax
        import numpy as np
        CIN, COUT, K, STYLE_DIM = (64, 64, 3, 128)
        N_LAYERS = 4
        TYPES = ('same', 'upsample', 'same', 'downsample')
        SCALE = 1.0 / float(np.sqrt(CIN * K ** 2))
        EPS = 1e-08
        _BK = np.array([1.0, 3.0, 3.0, 1.0], dtype=np.float32)
        BLUR_K = _BK / _BK.sum()

        def _blur(x, kern, pad):
            B, C, _ = x.shape
            xp = jnp.pad(x, ((0, 0), (0, 0), (pad[0], pad[1])))
            w = jnp.broadcast_to(kern.astype(x.dtype)[None, None, :], (C, 1, kern.shape[0]))
            return lax.conv_general_dilated(xp, w, (1,), 'VALID', feature_group_count=C, dimension_numbers=('NCH', 'OIH', 'NCH'))

        def _conv_same(x, w):
            p = (K - 1) // 2
            return lax.conv_general_dilated(x[None], w, (1,), [(p, p)], dimension_numbers=('NCH', 'OIH', 'NCH'))[0]

        def _conv_down(x, w):
            return lax.conv_general_dilated(x[None], w, (2,), 'VALID', dimension_numbers=('NCH', 'OIH', 'NCH'))[0]

        def _conv_up(x, w_t):
            return lax.conv_transpose(x[None], w_t, (2,), 'VALID', dimension_numbers=('NCH', 'IOH', 'NCH'), transpose_kernel=True)[0]

        def _layer(x, style, w, b, mw, mb, typ):
            s = style @ mw.T + mb
            weight = SCALE * w * s[:, None, :, None]
            demod = lax.rsqrt(jnp.sum(weight * weight, axis=(2, 3)) + EPS)
            weight = weight * demod[:, :, None, None]
            blur_k = jnp.asarray(BLUR_K)
            if typ == 'same':
                out = jax.vmap(_conv_same)(x, weight) + b[None, :, None]
            elif typ == 'upsample':
                out = jax.vmap(_conv_up)(x, weight.transpose(0, 2, 1, 3)) + b[None, :, None]
                out = _blur(out, 2.0 * blur_k, (1, 1))
            elif typ == 'downsample':
                xb = _blur(x, blur_k, (2, 2))
                out = jax.vmap(_conv_down)(xb, weight) + b[None, :, None]
            else:
                raise NotImplementedError(typ)
            return out
        out = x
        for i, typ in enumerate(TYPES):
            out = _layer(out, style, weights[i], biases[i], mod_w[i], mod_b[i], typ)
        return out

    def _L1_ffn_ref(x, gate, kernel, bias, lora_A, lora_B, lora_A_shared, lora_B_shared):
        import jax, jax.numpy as jnp
        import numpy as np
        B, T, D_IN, D_OUT = (8, 512, 1024, 1024)
        N_LORAS, RANK = (16, 32)
        SCALING = 1.0
        base_out = jnp.matmul(x, kernel) + bias
        b = gate.shape[0]
        x_flat = x.reshape(b, -1, x.shape[-1])
        A_eff = jnp.einsum('bn,nri->bri', gate, lora_A)
        B_eff = jnp.einsum('bn,nor->bor', gate, lora_B)
        Ax = jnp.einsum('bri,bti->btr', A_eff, x_flat)
        delta_flat = jnp.einsum('bor,btr->bto', B_eff, Ax)
        Ax_s = jnp.einsum('ri,bti->btr', lora_A_shared, x_flat)
        delta_flat = delta_flat + jnp.einsum('or,btr->bto', lora_B_shared, Ax_s)
        delta = delta_flat.reshape(x.shape[:-1] + (kernel.shape[-1],))
        return base_out + (SCALING * delta).astype(base_out.dtype)

    def _L2_cond_ref(x, style, weights, biases, mod_w, mod_b):
        import jax, jax.numpy as jnp
        from jax import lax
        import numpy as np
        CIN, COUT, K, STYLE_DIM = (64, 64, 3, 128)
        N_LAYERS = 4
        TYPES = ('same', 'upsample', 'same', 'downsample')
        SCALE = 1.0 / float(np.sqrt(CIN * K ** 2))
        EPS = 1e-08
        _BK = np.array([1.0, 3.0, 3.0, 1.0], dtype=np.float32)
        BLUR_K = _BK / _BK.sum()

        def _blur(x, kern, pad):
            B, C, _ = x.shape
            xp = jnp.pad(x, ((0, 0), (0, 0), (pad[0], pad[1])))
            w = jnp.broadcast_to(kern.astype(x.dtype)[None, None, :], (C, 1, kern.shape[0]))
            return lax.conv_general_dilated(xp, w, (1,), 'VALID', feature_group_count=C, dimension_numbers=('NCH', 'OIH', 'NCH'))

        def _conv_same(x, w):
            p = (K - 1) // 2
            return lax.conv_general_dilated(x[None], w, (1,), [(p, p)], dimension_numbers=('NCH', 'OIH', 'NCH'))[0]

        def _conv_down(x, w):
            return lax.conv_general_dilated(x[None], w, (2,), 'VALID', dimension_numbers=('NCH', 'OIH', 'NCH'))[0]

        def _conv_up(x, w_t):
            return lax.conv_transpose(x[None], w_t, (2,), 'VALID', dimension_numbers=('NCH', 'IOH', 'NCH'), transpose_kernel=True)[0]

        def _layer(x, style, w, b, mw, mb, typ):
            s = style @ mw.T + mb
            weight = SCALE * w * s[:, None, :, None]
            demod = lax.rsqrt(jnp.sum(weight * weight, axis=(2, 3)) + EPS)
            weight = weight * demod[:, :, None, None]
            blur_k = jnp.asarray(BLUR_K)
            if typ == 'same':
                out = jax.vmap(_conv_same)(x, weight) + b[None, :, None]
            elif typ == 'upsample':
                out = jax.vmap(_conv_up)(x, weight.transpose(0, 2, 1, 3)) + b[None, :, None]
                out = _blur(out, 2.0 * blur_k, (1, 1))
            elif typ == 'downsample':
                xb = _blur(x, blur_k, (2, 2))
                out = jax.vmap(_conv_down)(xb, weight) + b[None, :, None]
            else:
                raise NotImplementedError(typ)
            return out
        out = x
        for i, typ in enumerate(TYPES):
            out = _layer(out, style, weights[i], biases[i], mod_w[i], mod_b[i], typ)
        return out

    def _L2_ffn_ref(x, base_W, gate_W, lora_A, lora_B):
        import jax, jax.numpy as jnp
        import numpy as np
        N_EXPERTS = 28
        TOP_K = 2
        RANK = 8
        LORA_ALPHA = 16
        SCALING = LORA_ALPHA / RANK
        TEMP = 1.0
        B, S, D_in = x.shape
        xf = x.reshape(B * S, D_in)
        base = xf @ base_W.T
        logits = xf @ gate_W.T
        top_vals, top_idx = jax.lax.top_k(logits, TOP_K)
        top_probs = jax.nn.softmax(top_vals / TEMP, axis=-1)
        N = xf.shape[0]
        gate_full = jnp.zeros((N, N_EXPERTS), dtype=xf.dtype).at[jnp.arange(N)[:, None], top_idx].add(top_probs)
        h = jnp.einsum('nd,erd->ner', xf, lora_A)
        h = h * (gate_full * SCALING)[:, :, None]
        lora_out = jnp.einsum('ner,eor->no', h, lora_B)
        out = base + lora_out
        return out.reshape(B, S, -1)

    def _L3_cond_ref(x, style, weights, biases, mod_w, mod_b):
        import jax, jax.numpy as jnp
        from jax import lax
        import numpy as np
        CIN, COUT, K, STYLE_DIM = (64, 64, 3, 128)
        N_LAYERS = 4
        TYPES = ('same', 'upsample', 'same', 'downsample')
        SCALE = 1.0 / float(np.sqrt(CIN * K ** 2))
        EPS = 1e-08
        _BK = np.array([1.0, 3.0, 3.0, 1.0], dtype=np.float32)
        BLUR_K = _BK / _BK.sum()

        def _blur(x, kern, pad):
            B, C, _ = x.shape
            xp = jnp.pad(x, ((0, 0), (0, 0), (pad[0], pad[1])))
            w = jnp.broadcast_to(kern.astype(x.dtype)[None, None, :], (C, 1, kern.shape[0]))
            return lax.conv_general_dilated(xp, w, (1,), 'VALID', feature_group_count=C, dimension_numbers=('NCH', 'OIH', 'NCH'))

        def _conv_same(x, w):
            p = (K - 1) // 2
            return lax.conv_general_dilated(x[None], w, (1,), [(p, p)], dimension_numbers=('NCH', 'OIH', 'NCH'))[0]

        def _conv_down(x, w):
            return lax.conv_general_dilated(x[None], w, (2,), 'VALID', dimension_numbers=('NCH', 'OIH', 'NCH'))[0]

        def _conv_up(x, w_t):
            return lax.conv_transpose(x[None], w_t, (2,), 'VALID', dimension_numbers=('NCH', 'IOH', 'NCH'), transpose_kernel=True)[0]

        def _layer(x, style, w, b, mw, mb, typ):
            s = style @ mw.T + mb
            weight = SCALE * w * s[:, None, :, None]
            demod = lax.rsqrt(jnp.sum(weight * weight, axis=(2, 3)) + EPS)
            weight = weight * demod[:, :, None, None]
            blur_k = jnp.asarray(BLUR_K)
            if typ == 'same':
                out = jax.vmap(_conv_same)(x, weight) + b[None, :, None]
            elif typ == 'upsample':
                out = jax.vmap(_conv_up)(x, weight.transpose(0, 2, 1, 3)) + b[None, :, None]
                out = _blur(out, 2.0 * blur_k, (1, 1))
            elif typ == 'downsample':
                xb = _blur(x, blur_k, (2, 2))
                out = jax.vmap(_conv_down)(xb, weight) + b[None, :, None]
            else:
                raise NotImplementedError(typ)
            return out
        out = x
        for i, typ in enumerate(TYPES):
            out = _layer(out, style, weights[i], biases[i], mod_w[i], mod_b[i], typ)
        return out

    def _L3_ffn_ref(x, W, b, A, Bmat, LiMEs):
        import jax, jax.numpy as jnp
        import numpy as np
        NUM_EXPERTS = 8
        RANK = 32
        ALPHA = 16.0
        TOP_K = 2
        TEMPERATURE = 1.0
        GAMMA = 0.5
        SOFT_TOPK_TEMP = 0.5
        N_GRAM = 2
        EPS = 1e-06
        Bsz, T, d_in = x.shape
        E = LiMEs.shape[0]
        scaling = ALPHA / RANK
        H = jnp.einsum('btd,od->bto', x, W) + b
        z = jnp.einsum('btd,dr->btr', x, A)
        anchors = jnp.arange(N_GRAM - 1, T, N_GRAM)
        H_slice = H[:, anchors, :E]
        delta_slice = jnp.einsum('bar,er->bae', z[:, anchors], LiMEs)
        H_scale = jnp.maximum(jnp.max(jnp.abs(H_slice)), EPS)
        d_scale = jnp.maximum(jnp.max(jnp.abs(delta_slice)), EPS)
        logits = ((1.0 - GAMMA) * (H_slice / H_scale) + GAMMA * (delta_slice / d_scale)) / TEMPERATURE
        probs = jax.nn.softmax(logits, axis=-1)
        topk_vals, _ = jax.lax.top_k(probs, TOP_K)
        thresh = topk_vals[..., -1:]
        mask = jax.nn.sigmoid((probs - thresh) / SOFT_TOPK_TEMP)
        weights = probs * mask
        weights = weights / (jnp.sum(weights, axis=-1, keepdims=True) + 1e-09)
        weights_full = jnp.repeat(weights, N_GRAM, axis=1)
        p_mix = jnp.einsum('bte,er->btr', weights_full, LiMEs)
        delta = jnp.einsum('btr,ro->bto', z * p_mix, Bmat) * scaling
        return H + delta
    x = x + _L0_ffn_ref(_L0_cond_ref(x, cond_512, L0_cond_weights, L0_cond_biases, L0_cond_mod_w, L0_cond_mod_b), L0_ffn_A, L0_ffn_B, L0_ffn_Wr, L0_ffn_br)
    x = x + _L1_ffn_ref(_L1_cond_ref(x, cond_512, L1_cond_weights, L1_cond_biases, L1_cond_mod_w, L1_cond_mod_b), L1_ffn_gate, L1_ffn_kernel, L1_ffn_bias, L1_ffn_lora_A, L1_ffn_lora_B, L1_ffn_lora_A_shared, L1_ffn_lora_B_shared)
    x = x + _L2_ffn_ref(_L2_cond_ref(x, cond_512, L2_cond_weights, L2_cond_biases, L2_cond_mod_w, L2_cond_mod_b), L2_ffn_base_W, L2_ffn_gate_W, L2_ffn_lora_A, L2_ffn_lora_B)
    x = x + _L3_ffn_ref(_L3_cond_ref(x, cond_512, L3_cond_weights, L3_cond_biases, L3_cond_mod_w, L3_cond_mod_b), L3_ffn_W, L3_ffn_b, L3_ffn_A, L3_ffn_Bmat, L3_ffn_LiMEs)
    return x

_drawn_inputs = setup_inputs


def setup_inputs(seed=0):
    import zlib

    import numpy as np

    out = dict(_drawn_inputs(seed))
    spreads = {'L0_ffn_br': (0.0, 0.1), 'L1_ffn_bias': (0.0, 0.1)}
    factors = {'L2_ffn_gate_W': 3.142,
     'L2_ffn_lora_A': 3.043,
     'L2_ffn_lora_B': 3.022,
     'L3_ffn_b': 8.0,
     'L3_ffn_A': 8.0,
     'L3_ffn_Bmat': 8.0,
     'L3_ffn_LiMEs': 8.0}
    for name, (base, spread) in spreads.items():
        noise = np.random.default_rng([zlib.crc32(name.encode()), seed]).standard_normal(out[name].shape)
        drawn = base * np.exp(spread * noise) if base else spread * noise
        out[name] = jnp.asarray(drawn.astype(out[name].dtype))
    for name, factor in factors.items():
        out[name] = (out[name] * factor).astype(out[name].dtype)
    return out
```

```python
from contextlib import ExitStack

import concourse.bass as bass
from concourse import mybir

F32 = mybir.dt.float32
F32R = mybir.dt.float32r
U32 = mybir.dt.uint32
ACT = mybir.ActivationFunctionType
ALU = mybir.AluOpType
AX_X = mybir.AxisListType.X
RMAX = bass.bass_isa.ReduceOp.max
ds = bass.ds

LAYERS = 4
STOP_AFTER = 4
P = 128
B, C, L = 32, 64, 1024
M = L // 2
PAIRS = B // 2
GROUPS = PAIRS // 2
KB = L // P
STYLE = 128
TAPS = 3
CONV_SCALE = 1.0 / float((C * TAPS ** 2) ** 0.5)
DEMOD_EPS = 1e-8
S0, G1, G2, G3, DS, CB, BT1, BT2, BT3 = range(9)
NMOD = 9
EDGE_OPS = 10
PROJ_W = (136, 64, 252, 32)
Z_OPS = (5, 1, 16, 1)


def build(nc, a, out):
    ctx = ExitStack()
    with ctx:
        def sb(name, shape, dt=F32, stack=ctx):
            return stack.enter_context(nc.sbuf_tensor(name, shape, dt))

        def sem(name):
            return ctx.enter_context(nc.semaphore(name))

        def f(t):
            return t.bitcast(F32)

        if STOP_AFTER == LAYERS:
            xs = nc.dram_tensor("x_state", (B, C, 2, M), F32, kind="Internal").ap()
        else:
            xs = out
        xs_rows = xs.rearrange("(n s) c h m -> n (s c) (h m)", s=2)
        xs_conv = xs.rearrange("(n s) c h m -> h n c s m", s=2)
        xs_edge = xs.rearrange("(g s) c h m -> g h c s m", s=4)
        x_rows = a["x"].rearrange("(n s) c l -> n (s c) l", s=2)
        x_conv = a["x"].rearrange("(n s) c l -> n c s l", s=2)
        x_edge = a["x"].rearrange("(g s) c l -> g c s l", s=4)

        mixed_a_dram = nc.dram_tensor("mixed_a_dram", (GROUPS, P, KB * 32), F32, kind="Internal").ap()
        mixed_b_dram = nc.dram_tensor("mixed_b_dram", (GROUPS, 32, L), F32, kind="Internal").ap()
        out_rows = out.rearrange("(n s) c l -> n (s c) l", s=2) if STOP_AFTER == LAYERS else None

        with ExitStack() as area:
            mix_a = sb("mix_a", [P, 4, L], stack=area)
            mix_b = sb("mix_b", [P, 8, 16, 32], stack=area)
            mix_bt = sb("mix_bt", [P, 4, L], stack=area)
            gate_col = sb("gate_col", [P, 32], stack=area)
            same_rank = sb("same_rank", [P, 32], stack=area)
            gate_mat = sb("gate_mat", [P, 4, 8, 32], stack=area)
            mixed_a = sb("mixed_a", [P, 8, KB, 32], stack=area)
            mixed_b = mix_b[:].rearrange("p o n r -> p (o n r)")[:, 0:2 * L].rearrange("p (t o) -> p t o", t=2)
        with ExitStack() as area:
            zp_hi = sb("zp_hi", [32, B * C], F32R, stack=area)
            zp_lo = sb("zp_lo", [32, B * C], F32R, stack=area)
            bm_hi = sb("bm_hi", [32, L], F32R, stack=area)
            bm_lo = sb("bm_lo", [32, L], F32R, stack=area)
            w_T = sb("w_T", [8, B * C], stack=area)
            route = sb("route", [P, 9, P], stack=area)
            d_slice = sb("d_slice", [P, PAIRS, 8], stack=area)
            col = sb("col", [P, 4, PAIRS], stack=area)
            maxes = sb("maxes", [P, 8], stack=area)
            odd = sb("odd", [P, 1], stack=area)
            to_anchor = sb("to_anchor", [P, P], stack=area)
            limes_T = sb("limes_T", [32, 8], stack=area)
        w_hi = sb("w_hi", [P, KB, L], F32R)
        w_lo = sb("w_lo", [P, KB, L], F32R)
        with ExitStack() as area:
            nat_b = sb("nat_b", [P, 8, 224], stack=area)
            wsq_tmp = sb("wsq_tmp", [C, 4, C * TAPS], stack=area)
            scaled = sb("scaled", [P, 2, TAPS, C], stack=area)
            pair_sum = sb("pair_sum", [P, 2, 2, C], stack=area)
            down_nat = sb("down_nat", [P, TAPS, 2, C], stack=area)
            mod_w_nat = sb("mod_w_nat", [C, 4, STYLE], stack=area)
            mod_w_T = sb("mod_w_T", [STYLE, 4, 2, C], stack=area)
            wsq_nat = sb("wsq_nat", [C, 4, C], stack=area)
            wsq_T = sb("wsq_T", [C, 4, 2, C], stack=area)
            var = sb("var", [P, 4, B], stack=area)
            std = sb("std", [P, 4, B], stack=area)
            newton = sb("newton", [P, 4, B], stack=area)
        gw = [[sb(f"gw{q}{r}", [P, 4, C], F32R) for r in "hl"] for q in range(2)]
        gu = [[sb(f"gu{q}{r}", [P, TAPS, C], F32R) for r in "hl"] for q in range(2)]
        fb = [[sb(f"fb{q}{r}", [P, 5, C], F32R) for r in "hl"] for q in range(2)]
        y_nat = [sb(f"y_nat{q}", [P, M]) for q in range(2)]
        y_hi = sb("y_hi", [P, KB, P], F32R)
        y_lo = sb("y_lo", [P, KB, P], F32R)
        ident = sb("ident", [P, P])
        w_nat = sb("w_nat", [P, 4, C * TAPS])
        mod_b_col = sb("mod_b_col", [P, 4])
        bias_col = sb("bias_col", [P, 4])
        style_nat = sb("style_nat", [B, STYLE])
        up_st = sb("up_st", [P, TAPS, 2, C])
        mid_nat = sb("mid_nat", [P, TAPS, P])
        first_mov = sb("first_mov", [P, 4, C])
        up_hi = sb("up_hi", [P, 2, P], F32R)
        up_lo = sb("up_lo", [P, 2, P], F32R)
        mid_hi = sb("mid_hi", [P, TAPS, P], F32R)
        mid_lo = sb("mid_lo", [P, TAPS, P], F32R)
        down_T = sb("down_T", [P, TAPS, C])
        mid_T = sb("mid_T", [P, TAPS, P])
        first_T = sb("first_T", [C, TAPS, 2, C])
        style_T = sb("style_T", [STYLE, B])
        s_all = sb("s_all", [P, 4, B])
        s_sq = sb("s_sq", [P, 4, B])
        d_all = sb("d_all", [P, 4, B])
        bias_v = sb("bias_v", [P, 2, B])
        mods = sb("mods", [P, NMOD, B])
        up_bias = sb("up_bias", [P, B, 12])
        mods_pair = sb("mods_pair", [P, 2, NMOD, 2])
        x_in = sb("x_in", [P, 2, M])
        x_hi = sb("x_hi", [P, 2, M + 4], F32R)
        x_lo = sb("x_lo", [P, 2, M + 4], F32R)
        fa = [[sb(f"fa{q}{r}", [P, 7, C], F32R) for r in "hl"] for q in range(2)]
        filt = [sb(f"filt{q}", [P, 5, 2, 2, C], F32R) for q in range(2)]
        x_res = sb("x_res", [P, 2, L])
        e_in = sb("e_in", [C, 2, 4, 2, 4])
        e_in_nat = e_in[:].rearrange("p a b e m -> p (a b e m)").rearrange("p (b e w) -> p b e w", b=4, e=2)
        e_x = sb("e_x", [C, 4, 18])
        e_h = sb("e_h", [C, 4, 16])
        e_z = sb("e_z", [P, 4, 14])
        e_z2 = sb("e_z2", [P, 4, 12])
        e_y = sb("e_y", [P, 4, 2, 2])
        proj_hi = sb("proj_hi", [P, KB, max(PROJ_W)], F32R)
        proj_lo = sb("proj_lo", [P, KB, max(PROJ_W)], F32R)
        tail_hi = sb("tail_hi", [P, 2, L], F32R)
        tail_lo = sb("tail_lo", [P, 2, L], F32R)
        proj_raw = sb("proj_raw", [P, KB, C])
        tail_raw = sb("tail_raw", [C + 1, L])
        z_sb = sb("z_sb", [P, 256])
        z_small = sb("z_small", [P, 160])
        zt_hi = sb("zt_hi", [P, 2, P], F32R)
        zt_lo = sb("zt_lo", [P, 2, P], F32R)
        ones = sb("ones", [P, 28])
        two_ones = sb("two_ones", [C + 2, P], F32R)
        router_b = sb("router_b", [P, 8])
        limes = sb("limes", [8, 32])
        h_slice = sb("h_slice", [P, PAIRS, 8])
        raw = sb("raw", [P, 4, L])
        stage = raw[:, 0:2, :]
        x_nat = raw[:, 0:2, :]
        x_out = raw[:, 2:4, :]
        zt_nat = raw[0:32, 2:4, :].rearrange("p a b -> p (a b)")
        ps = ctx.enter_context(nc.psum_tensor("ps", [P, 8, 512], F32))

        names = """prep_loaded style_loaded ident_ready conv_forms forms_T forms_out s_pe sq_ready d_pe
            var_ready std_ready bias_in bias_pe mods_ready pads_ready
            small_loaded narrow_pe wide_pe raw_act raw_dve shared_ready bias_row
            mix_loaded mix_dve mix_pe mix_stored mixed_loaded mixed_act mixed_dve
            limes_pe limes_ready bm_act bm_ready fin_pe fin_dve fin_pool fin_act fin_o fin_x
            pe_t pe_y pe_ab pe_k pe_z pe_zt pe_o pe_e
            act_g act_t act_y act_x act_ab act_k act_z act_zt
            dve_mp dve_g dve_t dve_y dve_x dve_ab dve_k dve_z dve_zt dve_o dve_e
            x_loaded e_loaded chain""".split()
        s = {n: sem(n) for n in names}
        filt_shifted = [sem(f"filt_shifted{q}") for q in range(2)]
        res_loaded = [sem(f"res_loaded{q}") for q in range(2)]
        stored = [sem(f"stored{q}") for q in range(2)]
        raw_loaded = [sem(f"raw_loaded{t}") for t in range(4)]
        fin_loaded = [sem(f"fin_loaded{q}") for q in range(2)]
        fin_stored = [sem(f"fin_stored{q}") for q in range(2)]

        block = ctx.enter_context(nc.Block())

        def pid(l, k):
            return PAIRS * l + k

        def smp(l, k, q):
            return 2 * (PAIRS * l + k) + q + 1

        def edge_count(l, g, step):
            return EDGE_OPS * (GROUPS * l + g) + step

        def is_zero(k):
            return isinstance(k, int) and k == 0

        def w(l, name):
            return a[f"L{l}_{name}"]


        def sp_load_x(sp, l, k):
            if not (l == 0 and is_zero(k)):
                sp.wait_ge(s["dve_x"], pid(l, k))
            for h in range(2):
                r = slice(C * h, C * h + C)
                if l == 0:
                    sp.dma_start(x_nat[r], x_conv[k]).then_inc(s["x_loaded"], 16)
                else:
                    sp.dma_start(x_in[r], xs_conv[h, k]).then_inc(s["x_loaded"], 16)

        def pool_load_edge(gp, l, g):
            if not (l == 0 and is_zero(g)):
                gp.wait_ge(s["dve_e"], edge_count(l, g - 1, 2))
            if l == 0:
                for side in range(2):
                    gp.dma_start(e_in_nat[:, :, side, :],
                                 x_edge[g, :, :, side * (L - 8):side * (L - 8) + 8]).then_inc(s["e_loaded"], 16)
                return
            for q in range(2):
                gp.wait_ge(stored[q], 16 * (GROUPS * (l - 1) + g + 2))
            for h in range(2):
                for side in range(2):
                    gp.dma_start(e_in[:, h, :, side, :],
                                 xs_edge[g, h, :, :, side * (M - 4):side * (M - 4) + 4]).then_inc(s["e_loaded"], 16)

        def edge_loads(l, g):
            return 32 * (g + 1) if l == 0 else 32 * GROUPS + 64 * (GROUPS * (l - 1) + g + 1)

        def sp_shift_filter(sp, l, k):
            for q in range(2):
                sp.wait_ge(s["dve_k"], smp(l, k, q))
                t = f(filt[q][:])
                sp.dma_start(t[0:C, 1:5, :, 1, :], t[C:P, 0:4, :, 0, :]).then_inc(filt_shifted[q], 16)
                sp.dma_start(t[C:P, :, :, 1, :], t[0:C, :, :, 0, :]).then_inc(filt_shifted[q], 16)

        def sp_step(sp, l, i, j, more):
            n = 2 * i + j
            sp.wait_ge(stored[j], 16 * (i + GROUPS * l + 1))
            sp.dma_start(x_res[:, j, :], (x_rows if l == 0 else xs_rows)[n]).then_inc(res_loaded[j], 16)
            if more:
                sp_load_x(sp, l, n + 2)
                sp_shift_filter(sp, l, n + 2)
            sp.wait_ge(s["dve_o"], pid(l, n) + 2)
            sp.dma_start(xs_rows[n], (x_out if l == 0 else x_res)[:, j, :]).then_inc(stored[j], 16)
            if l == 1 and j == 0 and more:
                load_mixed(sp, i + 1)


        def act_load(act, l):
            if l > 0:
                act.wait_ge(s["mods_ready"], l)
                act.wait_ge(s["dve_o"], pid(l, 0) + 1)
            cw = w(l, "cond_weights").rearrange("i o c k -> o i (c k)")
            for h in range(2):
                r = slice(C * h, C * h + C)
                act.dma_start(w_nat[r], cw).then_inc(s["prep_loaded"], 16)
                act.dma_start(mod_b_col[r], w(l, "cond_mod_b").rearrange("i c -> c i"),
                              allow_slow_non_contiguous=True).then_inc(s["prep_loaded"], 16)
                act.dma_start(bias_col[r], w(l, "cond_biases").rearrange("i c -> c i"),
                              allow_slow_non_contiguous=True).then_inc(s["prep_loaded"], 16)
            act.dma_start(mod_w_nat[:], w(l, "cond_mod_w").rearrange("i c d -> c i d")).then_inc(s["prep_loaded"], 16)
            ffn_load(act, l)

        def act_root(act, l):
            act.wait_ge(s["var_ready"], l + 1)
            nc.scalar.activation(std[:], var[:], ACT.Sqrt).then_inc(s["std_ready"], 1)

        def act_filter_in(act, l, k, par):
            act.wait_ge(s["dve_mp"], pid(l, k) + 1)
            for q in range(2):
                if not (l == 0 and is_zero(k)):
                    act.wait_ge(s["pe_ab"], smp(l, k - 1, q))
                    act.wait_ge(s["dve_g"], smp(l, k - 1, q))
                nc.scalar.activation(gw[q][0][:], first_mov[:], ACT.Copy, scale=mods_pair[:, par, G1, q:q + 1])
                nc.scalar.activation(gu[q][0][:], down_T[:], ACT.Copy,
                                     scale=mods_pair[:, par, G3, q:q + 1]).then_inc(s["act_g"], 1)

        def act_filter_halves(act, l, k, par):
            for q in range(2):
                act.wait_ge(s["pe_ab"], smp(l, k, q))
                nc.scalar.activation(fa[q][0][:, 1:6, :], ps[:, 2 + 2 * q, 0:5 * C].rearrange("p (t c) -> p t c", c=C),
                                     ACT.Copy, scale=mods_pair[:, par, G2, q:q + 1])
                nc.scalar.activation(fb[q][0][:], ps[:, 3 + 2 * q, 0:5 * C].rearrange("p (t c) -> p t c", c=C),
                                     ACT.Copy).then_inc(s["act_ab"], 1)

        def act_split_x(act, l, k):
            act.wait_ge(s["x_loaded"], 32 * (pid(l, k) + 1))
            if not (l == 0 and is_zero(k)):
                act.wait_ge(s["pe_y"], smp(l, k - 1, 1))
            for dst, src in x_parts(l, x_hi):
                last = nc.scalar.activation(dst, src, ACT.Copy)
            last.then_inc(s["act_x"], 1)

        def x_parts(l, t):
            if l > 0:
                return [(t[:, :, 2:M + 2], x_in[:])]
            return [(t[C * h:C * h + C, :, 2:M + 2], x_nat[C * h:C * h + C, :, h:L:2]) for h in range(2)]

        def act_filter(act, l, k, par):
            for q in range(2):
                act.wait_ge(s["pe_k"], smp(l, k, q))
                nc.scalar.activation(filt[q][:, :, 0, 0, :], ps[:, 2 + 2 * q, 0:5 * C].rearrange("p (t c) -> p t c", c=C),
                                     ACT.Copy, scale=mods_pair[:, par, S0, q:q + 1]).then_inc(s["act_k"], 1)

        def act_y(act, l, k, par):
            for q in range(2):
                act.wait_ge(s["pe_y"], smp(l, k, q))
                nc.scalar.activation(y_nat[q][:], ps[:, 6 + q, :], ACT.Identity, bias=mods_pair[:, par, CB, q:q + 1],
                                     scale=mods_pair[:, par, DS, q:q + 1]).then_inc(s["act_y"], 1)

        def act_split_y(act, l, k):
            for q in range(2):
                act.wait_ge(s["pe_t"], smp(l, k, q))
                nc.scalar.activation(y_hi[:, :, C * q:C * q + C],
                                     ps[:, 3 + 2 * q, :].rearrange("p (b c) -> p b c", c=C), ACT.Copy).then_inc(s["act_t"], 1)

        def act_step(act, l, i, j, more, one_more):
            n = 2 * i + j
            act_split_y(act, l, n)
            if more:
                act_filter_in(act, l, n + 2, j)
            if one_more:
                act_y(act, l, n + 1, 1 - j)
            if l == 1 and j == 0:
                split_mixed_act(act, i)
            if more:
                act_filter_halves(act, l, n + 2, j)
                act_split_x(act, l, n + 2)
            ffn_act(act, l, i, j)
            if more:
                act_filter(act, l, n + 2, j)

        links = [0]

        def link(dve, ins):
            links[0] += 1
            ins.then_inc(s["chain"], 1)
            dve.wait_ge(s["chain"], links[0])

        def tap(t, i, k):
            return t[:, i, :].rearrange("p (c k) -> p c k", k=TAPS)[:, :, k]

        def dve_prep(dve, l):
            v = nc.vector
            dve.wait_ge(s["prep_loaded"], 7 * 16 * (l + 1))
            if l > 0:
                dve.wait_ge(s["pe_o"], pid(l, 0))
            for n, (conv, div) in enumerate(((1, 4.0), (3, 8.0))):
                v.tensor_scalar(scaled[:, n], w_nat[:, conv, :].rearrange("p (c k) -> p k c", k=TAPS), 1.0 / div, None, ALU.mult)
            for k in range(TAPS):
                v.tensor_copy(first_mov[0:C, k, :], tap(w_nat, 0, k)[0:C])
                v.tensor_copy(first_mov[C:P, k + 1, :], tap(w_nat, 0, k)[C:P])
            lo_r, hi_r = slice(0, C), slice(C, P)
            for r, t, c0, k in ((lo_r, 0, C, 0), (lo_r, 1, 0, 1), (lo_r, 1, C, 2),
                                (hi_r, 1, 0, 0), (hi_r, 1, C, 1), (hi_r, 2, 0, 2)):
                v.tensor_copy(mid_nat[r, t, c0:c0 + C], tap(w_nat, 2, k)[r])
            link(dve, v.tensor_tensor(wsq_tmp[:], w_nat[0:C], w_nat[0:C], ALU.mult))
            v.tensor_reduce(wsq_nat[:].rearrange("p i c -> p (i c)"),
                            wsq_tmp[:].rearrange("p i (c k) -> p (i c) k", k=TAPS), AX_X, ALU.add)
            link(dve, v.tensor_tensor(pair_sum[:], scaled[:, :, 0:2, :], scaled[:, :, 1:3, :], ALU.add))
            for n in range(2):
                q = scaled[:, n]
                for t, h, x0, x1 in ((0, 0, q[:, 2], q[:, 1]), (2, 1, q[:, 0], q[:, 1]),
                                     (1, 0, pair_sum[:, n, 0], q[:, 2]), (1, 1, pair_sum[:, n, 1], q[:, 0])):
                    dst = up_st[:, t, h] if n == 0 else down_nat[:, 2 - t, h]
                    v.scalar_tensor_tensor(dst, x0, 3.0, x1, ALU.mult, ALU.add)
                for t, h, x0 in ((0, 1, q[:, 2]), (2, 0, q[:, 0])):
                    dst = up_st[:, t, h] if n == 0 else down_nat[:, 2 - t, h]
                    v.tensor_copy(dst, x0)
            link(dve, v.tensor_copy(mid_hi[:], mid_nat[:]))
            v.tensor_tensor(mid_lo[:], mid_nat[:], f(mid_hi[:]), ALU.subtract).then_inc(s["conv_forms"], 1)
            up = up_st[:].rearrange("p t h c -> p t (h c)")
            for r, t, d in ((lo_r, 0, 0), (hi_r, 1, 0), (lo_r, 2, 1)):
                last = v.tensor_copy(up_hi[r, d], up[r, t])
            link(dve, last)
            for r, t, d in ((lo_r, 0, 0), (hi_r, 1, 0), (lo_r, 2, 1)):
                last = v.tensor_tensor(up_lo[r, d], up[r, t], f(up_hi[r, d]), ALU.subtract)
            link(dve, last)
            dve.wait_ge(s["forms_T"], l + 1)
            for h in range(2):
                v.tensor_copy(mod_w_T[:, :, h, :], ps[:, 2, 0:4 * C].rearrange("p (i c) -> p i c", c=C))
                v.tensor_copy(wsq_T[:, :, h, :], ps[0:C, 3, 3 * C:7 * C].rearrange("p (i c) -> p i c", c=C))
            v.tensor_copy(style_T[:], ps[:, 2, 4 * C:4 * C + B])
            for h in range(2):
                v.tensor_copy(first_T[:, :, h, :], ps[0:C, 3, 0:3 * C].rearrange("p (k c) -> p k c", c=C))
            v.tensor_copy(down_T[:], ps[:, 4, 0:3 * C].rearrange("p (k c) -> p k c", c=C))
            v.tensor_copy(mid_T[:], ps[:, 5, 0:3 * P].rearrange("p (k c) -> p k c", c=P)).then_inc(s["forms_out"], 1)
            dve.wait_ge(s["s_pe"], l + 1)
            for c in range(4):
                last = v.tensor_scalar(s_all[:, c], ps[:, 6, B * c:B * c + B], mod_b_col[:, c:c + 1], None, ALU.add)
            link(dve, last)
            v.tensor_tensor(s_sq[:], s_all[:], s_all[:], ALU.mult).then_inc(s["sq_ready"], 1)
            dve.wait_ge(s["d_pe"], l + 1)
            v.tensor_scalar(var[:], ps[:, 7, 0:4 * B].rearrange("p (c b) -> p c b", b=B), CONV_SCALE ** 2, DEMOD_EPS,
                            ALU.mult, ALU.add).then_inc(s["var_ready"], 1)
            dve.wait_ge(s["std_ready"], l + 1)
            link(dve, v.reciprocal(d_all[:], std[:]))
            link(dve, v.tensor_tensor(newton[:], d_all[:], d_all[:], ALU.mult))
            link(dve, v.tensor_tensor(newton[:], newton[:], var[:], ALU.mult))
            link(dve, v.tensor_scalar(newton[:], newton[:], -0.5, 1.5, ALU.mult, ALU.add))
            link(dve, v.tensor_tensor(d_all[:], d_all[:], newton[:], ALU.mult))
            v.tensor_copy(mods[:, S0], s_all[:, 0])
            for m, x0, x1 in ((G1, d_all[:, 0], d_all[:, 1]), (G2, s_all[:, 1], s_all[:, 2]), (G3, d_all[:, 2], s_all[:, 3])):
                v.scalar_tensor_tensor(mods[:, m], x0, CONV_SCALE, x1, ALU.mult, ALU.mult)
            v.tensor_scalar(mods[:, DS], d_all[:, 3], CONV_SCALE, None, ALU.mult)
            v.tensor_scalar(mods[:, BT1], d_all[:, 1], bias_col[:, 0:1], None, ALU.mult)
            v.tensor_scalar(mods[:, BT2], s_all[:, 2], bias_col[:, 1:2], 2.0, ALU.mult, ALU.mult)
            link(dve, v.tensor_scalar(mods[:, BT3], s_all[:, 3], bias_col[:, 2:3], None, ALU.mult))
            link(dve, v.tensor_copy(up_bias[:], mods[:, BT2].unsqueeze(2).to_broadcast([P, B, 12])))
            v.tensor_scalar(up_bias[0:C, :, 0:1], up_bias[0:C, :, 0:1], 7.0 / 8.0, None, ALU.mult)
            link(dve, v.tensor_scalar(up_bias[C:P, :, 11:12], up_bias[C:P, :, 11:12], 7.0 / 8.0, None, ALU.mult))
            v.tensor_copy(bias_v[:, 0], mods[:, BT1]).then_inc(s["bias_in"], 1)
            for step, (m, b) in enumerate(((G2, BT2), (G3, BT3))):
                dve.wait_ge(s["bias_pe"], 3 * l + step + 1)
                link(dve, v.tensor_tensor(bias_v[:, 1 - step], ps[:, 6 + step, 0:B], mods[:, m], ALU.mult))
                v.tensor_tensor(bias_v[:, 1 - step], bias_v[:, 1 - step], mods[:, b], ALU.add).then_inc(s["bias_in"], 1)
            dve.wait_ge(s["bias_pe"], 3 * l + 3)
            link(dve, v.tensor_tensor(mods[:, CB], ps[:, 6, 0:B], mods[:, DS], ALU.mult))
            link(dve, v.tensor_scalar(mods[:, CB], mods[:, CB], bias_col[:, 3:4], None, ALU.add))
            v.tensor_copy(newton[:, 0], mods[:, CB]).then_inc(s["mods_ready"], 1)

        def dve_mods_pair(dve, l, k, par):
            if l > 0 or not isinstance(k, int):
                dve.wait_ge(s["act_y"], smp(l, k - 2, 1))
            nc.vector.tensor_copy(mods_pair[:, par], mods[:, :, ds(2 * k, 2)]).then_inc(s["dve_mp"], 1)
            dve.wait_ge(s["dve_mp"], pid(l, k) + 1)

        def dve_filter_in(dve, l, k, par):
            for q in range(2):
                dve.wait_ge(s["act_g"], smp(l, k, q))
                nc.vector.scalar_tensor_tensor(gw[q][1][:], first_mov[:], mods_pair[:, par, G1, q:q + 1], f(gw[q][0][:]),
                                               ALU.mult, ALU.subtract)
                nc.vector.scalar_tensor_tensor(gu[q][1][:], down_T[:], mods_pair[:, par, G3, q:q + 1], f(gu[q][0][:]),
                                               ALU.mult, ALU.subtract).then_inc(s["dve_g"], 1)

        def dve_filter_halves(dve, l, k, q, par):
            dve.wait_ge(s["act_ab"], smp(l, k, q))
            nc.vector.scalar_tensor_tensor(fa[q][1][:, 1:6, :], ps[:, 2 + 2 * q, 0:5 * C].rearrange("p (t c) -> p t c", c=C),
                                           mods_pair[:, par, G2, q:q + 1], f(fa[q][0][:, 1:6, :]), ALU.mult, ALU.subtract)
            nc.vector.tensor_tensor(fb[q][1][:], ps[:, 3 + 2 * q, 0:5 * C].rearrange("p (t c) -> p t c", c=C),
                                    f(fb[q][0][:]), ALU.subtract).then_inc(s["dve_ab"], 1)

        def dve_split_x(dve, l, k):
            dve.wait_ge(s["act_x"], pid(l, k) + 1)
            for (dst, src), (hi, _) in zip(x_parts(l, x_lo), x_parts(l, x_hi)):
                last = nc.vector.tensor_tensor(dst, src, f(hi), ALU.subtract)
            last.then_inc(s["dve_x"], 1)

        def dve_filter(dve, l, k, par):
            for q in range(2):
                dve.wait_ge(s["act_k"], smp(l, k, q))
                nc.vector.scalar_tensor_tensor(filt[q][:, :, 1, 0, :], ps[:, 2 + 2 * q, 0:5 * C].rearrange("p (t c) -> p t c", c=C),
                                               mods_pair[:, par, S0, q:q + 1], f(filt[q][:, :, 0, 0, :]),
                                               ALU.mult, ALU.subtract).then_inc(s["dve_k"], 1)

        def dve_y(dve, l, g, k, q, par):
            dve.wait_ge(s["act_y"], smp(l, k, q))
            dve.wait_ge(s["dve_e"], edge_count(l, g, EDGE_OPS))
            ends = y_nat[q][:].rearrange("p (a b) -> p a b", b=2)[:, 0:M // 2:M // 2 - 1, :]
            nc.vector.tensor_copy(ends, e_y[:, 2 * par + q]).then_inc(s["dve_y"], 1)

        def dve_edge(dve, l, g, stage_no):
            v = nc.vector

            def mod(m, rows, width):
                return mods[rows, m, ds(4 * g, 4)].unsqueeze(2).to_broadcast([rows.stop - rows.start, 4, width])

            def done(ins, step, wait=True):
                ins.then_inc(s["dve_e"], 1)
                if wait:
                    dve.wait_ge(s["dve_e"], edge_count(l, g, step))
            lo_r, all_r = slice(0, C), slice(0, P)
            if stage_no == 0:
                dve.wait_ge(s["e_loaded"], edge_loads(l, g))
                if not (l == 0 and is_zero(g)):
                    dve.wait_ge(s["pe_e"], 4 * (GROUPS * l + g))
                m = mods[lo_r, S0, ds(4 * g, 4)].unsqueeze(2).unsqueeze(3).to_broadcast([C, 4, 2, 4])
                if l == 0:
                    dst = e_x[:, :, 1:17].rearrange("p b (e w) -> p b e w", e=2)
                    for side in range(2):
                        done(v.tensor_tensor(dst[:, :, side], e_in_nat[:, :, side],
                                             mod(S0, lo_r, 8), ALU.mult), side + 1, False)
                    return
                for h in range(2):
                    dst = e_x[:, :, 1:17].rearrange("p b (e m h) -> p b e m h", e=2, h=2)[:, :, :, :, h]
                    done(v.tensor_tensor(dst, e_in[:, h], m, ALU.mult), h + 1, False)
                return
            bank, rows, src_w, dst, mul, add = {
                1: (4, lo_r, 14, e_h[:, :, 1:15], G1, BT1),
                2: (2, all_r, 12, e_z[:, :, 1:13], G2, None),
                3: (4, all_r, 10, e_z2[:, :, 1:11], G3, BT3),
                4: (7, all_r, 4, e_y[:].rearrange("p b e m -> p b (e m)"), DS, None)}[stage_no]
            dve.wait_ge(s["pe_e"], 4 * (GROUPS * l + g) + stage_no)
            src = ps[rows, bank, 0:4 * src_w].rearrange("p (b w) -> p b w", w=src_w)
            first = 2 * stage_no + 1
            done(v.tensor_tensor(dst, src, mod(mul, rows, src_w), ALU.mult), first)
            if add is not None:
                done(v.tensor_tensor(dst, dst, mod(add, rows, src_w), ALU.add), first + 1)
            elif stage_no == 2:
                done(v.tensor_tensor(dst, dst, up_bias[:, ds(4 * g, 4), :], ALU.add), first + 1)
            else:
                done(v.tensor_scalar(dst, dst, bias_col[:, 3:4], None, ALU.add), first + 1)

        def dve_step(dve, l, i, j, more, one_more):
            n = 2 * i + j
            edges = more and j == 0
            g_y = i if j == 0 else i + 1
            if more:
                dve_mods_pair(dve, l, n + 2, j)
            if edges:
                dve_edge(dve, l, i + 1, 0)
            for q in range(2):
                dve.wait_ge(s["act_t"], smp(l, n, q))
                nc.vector.tensor_tensor(y_lo[:, :, C * q:C * q + C], ps[:, 3 + 2 * q, :].rearrange("p (b c) -> p b c", c=C),
                                        f(y_hi[:, :, C * q:C * q + C]), ALU.subtract).then_inc(s["dve_t"], 1)
            if edges:
                dve_edge(dve, l, i + 1, 1)
            if more:
                dve_filter_in(dve, l, n + 2, j)
            if one_more:
                dve_y(dve, l, g_y, n + 1, 0, 1 - j)
            if edges:
                dve_edge(dve, l, i + 1, 2)
            if one_more:
                dve_y(dve, l, g_y, n + 1, 1, 1 - j)
            if edges:
                dve_edge(dve, l, i + 1, 3)
            if l == 1 and j == 0:
                split_mixed_dve(dve, i)
            if more:
                dve_filter_halves(dve, l, n + 2, 0, j)
            if edges:
                dve_edge(dve, l, i + 1, 4)
            if more:
                dve_filter_halves(dve, l, n + 2, 1, j)
                dve_split_x(dve, l, n + 2)
            ffn_dve(dve, l, i, j)
            if more:
                dve_filter(dve, l, n + 2, j)
            dve.wait_ge(s["pe_o"], pid(l, n) + 1)
            dve.wait_ge(res_loaded[j], 16 * (i + GROUPS * l + 1))
            ffn_dve_out(dve, l, i, j)
            if l == 0:
                dst, res = x_out[:, j, :], x_res[:, j, :].rearrange("p (m h) -> p h m", h=2)
            else:
                dst, res = x_res[:, j, :], x_res[:, j, :].rearrange("p (h m) -> p h m", h=2)
            nc.vector.tensor_tensor(dst.rearrange("p (h m) -> p h m", h=2), ps[:, 0:2, :], res, ALU.add).then_inc(s["dve_o"], 1)


        def mm3(out, st, mv, first, last, **kw):
            for t, (x0, x1) in enumerate(((0, 0), (1, 0), (0, 1))):
                ins = nc.tensor.matmul(out, st[x0], mv[x1], start=first and t == 0, stop=last and t == 2, **kw)
            return ins

        def pe_prep(pe, l):
            mm, tr = nc.tensor.matmul, nc.tensor.transpose
            if l == 0:
                pe.wait_ge(s["ident_ready"], 2)
                pe.wait_ge(s["style_loaded"], 16)
            pe.wait_ge(s["prep_loaded"], 7 * 16 * (l + 1))
            pe.wait_ge(s["conv_forms"], l + 1)
            idc = ident[0:C, 0:C]
            for c in range(4):
                tr(ps[:, 2, C * c:C * c + C], mod_w_nat[:, c, :], idc)
                tr(ps[0:C, 3, C * (3 + c):C * (4 + c)], wsq_nat[:, c, :], idc)
            tr(ps[:, 2, 4 * C:4 * C + B], style_nat[:], ident[0:B, 0:B])
            for k in range(TAPS):
                tr(ps[0:C, 3, C * k:C * k + C], tap(w_nat, 0, k)[0:C], idc)
                tr(ps[:, 4, C * k:C * k + C], down_nat[0:C, k].rearrange("p h c -> p (h c)"), idc)
                last = tr(ps[:, 5, P * k:P * k + P], mid_nat[:, k, :], ident[:])
            last.then_inc(s["forms_T"], 1)
            pe.wait_ge(s["forms_out"], l + 1)
            for c in range(4):
                last = mm(ps[:, 6, B * c:B * c + B], mod_w_T[:, c].rearrange("p h c -> p (h c)"), style_T[:], start=True, stop=True)
            last.then_inc(s["s_pe"], 1)
            pe.wait_ge(s["sq_ready"], l + 1)
            for c in range(4):
                last = mm(ps[:, 7, B * c:B * c + B], wsq_T[:, c].rearrange("p h c -> p (h c)"), s_sq[0:C, c], start=True, stop=True)
            last.then_inc(s["d_pe"], 1)
            pe.wait_ge(s["bias_in"], 3 * l + 1)
            for k in range(TAPS):
                last = mm(ps[:, 6, 0:B], up_st[0:C, k].rearrange("p h c -> p (h c)"), bias_v[0:C, 0], start=k == 0, stop=k == 2)
            last.then_inc(s["bias_pe"], 1)
            pe.wait_ge(s["bias_in"], 3 * l + 2)
            for k in range(TAPS):
                last = mm(ps[:, 7, 0:B], mid_T[:, k], bias_v[:, 1], start=k == 0, stop=k == 2)
            last.then_inc(s["bias_pe"], 1)
            pe.wait_ge(s["bias_in"], 3 * l + 3)
            for h in range(2):
                for k in range(TAPS):
                    last = mm(ps[C * h:C * h + C, 6, 0:B], down_T[:, k], bias_v[:, 0], start=k == 0, stop=k == 2)
            last.then_inc(s["bias_pe"], 1)
            pe.wait_ge(s["mods_ready"], l + 1)

        def pe_edge(pe, l, g, stage_no):
            mm = nc.tensor.matmul
            pe.wait_ge(s["dve_e"], edge_count(l, g, 2 * stage_no))
            if stage_no == 4:
                for h in range(2):
                    for k in range(TAPS):
                        rhs = e_z2[:].rearrange("p b (e w) -> p b e w", e=2)[:, :, :, k + h:k + h + 3:2]
                        last = mm(ps[C * h:C * h + C, 7, 0:16].rearrange("p (b e w) -> p b e w", b=4, e=2),
                                  down_T[:, k], rhs, start=k == 0, stop=k == 2)
            else:
                bank, rows, st, src, width = {
                    1: (4, P, [first_T[:, k].rearrange("p h c -> p (h c)") for k in range(3)], e_x, 7),
                    2: (2, P, [up_st[0:C, k].rearrange("p h c -> p (h c)") for k in range(3)], e_h, 6),
                    3: (4, P, [mid_T[:, k] for k in range(3)], e_z, 5)}[stage_no]
                for k in range(TAPS):
                    rhs = src[:].rearrange("p b (e w) -> p b e w", e=2)[:, :, :, k:k + width]
                    last = mm(ps[0:rows, bank, 0:8 * width].rearrange("p (b e w) -> p b e w", b=4, e=2),
                              st[k], rhs, start=k == 0, stop=k == 2)
            last.then_inc(s["pe_e"], 1)

        def pe_filter_halves(pe, l, k, q):
            pe.wait_ge(s["dve_g"], smp(l, k, q))
            up = [t for t in (up_hi, up_lo)]
            o = ps[:, 2 + 2 * q]
            mm3(o[:, 0:4 * C], [t[:, 0] for t in up], [t[:].rearrange("p t c -> p (t c)") for t in gw[q]],
                True, True, skip_group_check=True)
            mm3(o[:, 2 * C:5 * C], [t[:, 1] for t in up], [t[:, 0:3].rearrange("p t c -> p (t c)") for t in gw[q]],
                False, True, skip_group_check=True)
            o = ps[:, 3 + 2 * q]
            for t in range(TAPS):
                last = mm3(o[:, C * t:C * (t + 3)], [x[:, t] for x in (mid_hi, mid_lo)],
                           [x[:].rearrange("p t c -> p (t c)") for x in gu[q]], t == 0, True, skip_group_check=True)
            last.then_inc(s["pe_ab"], 1)

        def pe_filter(pe, l, k, samples=(0, 1)):
            for q in samples:
                pe.wait_ge(s["dve_ab"], smp(l, k, q))
                o = ps[:, 2 + 2 * q]
                for n, j in enumerate((-2, -3, -1, 0, 1, 2)):
                    u = [x for x in (-4, -2, 0, 2, 4) if -2 <= x - j <= 2]
                    b0 = u[0] - j + 2
                    st = [t[:, j + 3:j + 5].rearrange("p t c -> p (t c)") for t in fa[q]]
                    mv = [t[:, b0:b0 + 2 * len(u) - 1:2] for t in fb[q]]
                    c0 = (u[0] + 4) // 2
                    last = mm3(o[:, C * c0:C * (c0 + len(u))].rearrange("p (t c) -> p t c", c=C), st, mv, n == 0, True,
                               skip_group_check=True)
                last.then_inc(s["pe_k"], 1)

        def pe_conv(pe, l, k, q):
            if q == 0:
                pe.wait_ge(s["dve_x"], pid(l, k) + 1)
            pe.wait_ge(filt_shifted[q], 32 * (pid(l, k) + 1))
            for t in range(5):
                st = [filt[q][:, t, r].rearrange("p h c -> p (h c)") for r in range(2)]
                mv = [x[:, q, t:t + M] for x in (x_hi, x_lo)]
                last = mm3(ps[:, 6 + q, :], st, mv, t == 0, t == 4)
            last.then_inc(s["pe_y"], 1)

        def pe_transpose_y(pe, l, k):
            for q in range(2):
                pe.wait_ge(s["dve_y"], smp(l, k, q))
                for t in range(4):
                    last = nc.tensor.transpose(ps[:, 3 + 2 * q, P * t:P * t + P], y_nat[q][:, P * t:P * t + P], ident[:])
                last.then_inc(s["pe_t"], 1)

        def pe_step(pe, l, i, j, more, one_more):
            n = 2 * i + j
            edges = more and j == 0
            pe_transpose_y(pe, l, n)
            if edges:
                pe_edge(pe, l, i + 1, 1)
            if one_more:
                pe_conv(pe, l, n + 1, 0)
            if edges:
                pe_edge(pe, l, i + 1, 2)
            if one_more:
                pe_conv(pe, l, n + 1, 1)
            if edges:
                pe_edge(pe, l, i + 1, 3)
            pe.wait_ge(s["dve_t"], smp(l, n, 1))
            if more:
                pe_filter_halves(pe, l, n + 2, 0)
            if one_more:
                pe.wait_ge(s["act_y"], smp(l, n + 1, 1))
            if edges:
                pe_edge(pe, l, i + 1, 4)
            if more:
                pe_filter_halves(pe, l, n + 2, 1)
            pe_project(pe, l, i, j)
            pe.wait_ge(s["dve_o"], pid(l, n) + 1)
            if edges:
                pe.wait_ge(s["dve_e"], edge_count(l, i + 1, EDGE_OPS))
            pe_ffn(pe, l, n, 0)
            if more:
                pe_filter(pe, l, n + 2, (0,))
            pe_project_T(pe, l, i, j)
            if more:
                pe_filter(pe, l, n + 2, (1,))
            pe_ffn(pe, l, n, 1)
            pe_tail(pe, l, i, j)

        def kb_cols(t, kb):
            return t[:, (kb // 2) * 2 * P + kb % 2:(kb // 2 + 1) * 2 * P:2]

        def natural(t):
            return t.rearrange("p (h m) -> p m h", h=2)

        def raw_count(l, t):
            if l == 1:
                return 16 * (t // 2 + 1)
            return 16 * ((2 if t % 4 < 2 else 0) + 2 * (l - 2) + t // 4 + 1)

        def ffn_load(act, l):
            def small(dst, src):
                act.dma_start(dst, src).then_inc(s["small_loaded"], 16)
            if l == 0:
                small(raw[:, 2], w(0, "ffn_A").rearrange("h r d -> (h r) d"))
                small(tail_raw[0:8], w(0, "ffn_Wr"))
                for ob in range(8):
                    small(nat_b[:, ob, 0:P].rearrange("p (h r) -> p h r", h=8),
                          w(0, "ffn_B")[:, P * ob:P * ob + P, :].rearrange("h o r -> o h r"))
                small(router_b[:], w(0, "ffn_br").partition_broadcast(P))
            if l == 1:
                small(shared_a, w(1, "ffn_lora_A_shared"))
                small(shared_b[:, :, 32:64], w(1, "ffn_lora_B_shared").rearrange("(ob p) r -> p ob r", p=P))
                small(tail_raw[64:65, :], w(1, "ffn_bias").rearrange("(a n) -> a n", a=1))
                load_wide(act, l, 0)
                for q in range(2):
                    act.wait_ge(stored[q], 16 * (GROUPS + 1))
                load_wide(act, l, 1)
            if l == 2:
                small(tail_raw[0:28], w(2, "ffn_gate_W"))
                la = w(2, "ffn_lora_A").rearrange("e r d -> (e r) d")
                small(raw[:, 2], la[0:P])
                small(raw[0:96, 3], la[P:224])
                for ob in range(8):
                    small(nat_b[:, ob, :].rearrange("p (e r) -> p e r", r=8),
                          w(2, "ffn_lora_B")[:, P * ob:P * ob + P, :].rearrange("e o r -> o e r"))
            if l == 3:
                for mb in range(4):
                    small(proj_raw[:, 2 * mb:2 * mb + 2, 0:32],
                          w(3, "ffn_A")[2 * P * mb:2 * P * (mb + 1), :].rearrange("(p h) r -> p h r", h=2))
                small(tail_raw[64:65, :], w(3, "ffn_b").rearrange("(a n) -> a n", a=1))
                small(tail_raw[0:32, :], w(3, "ffn_Bmat"))
                small(limes[:], w(3, "ffn_LiMEs"))
            if l >= 2:
                for ob in range(2 if l == 2 else 4):
                    load_wide(act, l, ob)

        SMALL_LOADS = (11, 3, 11, 7)
        shared_a = nat_b[0:32].rearrange("p o c -> p (o c)")[:, 768:768 + L]
        shared_b = nat_b[:].rearrange("p o c -> p (o c)")[:, 0:512].rearrange("p (o c) -> p o c", c=C)

        def small_count(l):
            return 16 * sum(SMALL_LOADS[:l + 1])

        def load_wide(act, l, t):
            if l == 1:
                act.dma_start(raw[:, 2 * (t % 2):2 * (t % 2) + 2, :],
                              w(1, "ffn_kernel")[2 * P * t:2 * P * (t + 1), :].rearrange("(p h) n -> p h n", h=2)) \
                    .then_inc(raw_loaded[t % 2], 16)
            else:
                act.dma_start(raw[:, t % 4, :], w(l, "ffn_base_W" if l == 2 else "ffn_W")[P * t:P * t + P, :]) \
                    .then_inc(raw_loaded[t % 4], 16)

        NARROW_PARTS = (5, 0, 8, 2)
        WIDE_PARTS = (0, 4, 16, 16)

        def part_count(l, n):
            return sum(NARROW_PARTS[:l]) + sum(WIDE_PARTS[:l]) + n + 1

        def narrow_parts(l):
            parts = []
            if l in (0, 2):
                width = PROJ_W[l]
                per = 512 // width
                for b, k0 in enumerate(range(0, KB, per)):
                    kn = min(per, KB - k0)
                    parts.append((proj_hi[:, k0:k0 + kn, 0:width], proj_lo[:, k0:k0 + kn, 0:width],
                                  ps[:, 2 + b, 0:width * kn].rearrange("p (k w) -> p k w", w=width)))
                for blk, rows in ((0, P),) if l == 0 else ((0, P), (1, 96)):
                    for half in range(2):
                        hi, lo = (natural(t[0:rows, blk])[:, 256 * half:256 * half + 256] for t in (tail_hi, tail_lo))
                        bank = (5 + half) if l == 0 else 2 + 2 * blk + half
                        parts.append((hi, lo, ps[0:rows, bank, :].rearrange("p (m h) -> p m h", h=2)))
            if l == 3:
                parts.append((proj_hi[:, :, 0:32], proj_lo[:, :, 0:32], proj_raw[:, :, 0:32]))
                parts.append((natural(tail_hi[64:65, 0]), natural(tail_lo[64:65, 0]),
                              tail_raw[64:65, :].rearrange("p (m h) -> p m h", h=2)))
            return parts

        def wide_part(l, n):
            if l == 1:
                hi, lo = (t[:, 2 * n:2 * n + 2, :].rearrange("p k (h m) -> p k m h", h=2) for t in (w_hi, w_lo))
                return hi, lo, raw[:, 2 * (n % 2):2 * (n % 2) + 2, :].rearrange("p k (m h) -> p k m h", h=2)
            ob, half = n // 2, n % 2
            hi, lo = (t[:, 4 * half:4 * half + 4, :].rearrange("p k (h m) -> p k m h", h=2)[:, :, C * ob:C * ob + C, :] for t in (w_hi, w_lo))
            return hi, lo, ps[:, 2 + n % 4, :].rearrange("p (k m h) -> p k m h", k=4, h=2)

        def ffn_act_prep(act, l):
            def split(part):
                nc.scalar.activation(part[0], part[2], ACT.Copy).then_inc(s["raw_act"], 1)
            for n, part in enumerate(narrow_parts(l)):
                if l == 3:
                    act.wait_ge(s["small_loaded"], small_count(3))
                elif n == 0:
                    act.wait_ge(s["narrow_pe"], (1, 0, 3)[l])
                elif l == 2 and n == 4:
                    act.wait_ge(s["narrow_pe"], 4)
                    for ob in (2, 3):
                        load_wide(act, 2, ob)
                split(part)
            for n in range(WIDE_PARTS[l]):
                if l == 1:
                    act.wait_ge(raw_loaded[n % 2], raw_count(1, n))
                else:
                    act.wait_ge(s["wide_pe"], 16 * (l - 2) + n + 1)
                split(wide_part(l, n))
                if l == 1 and n < 2:
                    act.wait_ge(s["raw_dve"], part_count(1, n))
                    load_wide(act, 1, n + 2)
                if l >= 2 and n % 2 == 1 and n // 2 < 4:
                    load_wide(act, l, n // 2 + 4)
            if l == 1:
                act.wait_ge(s["small_loaded"], small_count(1))
                act.wait_ge(s["shared_ready"], 2)

        def ffn_dve_prep(dve, l):
            v = nc.vector
            base = part_count(l, -1)
            if l == 1:
                v.memset(f(zt_hi[C:C + 1, 0]), 1.0)
                v.memset(f(zt_lo[C:C + 1, 0]), 0.0)
                v.memset(shared_b[:, :, 0:32], 0.0).then_inc(s["shared_ready"], 1)
                dve.wait_ge(s["narrow_pe"], 2)
                v.tensor_copy(proj_raw[:, :, 32:64], ps[:, 2, 0:256].rearrange("p (k r) -> p k r", r=32))
                for half in range(2):
                    last = v.tensor_copy(tail_raw[32:64, 512 * half:512 * half + 512], ps[32:64, 3 + half, :])
                last.then_inc(s["shared_ready"], 1)
            parts = narrow_parts(l) + [wide_part(l, n) for n in range(WIDE_PARTS[l])]
            for n, part in enumerate(parts):
                dve.wait_ge(s["raw_act"], base + n + 1)
                v.tensor_tensor(part[1], part[2], f(part[0]), ALU.subtract).then_inc(s["raw_dve"], 1)

        def ffn_pe_prep(pe, l):
            tr = nc.tensor.transpose
            if l < 3:
                pe.wait_ge(s["small_loaded"], small_count(l))
            if l == 0:
                for kb in range(KB):
                    b, c = 2 + kb // 3, 136 * (kb % 3)
                    tr(ps[:, b, c:c + P], kb_cols(raw[:, 2], kb), ident[:])
                    tr(ps[:, b, c + P:c + P + 8], kb_cols(tail_raw[0:8], kb), ident[0:8, 0:8])
                for ob in range(8):
                    last = tr(ps[:, 5 + ob // 4, P * (ob % 4):P * (ob % 4) + P], nat_b[:, ob, 0:P], ident[:])
                last.then_inc(s["narrow_pe"], 1)
                pe.wait_ge(s["raw_dve"], part_count(0, 4))
            if l == 1:
                for kb in range(KB):
                    tr(ps[:, 2, 32 * kb:32 * kb + 32], kb_cols(shared_a, kb), ident[0:32, 0:32])
                pe.wait_ge(s["shared_ready"], 1)
                for ob in range(8):
                    last = tr(ps[0:C, 3 + ob // 4, P * (ob % 4):P * (ob % 4) + P], shared_b[:, ob], ident[:])
                last.then_inc(s["narrow_pe"], 1)
                pe.wait_ge(s["raw_dve"], part_count(1, 3))
            if l == 2:
                for kb in range(KB):
                    b, c = 2 + kb // 2, 252 * (kb % 2)
                    tr(ps[:, b, c:c + 28], kb_cols(tail_raw[0:28], kb), ident[0:28, 0:28])
                    tr(ps[:, b, c + 28:c + 28 + P], kb_cols(raw[:, 2], kb), ident[:])
                    last = tr(ps[:, b, c + 28 + P:c + 252], kb_cols(raw[0:96, 3], kb), ident[0:96, 0:96])
                last.then_inc(s["narrow_pe"], 1)
                pe.wait_ge(s["raw_dve"], part_count(2, 3))
                for ob in range(8):
                    c = P * (ob % 4)
                    tr(ps[:, 2 + ob // 4, c:c + P], nat_b[:, ob, 0:P], ident[:])
                    last = tr(ps[0:96, 4 + ob // 4, c:c + P], nat_b[:, ob, P:224], ident[:])
                last.then_inc(s["narrow_pe"], 1)
            if l >= 2:
                for ob in range(8):
                    pe.wait_ge(raw_loaded[ob % 4], raw_count(l, ob))
                    for half in range(2):
                        n = 2 * ob + half
                        pe.wait_ge(s["raw_dve"], part_count(l, NARROW_PARTS[l] + n - 4))
                        for k in range(4):
                            last = tr(ps[:, 2 + n % 4, P * k:P * k + P], kb_cols(raw[:, ob % 4], 4 * half + k), ident[:])
                        last.then_inc(s["wide_pe"], 1)
                pe.wait_ge(s["raw_dve"], part_count(l, NARROW_PARTS[l] + 15))

        def mix_loads(act):
            for g in range(4):
                act.dma_start(mix_a[:, g], w(1, "ffn_lora_A")[4 * g:4 * g + 4].rearrange("n r d -> (n r) d")).then_inc(s["mix_loaded"], 16)
                act.dma_start(gate_col[32 * g:32 * g + 32], w(1, "ffn_gate").rearrange("b (g n) -> n (b g)", n=4)[g]
                              .partition_broadcast(32), allow_slow_non_contiguous=True).then_inc(s["mix_loaded"], 16)
            for ob in range(8):
                act.dma_start(mix_b[:, ob], w(1, "ffn_lora_B")[:, P * ob:P * ob + P, :].rearrange("n o r -> o n r")).then_inc(s["mix_loaded"], 16)

        MIX_LOADS = 16 * 16

        def mix_dve(dve):
            v = nc.vector
            dve.wait_ge(s["mix_loaded"], MIX_LOADS)
            dve.wait_ge(s["ident_ready"], 2)
            link(dve, v.tensor_reduce(same_rank[:], ident[:].rearrange("p (n r) -> p r n", n=4), AX_X, ALU.add))
            for g in range(4):
                last = v.tensor_tensor(gate_mat[:, g], gate_col[:].rearrange("p (b g) -> p g b", g=4)[:, g].unsqueeze(2).to_broadcast([P, 8, 32]),
                                       same_rank[:].unsqueeze(1).to_broadcast([P, 8, 32]), ALU.mult)
            last.then_inc(s["mix_dve"], 1)
            for half in range(2):
                for g in range(4):
                    dve.wait_ge(s["mix_pe"], 4 * half + g + 1)
                    v.tensor_copy(mix_bt[:, g, 512 * half:512 * half + 512], ps[:, 2 + g, :]).then_inc(s["mix_dve"], 1)
            for t in range(4):
                dve.wait_ge(s["mix_pe"], 8 + t + 1)
                v.tensor_copy(mixed_a[:, :, 2 * t:2 * t + 2, :],
                              ps[:, 2 + t, :].rearrange("p (k b r) -> p b k r", k=2, b=8)).then_inc(s["mix_dve"], 1)
            for t in range(4):
                dve.wait_ge(s["mix_pe"], 12 + t + 1)
                v.tensor_copy(mixed_b[:, t // 2, 512 * (t % 2):512 * (t % 2) + 512], ps[:, 2 + t, :]).then_inc(s["mix_dve"], 1)

        def mix_pe(pe):
            mm, tr = nc.tensor.matmul, nc.tensor.transpose
            pe.wait_ge(s["mix_loaded"], MIX_LOADS)
            pe.wait_ge(s["mix_dve"], 1)
            for half in range(2):
                for g in range(4):
                    if half:
                        pe.wait_ge(s["mix_dve"], 1 + g + 1)
                    for ob in range(4):
                        last = tr(ps[:, 2 + g, P * ob:P * ob + P],
                                  mix_b[:, 4 * half + ob, 4 * g:4 * g + 4, :].rearrange("p n r -> p (n r)"), ident[:])
                    last.then_inc(s["mix_pe"], 1)
            for t in range(4):
                pe.wait_ge(s["mix_dve"], 1 + 4 + t + 1)
                for k in range(2):
                    for g in range(4):
                        last = mm(ps[:, 2 + t, 256 * k:256 * k + 256], kb_cols(mix_a[:, g], 2 * t + k),
                                  gate_mat[:, g].rearrange("p b r -> p (b r)"), start=g == 0, stop=g == 3)
                last.then_inc(s["mix_pe"], 1)
            for t in range(4):
                pe.wait_ge(s["mix_dve"], 9 + t + 1)
                for g in range(4):
                    last = mm(ps[:, 2 + t, :], gate_mat[:, g, 4 * (t // 2):4 * (t // 2) + 4].rearrange("p b r -> p (b r)"),
                              mix_bt[:, g, 512 * (t % 2):512 * (t % 2) + 512], start=g == 0, stop=g == 3)
                last.then_inc(s["mix_pe"], 1)
            pe.wait_ge(s["mix_dve"], 17)

        def mix_store(sp):
            sp.wait_ge(s["mix_dve"], 13)
            sp.dma_start(mixed_a_dram.rearrange("b p w -> p b w"), mixed_a[:].rearrange("p b k r -> p b (k r)")).then_inc(s["mix_stored"], 16)
            sp.wait_ge(s["mix_dve"], 17)
            for t in range(2):
                sp.dma_start(mixed_b_dram[4 * t:4 * t + 4].rearrange("b r n -> (b r) n"), mixed_b[:, t]).then_inc(s["mix_stored"], 16)

        def load_mixed(sp, g):
            if not is_zero(g):
                sp.wait_ge(s["mixed_dve"], 2 * g)
            sp.dma_start(proj_raw[:, :, 0:32], mixed_a_dram[g].rearrange("p (k r) -> p k r", r=32)).then_inc(s["mixed_loaded"], 16)
            sp.dma_start(tail_raw[0:32, :], mixed_b_dram[g]).then_inc(s["mixed_loaded"], 16)

        def split_mixed_act(act, g):
            act.wait_ge(s["mixed_loaded"], 32 * g + 32)
            act.wait_ge(s["pe_o"], pid(1, 2 * g))
            nc.scalar.activation(proj_hi[:, :, 0:64], proj_raw[:], ACT.Copy).then_inc(s["mixed_act"], 1)
            nc.scalar.activation(natural(tail_hi[0:65, 0]), tail_raw[0:65, :].rearrange("p (m h) -> p m h", h=2),
                                 ACT.Copy).then_inc(s["mixed_act"], 1)

        def split_mixed_dve(dve, g):
            dve.wait_ge(s["mixed_act"], 2 * g + 1)
            nc.vector.tensor_tensor(proj_lo[:, :, 0:64], proj_raw[:], f(proj_hi[:, :, 0:64]), ALU.subtract).then_inc(s["mixed_dve"], 1)
            dve.wait_ge(s["mixed_act"], 2 * g + 2)
            nc.vector.tensor_tensor(natural(tail_lo[0:65, 0]), tail_raw[0:65, :].rearrange("p (m h) -> p m h", h=2),
                                    f(natural(tail_hi[0:65, 0])), ALU.subtract).then_inc(s["mixed_dve"], 1)

        def zc(l, n, step):
            return sum(PAIRS * x for x in Z_OPS[:l]) + Z_OPS[l] * n + step

        ZT_ROWS = ((P,), (64,), (P, 96), (32,))

        def ffn_act(act, l, i, j):
            n = 2 * i + j
            if l == 0:
                act.wait_ge(s["dve_z"], zc(l, n, 2))
                nc.scalar.activation(z_small[:, 16:24], z_small[:, 0:8], ACT.Exp, bias=z_small[:, 8:9],
                                     accum_out=z_small[:, 9:10]).then_inc(s["act_z"], 1)
            if l == 2:
                act.wait_ge(s["dve_z"], zc(l, n, 3))
                nc.scalar.activation(z_small[:, 41:42], z_small[:, 40:41], ACT.Exp).then_inc(s["act_z"], 1)
            if l == 3:
                return
            act.wait_ge(s["pe_zt"], pid(l, n) + 1)
            for b, rows in enumerate(ZT_ROWS[l]):
                last = nc.scalar.activation(zt_hi[0:rows, b, :], ps[0:rows, 7, P * b:P * b + P], ACT.Copy)
            last.then_inc(s["act_zt"], 1)

        def ffn_dve(dve, l, i, j):
            n = 2 * i + j
            v = nc.vector

            def done(ins, step):
                ins.then_inc(s["dve_z"], 1)
                dve.wait_ge(s["dve_z"], zc(l, n, step))

            dve.wait_ge(s["pe_z"], pid(l, n) + 1)
            if l == 0:
                done(v.tensor_tensor(z_small[:, 0:8], ps[:, 6, P:P + 8], router_b[:], ALU.add), 1)
                done(v.tensor_reduce(z_small[:, 8:9], z_small[:, 0:8], AX_X, ALU.max, negate=True), 2)
                dve.wait_ge(s["act_z"], n + 1)
                done(v.reciprocal(z_small[:, 10:11], z_small[:, 9:10]), 3)
                done(v.tensor_scalar(z_small[:, 11:12], z_small[:, 10:11], 16.0, None, ALU.mult), 4)
                done(v.scalar_tensor_tensor(z_sb[:, 0:P].rearrange("p (h r) -> p h r", h=8),
                                            ps[:, 6, 0:P].rearrange("p (h r) -> p h r", h=8), z_small[:, 11:12],
                                            z_small[:, 16:24].unsqueeze(2).to_broadcast([P, 8, 16]), ALU.mult, ALU.mult), 5)
            if l in (1, 3):
                done(v.tensor_copy(z_sb[:, 0:PROJ_W[l]], ps[:, 6, 0:PROJ_W[l]]), 1)
            if l == 2:
                lg, first, second = z_small[:, 0:28], z_small[:, 32:33], z_small[:, 33:34]
                diff, e2, den, p1, p2, apart = (z_small[:, c:c + 1] for c in range(40, 46))
                above, equal, seen, keep = (z_small[:, c:c + 28] for c in (48, 76, 104, 132))
                v.tensor_copy(lg, ps[:, 6, 0:28]).then_inc(s["dve_z"], 1)
                done(v.max(z_small[:, 32:40], ps[:, 6, 0:28]), 2)
                done(v.tensor_tensor(diff, second, first, ALU.subtract), 3)
                done(v.tensor_scalar(above, lg, second, None, ALU.is_gt), 4)
                done(v.tensor_scalar(equal, lg, second, None, ALU.is_equal), 5)
                done(v.tensor_tensor_scan(seen, ones[:, 0:28], equal, 0.0, ALU.mult, ALU.add), 6)
                done(v.tensor_tensor(apart, first, second, ALU.is_gt), 7)
                done(v.tensor_scalar(keep, seen, apart, 2.0, ALU.add, ALU.is_le), 8)
                done(v.tensor_tensor(keep, keep, equal, ALU.mult), 9)
                dve.wait_ge(s["act_z"], PAIRS + n + 1)
                done(v.tensor_scalar(den, e2, 1.0, None, ALU.add), 10)
                done(v.reciprocal(den, den), 11)
                done(v.tensor_scalar(p1, den, 2.0, None, ALU.mult), 12)
                done(v.tensor_tensor(p2, e2, p1, ALU.mult), 13)
                done(v.tensor_scalar(above, above, p1, None, ALU.mult), 14)
                done(v.scalar_tensor_tensor(above, keep, p2, above, ALU.mult, ALU.add), 15)
                done(v.tensor_tensor(z_sb[:, 0:224].rearrange("p (e r) -> p e r", r=8),
                                     ps[:, 6, 28:252].rearrange("p (e r) -> p e r", r=8),
                                     above.unsqueeze(2).to_broadcast([P, 28, 8]), ALU.mult), 16)
            if l == 3:
                dve.wait_ge(s["pe_zt"], pid(l, n) + 1)
                v.tensor_copy(zt_nat[:, ds(P * n, P)], ps[0:32, 7, 0:P]).then_inc(s["dve_zt"], 1)
                return
            dve.wait_ge(s["act_zt"], pid(l, n) + 1)
            for b, rows in enumerate(ZT_ROWS[l]):
                last = v.tensor_tensor(zt_lo[0:rows, b, :], ps[0:rows, 7, P * b:P * b + P], f(zt_hi[0:rows, b, :]), ALU.subtract)
            last.then_inc(s["dve_zt"], 1)

        def ffn_dve_out(dve, l, i, j):
            if l == 3:
                n = 2 * i + j
                nc.vector.tensor_copy(h_slice[:, ds(n, 1), :].rearrange("p a (m h) -> p (a h) m", h=2), ps[:, 0:2, 0:4])

        def pe_project(pe, l, i, j):
            n = 2 * i + j
            if l == 1 and j == 0:
                pe.wait_ge(s["mixed_dve"], 2 * i + 2)
            for kb in range(KB):
                last = mm3(ps[:, 6, 0:PROJ_W[l]], [t[:, kb] for t in (y_hi, y_lo)],
                           [t[:, kb, 0:PROJ_W[l]] for t in (proj_hi, proj_lo)], kb == 0, kb == KB - 1)
            last.then_inc(s["pe_z"], 1)

        def pe_ffn(pe, l, n, h):
            if l == 0:
                return
            for kb in range(KB):
                mm3(ps[:, h, :], [t[:, kb] for t in (y_hi, y_lo)], [t[:, kb, M * h:M * h + M] for t in (w_hi, w_lo)],
                    kb == 0, False)

        def pe_project_T(pe, l, i, j):
            n = 2 * i + j
            pe.wait_ge(s["dve_z"], zc(l, n, Z_OPS[l]))
            for b in range(len(ZT_ROWS[l])):
                last = nc.tensor.transpose(ps[:, 7, P * b:P * b + P], z_sb[:, P * b:P * b + P], ident[:])
            last.then_inc(s["pe_zt"], 1)

        def pe_tail(pe, l, i, j):
            n = 2 * i + j
            pe.wait_ge(s["dve_zt"], pid(l, n) + 1)
            if l == 3:
                pe.wait_ge(s["bias_row"], 16)
            for h in range(2):
                cols = slice(M * h, M * h + M)
                if l == 3:
                    last = nc.tensor.matmul(ps[:, h, :], two_ones[64:66], tail_hi[64:66, 0, cols], start=False, stop=True)
                    continue
                rows = (P,) if l == 0 else (65,) if l == 1 else (P, 96)
                for b, r in enumerate(rows):
                    last = mm3(ps[:, h, :], [t[0:r, b] for t in (zt_hi, zt_lo)], [t[0:r, b, cols] for t in (tail_hi, tail_lo)],
                               l == 0, b == len(rows) - 1)
            last.then_inc(s["pe_o"], 1)

        def join_bias(sp):
            sp.wait_ge(s["raw_dve"], part_count(3, 1))
            sp.dma_start(f(tail_hi[65:66, 0, :]), f(tail_lo[64:65, 0, :])).then_inc(s["bias_row"], 16)

        def final_dve(dve):
            v = nc.vector
            hs = h_slice[:].rearrange("p n e -> p (n e)")
            dve.wait_ge(s["limes_pe"], 1)
            v.tensor_copy(limes_T[:], ps[0:32, 3, 0:8]).then_inc(s["limes_ready"], 1)
            v.tensor_copy(to_anchor[:].rearrange("p (a t) -> p a t", t=2), ident[:, 1:P:2].unsqueeze(2).to_broadcast([P, C, 2]))
            v.tensor_reduce(odd[:], ident[:, 1:P:2], AX_X, ALU.add)
            dve.wait_ge(s["bm_act"], 1)
            v.scalar_tensor_tensor(natural(bm_lo[:]), tail_raw[0:32].rearrange("p (m h) -> p m h", h=2), 0.5,
                                   f(natural(bm_hi[:])), ALU.mult, ALU.subtract).then_inc(s["bm_ready"], 1)
            dve.wait_ge(s["fin_pe"], 1)
            link(dve, v.tensor_copy(d_slice[:].rearrange("p n e -> p (n e)"), ps[:, 2, 0:P]))
            link(dve, v.tensor_reduce(maxes[:, 0:1], hs, AX_X, ALU.max, apply_absolute_value=True))
            link(dve, v.tensor_reduce(maxes[:, 1:2], d_slice[:].rearrange("p n e -> p (n e)"), AX_X, ALU.max, apply_absolute_value=True))
            v.tensor_scalar(maxes[:, 2:4], maxes[:, 0:2], odd[:], None, ALU.mult).then_inc(s["fin_dve"], 1)
            dve.wait_ge(s["fin_pool"], 1)
            link(dve, v.tensor_scalar(maxes[:, 6:8], maxes[:, 4:6], 1e-6, None, ALU.max))
            link(dve, v.reciprocal(maxes[:, 6:8], maxes[:, 6:8]))
            link(dve, v.tensor_scalar(maxes[:, 6:8], maxes[:, 6:8], 0.5, None, ALU.mult))
            link(dve, v.tensor_scalar(hs, hs, maxes[:, 6:7], None, ALU.mult))
            lgs = route[:, 0]
            link(dve, v.scalar_tensor_tensor(lgs, d_slice[:].rearrange("p n e -> p (n e)"), maxes[:, 7:8], hs, ALU.mult, ALU.add))

            def per(t):
                return t.rearrange("p (n e) -> p n e", e=8)

            def bc(c):
                return col[:, c].unsqueeze(2).to_broadcast([P, PAIRS, 8])
            link(dve, v.tensor_reduce(col[:, 0], per(lgs), AX_X, ALU.max))
            v.tensor_tensor(per(route[:, 1]), per(lgs), bc(0), ALU.subtract).then_inc(s["fin_dve"], 1)
            dve.wait_ge(s["fin_act"], 1)
            link(dve, v.tensor_reduce(col[:, 1], per(route[:, 2]), AX_X, ALU.add))
            link(dve, v.reciprocal(col[:, 1], col[:, 1]))
            link(dve, v.tensor_tensor(per(route[:, 3]), per(route[:, 2]), bc(1), ALU.mult))
            for n in range(PAIRS):
                last = v.max(per(route[:, 4])[:, n], per(route[:, 3])[:, n])
            link(dve, last)
            link(dve, v.tensor_copy(col[:, 2], per(route[:, 4])[:, :, 1]))
            v.tensor_tensor(per(route[:, 5]), per(route[:, 3]), bc(2), ALU.subtract).then_inc(s["fin_dve"], 1)
            dve.wait_ge(s["fin_act"], 2)
            link(dve, v.tensor_scalar(route[:, 6], route[:, 6], 1.0, None, ALU.add))
            link(dve, v.reciprocal(route[:, 6], route[:, 6]))
            link(dve, v.tensor_tensor(route[:, 7], route[:, 3], route[:, 6], ALU.mult))
            link(dve, v.tensor_reduce(col[:, 3], per(route[:, 7]), AX_X, ALU.add))
            link(dve, v.tensor_scalar(col[:, 3], col[:, 3], 1e-9, None, ALU.add))
            link(dve, v.reciprocal(col[:, 3], col[:, 3]))
            v.tensor_tensor(per(route[:, 8]), per(route[:, 7]), bc(3), ALU.mult).then_inc(s["fin_dve"], 1)
            for t in range(4):
                dve.wait_ge(s["fin_pe"], 2 + t)
                v.tensor_copy(w_T[:, 512 * t:512 * t + 512], ps[0:8, 2 + t, :]).then_inc(s["fin_dve"], 1)
            for t in range(4):
                c = slice(512 * t, 512 * t + 512)
                dve.wait_ge(s["fin_pe"], 6 + t)
                link(dve, v.tensor_tensor(zt_nat[:, c], zt_nat[:, c], ps[0:32, 2 + t, :], ALU.mult))
                link(dve, v.tensor_copy(zp_hi[:, c], zt_nat[:, c]))
                v.tensor_tensor(zp_lo[:, c], zt_nat[:, c], f(zp_hi[:, c]), ALU.subtract).then_inc(s["fin_dve"], 1)
            for n in range(PAIRS):
                dve.wait_ge(s["fin_o"], n + 1)
                dve.wait_ge(fin_loaded[n % 2], 16 * (n // 2 + 1))
                if n >= 2:
                    dve.wait_ge(fin_stored[n % 2], 16 * (n // 2))
                b = 2 * (n % 2)
                v.tensor_tensor(stage[:, n % 2].rearrange("p (m h) -> p h m", h=2), ps[:, b:b + 2, :],
                                x_res[:, n % 2].rearrange("p (h m) -> p h m", h=2), ALU.add).then_inc(s["fin_x"], 1)

        def final_act(act):
            act.wait_ge(s["pe_o"], pid(LAYERS, 0))
            nc.scalar.activation(natural(bm_hi[:]), tail_raw[0:32].rearrange("p (m h) -> p m h", h=2), ACT.Copy,
                                 scale=0.5).then_inc(s["bm_act"], 1)
            act.wait_ge(s["fin_dve"], 2)
            nc.scalar.activation(route[:, 2], route[:, 1], ACT.Exp).then_inc(s["fin_act"], 1)
            act.wait_ge(s["fin_dve"], 3)
            nc.scalar.activation(route[:, 6], route[:, 5], ACT.Exp, scale=-2.0).then_inc(s["fin_act"], 1)

        def final_pool(gp):
            gp.wait_ge(s["fin_dve"], 1)
            gp.partition_all_reduce(maxes[:, 4:6], maxes[:, 2:4], P, RMAX).then_inc(s["fin_pool"], 1)

        def final_pe(pe):
            mm = nc.tensor.matmul
            pe.wait_ge(s["dve_zt"], pid(LAYERS, 0))
            nc.tensor.transpose(ps[0:32, 3, 0:8], limes[:], ident[0:8, 0:8]).then_inc(s["limes_pe"], 1)
            pe.wait_ge(s["limes_ready"], 1)
            for n in range(PAIRS):
                last = mm(ps[:, 2, 8 * n:8 * n + 8], zt_nat[:, P * n:P * n + P], limes_T[:], start=True, stop=True)
            last.then_inc(s["fin_pe"], 1)
            pe.wait_ge(s["fin_dve"], 4)
            for t in range(4):
                for n in range(4 * t, 4 * t + 4):
                    last = mm(ps[0:8, 2 + t, P * (n % 4):P * (n % 4) + P], route[:, 8, 8 * n:8 * n + 8], to_anchor[:], start=True, stop=True)
                last.then_inc(s["fin_pe"], 1)
            for t in range(4):
                pe.wait_ge(s["fin_dve"], 5 + t)
                mm(ps[0:32, 2 + t, :], limes[:], w_T[:, 512 * t:512 * t + 512], start=True, stop=True).then_inc(s["fin_pe"], 1)
            for n in range(PAIRS):
                pe.wait_ge(s["fin_dve"], 9 + n // 4)
                if n >= 2:
                    pe.wait_ge(s["fin_x"], n - 1)
                else:
                    pe.wait_ge(s["dve_o"], pid(LAYERS, 0) + 1)
                    pe.wait_ge(s["bm_ready"], 1)
                    pe.wait_ge(s["fin_dve"], 12)
                for h in range(2):
                    last = mm3(ps[:, 2 * (n % 2) + h, :], [t[:, P * n:P * n + P] for t in (zp_hi, zp_lo)],
                               [t[:, M * h:M * h + M] for t in (bm_hi, bm_lo)], True, True)
                last.then_inc(s["fin_o"], 1)

        def final_sp(sp):
            for n in range(PAIRS):
                if n >= 2:
                    sp.wait_ge(s["fin_x"], n - 1)
                else:
                    sp.wait_ge(stored[n], 16 * (GROUPS * LAYERS + 1))
                sp.dma_start(x_res[:, n % 2], xs_rows[n]).then_inc(fin_loaded[n % 2], 16)
                if n >= 1:
                    final_store(sp, n - 1)
            final_store(sp, PAIRS - 1)
            for q in range(2):
                sp.wait_ge(fin_stored[q], 16 * (PAIRS // 2))

        def final_store(sp, n):
            sp.wait_ge(s["fin_x"], n + 1)
            sp.dma_start(out_rows[n], stage[:, n % 2]).then_inc(fin_stored[n % 2], 16)

        @block.sync
        def _(sp):
            if STOP_AFTER > 1:
                mix_store(sp)
            for l in range(STOP_AFTER):
                sp_load_x(sp, l, 0)
                sp_shift_filter(sp, l, 0)
                sp_load_x(sp, l, 1)
                sp_shift_filter(sp, l, 1)
                if l == 1:
                    load_mixed(sp, 0)
                if l == 3:
                    join_bias(sp)
                with sp.Fori(0, GROUPS - 1) as i:
                    for j in range(2):
                        sp_step(sp, l, i, j, True)
                for j in range(2):
                    sp_step(sp, l, GROUPS - 1, j, False)
            for q in range(2):
                sp.wait_ge(stored[q], 16 * (GROUPS * STOP_AFTER + 1))
            if STOP_AFTER == LAYERS:
                final_sp(sp)

        @block.gpsimd
        def _(gp):
            gp.memset(ident[:], 0.0).then_inc(s["ident_ready"], 1)
            gp.wait_ge(s["ident_ready"], 1)
            gp.affine_select(out=ident[:], in_=ident[:], compare_op=ALU.not_equal, fill=1.0, base=0,
                             pattern=[[-1, P]], channel_multiplier=1).then_inc(s["ident_ready"], 1)
            for l in range(STOP_AFTER):
                pool_load_edge(gp, l, 0)
                with gp.Fori(0, GROUPS - 1) as i:
                    pool_load_edge(gp, l, i + 1)
            if STOP_AFTER == LAYERS:
                final_pool(gp)

        @block.scalar
        def _(act):
            act.dma_start(style_nat[:], a["cond_512"]).then_inc(s["style_loaded"], 16)
            act_load(act, 0)
            if STOP_AFTER > 1:
                mix_loads(act)
            for q in range(2):
                act.sem_inc(stored[q], 16)
            for l in range(STOP_AFTER):
                if l > 0:
                    act_load(act, l)
                act_root(act, l)
                ffn_act_prep(act, l)
                act_filter_in(act, l, 0, 0)
                act_filter_halves(act, l, 0, 0)
                act_split_x(act, l, 0)
                act_filter(act, l, 0, 0)
                act_filter_in(act, l, 1, 1)
                act_y(act, l, 0, 0)
                act_filter_halves(act, l, 1, 1)
                act_split_x(act, l, 1)
                act_filter(act, l, 1, 1)
                with act.Fori(0, GROUPS - 1) as i:
                    for j in range(2):
                        act_step(act, l, i, j, True, True)
                for j in range(2):
                    act_step(act, l, GROUPS - 1, j, False, j == 0)
            if STOP_AFTER == LAYERS:
                final_act(act)

        @block.vector
        def _(dve):
            dve.sem_inc(s["dve_o"], 1)
            for t in (x_hi, x_lo):
                nc.vector.memset(f(t[:]), 0.0)
            for q in range(2):
                for r in range(2):
                    nc.vector.memset(f(fa[q][r][:]), 0.0)
                nc.vector.memset(f(filt[q][:]), 0.0)
            for t in (e_x, e_h, e_z, e_z2, first_mov, mid_nat):
                nc.vector.memset(t[:], 0.0)
            for t in (up_hi, up_lo):
                nc.vector.memset(f(t[:]), 0.0)
            for t in (ones, two_ones):
                nc.vector.memset(f(t[:]), 1.0)
            link(dve, nc.vector.memset(z_sb[:], 0.0))
            for l in range(STOP_AFTER):
                dve_prep(dve, l)
                ffn_dve_prep(dve, l)
                if l == 0 and STOP_AFTER > 1:
                    mix_dve(dve)
                dve_mods_pair(dve, l, 0, 0)
                dve_filter_in(dve, l, 0, 0)
                dve_edge(dve, l, 0, 0)
                dve_edge(dve, l, 0, 1)
                dve_edge(dve, l, 0, 2)
                dve_edge(dve, l, 0, 3)
                dve_filter_halves(dve, l, 0, 0, 0)
                dve_edge(dve, l, 0, 4)
                dve_filter_halves(dve, l, 0, 1, 0)
                dve_split_x(dve, l, 0)
                dve_filter(dve, l, 0, 0)
                dve_mods_pair(dve, l, 1, 1)
                dve_filter_in(dve, l, 1, 1)
                dve_y(dve, l, 0, 0, 0, 0)
                dve_y(dve, l, 0, 0, 1, 0)
                dve_filter_halves(dve, l, 1, 0, 1)
                dve_filter_halves(dve, l, 1, 1, 1)
                dve_split_x(dve, l, 1)
                dve_filter(dve, l, 1, 1)
                with dve.Fori(0, GROUPS - 1) as i:
                    for j in range(2):
                        dve_step(dve, l, i, j, True, True)
                for j in range(2):
                    dve_step(dve, l, GROUPS - 1, j, False, j == 0)
            if STOP_AFTER == LAYERS:
                final_dve(dve)

        @block.tensor
        def _(pe):
            for l in range(STOP_AFTER):
                pe_prep(pe, l)
                ffn_pe_prep(pe, l)
                if l == 0 and STOP_AFTER > 1:
                    mix_pe(pe)
                for stage_no in range(1, 4):
                    pe_edge(pe, l, 0, stage_no)
                pe_filter_halves(pe, l, 0, 0)
                pe_edge(pe, l, 0, 4)
                pe_filter_halves(pe, l, 0, 1)
                pe_filter(pe, l, 0)
                pe_conv(pe, l, 0, 0)
                pe_conv(pe, l, 0, 1)
                pe_filter_halves(pe, l, 1, 0)
                pe_filter_halves(pe, l, 1, 1)
                pe_filter(pe, l, 1)
                with pe.Fori(0, GROUPS - 1) as i:
                    for j in range(2):
                        pe_step(pe, l, i, j, True, True)
                for j in range(2):
                    pe_step(pe, l, GROUPS - 1, j, False, j == 0)
            if STOP_AFTER == LAYERS:
                final_pe(pe)


def kernel(**inputs):
    import numpy as np
    import concourse.bacc as bacc
    from concourse.bass_utils import run_bass_kernel_spmd

    nc = bacc.Bacc("TRN2", target_bir_lowering=False, num_devices=1)
    arrays, args = {}, {}
    for name in inputs:
        if STOP_AFTER < LAYERS and name[0] == "L" and int(name[1]) >= STOP_AFTER and int(name[1]) > 1:
            continue
        arr = np.ascontiguousarray(inputs[name])
        arrays["in_" + name] = arr
        args[name] = nc.dram_tensor("in_" + name, arr.shape, mybir.dt.from_np(arr.dtype), kind="ExternalInput").ap()
    shape = (B, C, L) if STOP_AFTER == LAYERS else (B, C, 2, M)
    out = nc.dram_tensor("out_x", shape, F32, kind="ExternalOutput").ap()
    build(nc, args, out)
    r = run_bass_kernel_spmd(nc, [arrays], core_ids=[0])
    return r.results[0]["out_x"]
```

```python
from contextlib import ExitStack

import concourse.bass as bass
from concourse import mybir

F32 = mybir.dt.float32
F32R = mybir.dt.float32r
U32 = mybir.dt.uint32
ACT = mybir.ActivationFunctionType
ALU = mybir.AluOpType
AX_X = mybir.AxisListType.X
RMAX = bass.bass_isa.ReduceOp.max
ds = bass.ds

LAYERS = 4
P = 128
B, C, L = 32, 64, 1024
M = L // 2
PAIRS = B // 2
GROUPS = PAIRS // 2
KB = L // P
STYLE = 128
TAPS = 3
CONV_SCALE = 1.0 / float((C * TAPS ** 2) ** 0.5)
DEMOD_EPS = 1e-8
S0, G1, G2, G3, DS, CB, BT1, BT2, BT3 = range(9)
NMOD = 9
EDGE_OPS = 10
X_LAST = 6
PROJ_W = (136, 64, 252, 32)
Z_OPS = (5, 1, 16, 1)


def build(nc, a, out):
    ctx = ExitStack()
    with ctx:
        def sb(name, shape, dt=F32, stack=ctx):
            return stack.enter_context(nc.sbuf_tensor(name, shape, dt))

        def sem(name):
            return ctx.enter_context(nc.semaphore(name))

        def f(t):
            return t.bitcast(F32)

        xs = nc.dram_tensor("x_state", (B, C, 2, M), F32, kind="Internal").ap()
        xs_rows = xs.rearrange("(n s) c h m -> n (s c) (h m)", s=2)
        xs_conv = xs.rearrange("(n s) c h m -> h n c s m", s=2)
        xs_edge = xs.rearrange("(g s) c h m -> g h c s m", s=4)
        x_rows = a["x"].rearrange("(n s) c l -> n (s c) l", s=2)
        x_conv = a["x"].rearrange("(n s) c l -> n c s l", s=2)
        x_edge = a["x"].rearrange("(g s) c l -> g c s l", s=4)

        mixed_a_dram = nc.dram_tensor("mixed_a_dram", (GROUPS, P, KB * 32), F32, kind="Internal").ap()
        mixed_b_dram = nc.dram_tensor("mixed_b_dram", (GROUPS, 32, L), F32, kind="Internal").ap()
        out_rows = out.rearrange("(n s) c l -> n (s c) l", s=2)

        kernel_cols = a["L1_ffn_kernel"].rearrange("(b p h) (s n) -> h s p b n", h=2, p=P, s=8)

        with ExitStack() as area:
            mix_a = sb("mix_a", [P, 4, L], stack=area)
            mix_b = sb("mix_b", [P, 8, 16, 32], stack=area)
            mix_bt = sb("mix_bt", [P, 4, L], stack=area)
            gate_col = sb("gate_col", [P, 32], stack=area)
            same_rank = sb("same_rank", [P, 32], stack=area)
            gate_mat = sb("gate_mat", [P, 4, 8, 32], stack=area)
            mixed_a = sb("mixed_a", [P, 8, KB, 32], stack=area)
            mixed_b = mix_b[:].rearrange("p o n r -> p (o n r)")[:, 0:2 * L].rearrange("p (t o) -> p t o", t=2)
        with ExitStack() as area:
            zp_hi = sb("zp_hi", [32, B * C], F32R, stack=area)
            zp_lo = sb("zp_lo", [32, B * C], F32R, stack=area)
            bm_hi = sb("bm_hi", [32, L], F32R, stack=area)
            bm_lo = sb("bm_lo", [32, L], F32R, stack=area)
            w_T = sb("w_T", [8, B * C], stack=area)
            route = sb("route", [P, 9, P], stack=area)
            d_slice = sb("d_slice", [P, PAIRS, 8], stack=area)
            col = sb("col", [P, 4, PAIRS], stack=area)
            maxes = sb("maxes", [P, 8], stack=area)
            odd = sb("odd", [P, 1], stack=area)
            to_anchor = sb("to_anchor", [P, P], stack=area)
            limes_T = sb("limes_T", [32, 8], stack=area)
            x_last = sb("x_last", [P, X_LAST, L], stack=area)
        w_hi = sb("w_hi", [P, KB, L], F32R)
        w_lo = sb("w_lo", [P, KB, L], F32R)
        with ExitStack() as area:
            nat_b = sb("nat_b", [P, 8, 224], stack=area)
        gw = [[sb(f"gw{q}{r}", [P, 4, C], F32R) for r in "hl"] for q in range(2)]
        gu = [sb(f"gu{q}", [P, TAPS, C]) for q in range(2)]
        fb = [sb(f"fb{q}", [P, 5, C]) for q in range(2)]
        scaled = sb("scaled", [P, 2, TAPS, C])
        down_nat = sb("down_nat", [P, TAPS, 2, C])
        mod_w_nat = sb("mod_w_nat", [C, 4, STYLE])
        wsq_nat = sb("wsq_nat", [C, 4, C])
        wsq_T = sb("wsq_T", [C, 4, 2, C])
        with ExitStack() as area:
            mod_w_T = sb("mod_w_T", [STYLE, 4, 2, C], stack=area)
            var = sb("var", [P, 4, B], stack=area)
            std = sb("std", [P, 4, B], stack=area)
            newton = sb("newton", [P, 4, B], stack=area)
        fa = [sb(f"fa{q}", [P, 7, C]) for q in range(2)]
        with ExitStack() as area:
            wsq_tmp = sb("wsq_tmp", [C, 4, C * TAPS], stack=area)
            pair_sum = sb("pair_sum", [P, 2, 2, C], stack=area)
        x_in = sb("x_in", [P, 2, M])
        y_nat = [sb(f"y_nat{q}", [P, M]) for q in range(2)]
        y_hi = sb("y_hi", [P, KB, P], F32R)
        y_lo = sb("y_lo", [P, KB, P], F32R)
        ident = sb("ident", [P, P])
        w_nat = sb("w_nat", [P, 4, C * TAPS])
        mod_b_col = sb("mod_b_col", [P, 4])
        bias_col = sb("bias_col", [P, 4])
        style_nat = sb("style_nat", [B, STYLE])
        up_st = sb("up_st", [P, TAPS, 2, C])
        mid_nat = sb("mid_nat", [P, TAPS, P])
        first_mov = sb("first_mov", [P, 4, C])
        up_hi = sb("up_hi", [P, 2, P], F32R)
        up_lo = sb("up_lo", [P, 2, P], F32R)
        down_T = sb("down_T", [P, TAPS, C])
        mid_T = sb("mid_T", [P, TAPS, P])
        first_T = sb("first_T", [C, TAPS, 2, C])
        style_T = sb("style_T", [STYLE, B])
        s_all = sb("s_all", [P, 4, B])
        s_sq = sb("s_sq", [P, 4, B])
        d_all = sb("d_all", [P, 4, B])
        bias_v = sb("bias_v", [P, 2, B])
        mods = sb("mods", [P, NMOD, B])
        up_bias = sb("up_bias", [P, B, 12])
        mods_pair = sb("mods_pair", [P, 2, NMOD, 2])
        x_hi = sb("x_hi", [P, 2, M + 4], F32R)
        x_lo = sb("x_lo", [P, 2, M + 4], F32R)
        filt = [sb(f"filt{q}", [P, 5, 2, 2, C], F32R) for q in range(2)]
        x_res = sb("x_res", [P, 2, L])
        kernel_in = x_in[:].rearrange("p s n -> p (s n)").rearrange("p (k n) -> p k n", k=KB)
        e_in = sb("e_in", [C, 2, 4, 2, 4])
        e_in_nat = e_in[:].rearrange("p a b e m -> p (a b e m)").rearrange("p (b e w) -> p b e w", b=4, e=2)
        e_x = sb("e_x", [C, 4, 18])
        e_h = sb("e_h", [C, 4, 16])
        e_z = sb("e_z", [P, 4, 14])
        e_z2 = sb("e_z2", [P, 4, 12])
        e_y = sb("e_y", [P, 4, 2, 2])
        with ExitStack() as area:
            proj_0 = sb("proj_0", [P, KB, PROJ_W[0]], stack=area)
            y_f = sb("y_f", [P, KB, P], stack=area)
        proj_hi = sb("proj_hi", [P, KB, max(PROJ_W)], F32R)
        proj_lo = sb("proj_lo", [P, KB, max(PROJ_W)], F32R)
        tail_hi = sb("tail_hi", [P, 2, L], F32R)
        tail_lo = sb("tail_lo", [P, 2, L], F32R)
        proj_raw = sb("proj_raw", [P, KB, C])
        tail_raw = sb("tail_raw", [C + 1, L])
        z_sb = sb("z_sb", [P, 256])
        z_small = sb("z_small", [P, 160])
        zt_hi = sb("zt_hi", [P, 2, P], F32R)
        zt_lo = sb("zt_lo", [P, 2, P], F32R)
        ones = sb("ones", [P, 28])
        two_ones = sb("two_ones", [C + 2, P], F32R)
        router_b = sb("router_b", [P, 8])
        limes = sb("limes", [8, 32])
        h_slice = sb("h_slice", [P, PAIRS, 8])
        raw = sb("raw", [P, 4, L])
        stage = raw[:, 0:2, :]
        x_nat = raw[:, 0:2, :]
        x_out = raw[:, 2:4, :]
        zt_nat = raw[0:32, 2:4, :].rearrange("p a b -> p (a b)")
        ps = ctx.enter_context(nc.psum_tensor("ps", [P, 8, 512], F32))

        names = """first_loaded prep_loaded style_loaded ident_ready conv_forms forms_T forms_out s_pe sq_ready d_pe
            var_ready std_ready bias_in bias_pe mods_ready pads_ready
            small_loaded narrow_pe wide_pe raw_act raw_dve shared_ready bias_row kernel_loaded kernel_act kernel_dve
            mix_loaded mix_dve mix_pe mix_stored mixed_loaded mixed_act mixed_dve
            limes_pe limes_ready bm_act bm_ready fin_pe fin_dve fin_pool fin_act fin_o fin_x
            pe_t pe_y pe_ab pe_k pe_z pe_zt pe_o pe_e
            act_g act_t act_f act_y act_x act_ab act_k act_z act_zt
            dve_mp dve_g dve_t dve_y dve_x dve_ab dve_k dve_z dve_zt dve_o dve_e
            x_loaded e_loaded chain""".split()
        s = {n: sem(n) for n in names}
        filt_shifted = [sem(f"filt_shifted{q}") for q in range(2)]
        res_loaded = [sem(f"res_loaded{q}") for q in range(2)]
        stored = [sem(f"stored{q}") for q in range(2)]
        raw_loaded = [sem(f"raw_loaded{t}") for t in range(4)]
        fin_loaded = [sem(f"fin_loaded{t}") for t in range(X_LAST)]
        fin_stored = [sem(f"fin_stored{q}") for q in range(2)]

        block = ctx.enter_context(nc.Block())

        def pid(l, k):
            return PAIRS * l + k

        def smp(l, k, q):
            return 2 * (PAIRS * l + k) + q + 1

        def edge_count(l, g, step):
            return EDGE_OPS * (GROUPS * l + g) + step

        def is_zero(k):
            return isinstance(k, int) and k == 0

        def w(l, name):
            return a[f"L{l}_{name}"]


        def cond_loaded(l):
            return (s["first_loaded"], 7 * 16) if l == 0 else (s["prep_loaded"], 7 * 16 * l)

        def load_cond_weights(eng, l):
            if l > 0:
                eng.wait_ge(s["mods_ready"], l)
            for h in range(2):
                r = slice(C * h, C * h + C)
                eng.dma_start(w_nat[r], w(l, "cond_weights").rearrange("i o c k -> o i (c k)")).then_inc(cond_loaded(l)[0], 16)
                eng.dma_start(mod_b_col[r], w(l, "cond_mod_b").rearrange("i c -> c i"),
                              allow_slow_non_contiguous=True).then_inc(cond_loaded(l)[0], 16)

        def load_cond_rest(eng, l):
            if l > 0:
                eng.wait_ge(s["dve_e"], edge_count(l, 0, 0))
                eng.wait_ge(s["pe_k"], smp(l - 1, PAIRS - 1, 1))
            for h in range(2):
                eng.dma_start(bias_col[C * h:C * h + C], w(l, "cond_biases").rearrange("i c -> c i"),
                              allow_slow_non_contiguous=True).then_inc(cond_loaded(l)[0], 16)
            eng.dma_start(mod_w_nat[:], w(l, "cond_mod_w").rearrange("i c d -> c i d")).then_inc(cond_loaded(l)[0], 16)

        def sp_load_x(sp, l, k):
            if not (l == 0 and is_zero(k)):
                sp.wait_ge(s["dve_x"], pid(l, k))
            if l > 0 and is_zero(k):
                sp.wait_ge(s["mods_ready"], l + 1)
            for h in range(2):
                r = slice(C * h, C * h + C)
                if l == 0:
                    sp.dma_start(x_nat[r], x_conv[k]).then_inc(s["x_loaded"], 16)
                else:
                    sp.dma_start(x_in[r], xs_conv[h, k]).then_inc(s["x_loaded"], 16)

        def pool_load_edge(gp, l, g):
            if not (l == 0 and is_zero(g)):
                gp.wait_ge(s["dve_e"], edge_count(l, g - 1, 2))
            if l == 0:
                for side in range(2):
                    gp.dma_start(e_in_nat[:, :, side, :],
                                 x_edge[g, :, :, side * (L - 8):side * (L - 8) + 8]).then_inc(s["e_loaded"], 16)
                return
            for q in range(2):
                gp.wait_ge(stored[q], 16 * (GROUPS * (l - 1) + g + 2))
            for h in range(2):
                for side in range(2):
                    gp.dma_start(e_in[:, h, :, side, :],
                                 xs_edge[g, h, :, :, side * (M - 4):side * (M - 4) + 4]).then_inc(s["e_loaded"], 16)

        def edge_loads(l, g):
            return 32 * (g + 1) if l == 0 else 32 * GROUPS + 64 * (GROUPS * (l - 1) + g + 1)

        def sp_shift_filter(sp, l, k):
            for q in range(2):
                sp.wait_ge(s["dve_k"], smp(l, k, q))
                t = f(filt[q][:])
                sp.dma_start(t[0:C, 1:5, :, 1, :], t[C:P, 0:4, :, 0, :]).then_inc(filt_shifted[q], 16)
                sp.dma_start(t[C:P, :, :, 1, :], t[0:C, :, :, 0, :]).then_inc(filt_shifted[q], 16)

        def sp_step(sp, l, i, j, more):
            n = 2 * i + j
            if l == 0 and j == 0:
                load_kernel(sp, i)
            sp.wait_ge(stored[j], 16 * (i + GROUPS * l + 1))
            sp.dma_start(x_res[:, j, :], (x_rows if l == 0 else xs_rows)[n]).then_inc(res_loaded[j], 16)
            if more:
                sp_load_x(sp, l, n + 2)
                sp_shift_filter(sp, l, n + 2)
            if not more and j == 1 and l + 1 < LAYERS:
                if l + 1 == 2:
                    sp.wait_ge(s["mixed_dve"], GROUPS)
                sp.wait_ge(s["pe_k"], smp(l, PAIRS - 1, 1))
                ffn_load(sp, l + 1)
            sp.wait_ge(s["dve_o"], pid(l, n) + 2)
            sp.dma_start(xs_rows[n], (x_out if l == 0 else x_res)[:, j, :]).then_inc(stored[j], 16)
            if l == 1 and j == 1 and more:
                load_mixed(sp, i + 1)


        def act_root(act, l):
            act.wait_ge(s["var_ready"], l + 1)
            nc.scalar.activation(std[:], var[:], ACT.Sqrt).then_inc(s["std_ready"], 1)

        def act_filter_in(act, l, k, par):
            act.wait_ge(s["dve_mp"], pid(l, k) + 1)
            for q in range(2):
                if not (l == 0 and is_zero(k)):
                    act.wait_ge(s["pe_ab"], smp(l, k - 1, q))
                    act.wait_ge(s["dve_g"], smp(l, k - 1, q))
                nc.scalar.activation(gw[q][0][:], first_mov[:], ACT.Copy, scale=mods_pair[:, par, G1, q:q + 1])
                nc.scalar.activation(gu[q][:], down_T[:], ACT.Copy,
                                     scale=mods_pair[:, par, G3, q:q + 1]).then_inc(s["act_g"], 1)

        def act_filter_halves(act, l, k, par):
            for q in range(2):
                act.wait_ge(s["pe_ab"], smp(l, k, q))
                nc.scalar.activation(fa[q][:, 1:6, :], ps[:, 2 + 2 * q, 0:5 * C].rearrange("p (t c) -> p t c", c=C),
                                     ACT.Copy, scale=mods_pair[:, par, G2, q:q + 1]).then_inc(s["act_ab"], 1)

        def act_split_x(act, l, k):
            act.wait_ge(s["x_loaded"], 32 * (pid(l, k) + 1))
            if not (l == 0 and is_zero(k)):
                act.wait_ge(s["pe_y"], smp(l, k - 1, 1))
            for dst, src in x_parts(l, x_hi):
                last = nc.scalar.activation(dst, src, ACT.Copy)
            last.then_inc(s["act_x"], 1)

        def x_parts(l, t):
            if l > 0:
                return [(t[:, :, 2:M + 2], x_in[:])]
            return [(t[C * h:C * h + C, :, 2:M + 2], x_nat[C * h:C * h + C, :, h:L:2]) for h in range(2)]

        def act_filter(act, l, k, par):
            for q in range(2):
                act.wait_ge(s["pe_k"], smp(l, k, q))
                nc.scalar.activation(filt[q][:, :, 0, 0, :], ps[:, 2 + 2 * q, 0:5 * C].rearrange("p (t c) -> p t c", c=C),
                                     ACT.Copy, scale=mods_pair[:, par, S0, q:q + 1]).then_inc(s["act_k"], 1)

        def act_y(act, l, k, par):
            for q in range(2):
                act.wait_ge(s["pe_y"], smp(l, k, q))
                nc.scalar.activation(y_nat[q][:], ps[:, 6 + q, :], ACT.Identity, bias=mods_pair[:, par, CB, q:q + 1],
                                     scale=mods_pair[:, par, DS, q:q + 1]).then_inc(s["act_y"], 1)

        def act_split_y(act, l, k):
            for q in range(2):
                src = ps[:, 3 + 2 * q, :].rearrange("p (b c) -> p b c", c=C)
                act.wait_ge(s["pe_t"], smp(l, k, q))
                if l > 0:
                    nc.scalar.activation(y_hi[:, :, C * q:C * q + C], src, ACT.Copy).then_inc(s["act_t"], 1)
                if l != 2:
                    nc.scalar.activation(y_f[:, :, C * q:C * q + C], src, ACT.Copy).then_inc(s["act_f"], 1)

        def whole_y(l, n, q):
            return smp(l if l < 2 else 2, n, q)

        def act_step(act, l, i, j, more, one_more):
            n = 2 * i + j
            act_split_y(act, l, n)
            if l == 0 and j == 0 and not more:
                split_kernel_act(act, i)
            if more:
                act_filter_in(act, l, n + 2, j)
            if one_more:
                act_y(act, l, n + 1, 1 - j)
            if l == 1 and j == 0:
                split_mixed_act(act, i)
            if l == 0 and j == 0 and more:
                split_kernel_act(act, i)
            if more:
                act_filter_halves(act, l, n + 2, j)
                act_split_x(act, l, n + 2)
            ffn_act(act, l, i, j)
            if more:
                act_filter(act, l, n + 2, j)
            elif j == 0 and l + 1 < LAYERS:
                act_root(act, l + 1)

        links = [0]

        def link(dve, ins):
            links[0] += 1
            ins.then_inc(s["chain"], 1)
            dve.wait_ge(s["chain"], links[0])

        def tap(t, i, k):
            return t[:, i, :].rearrange("p (c k) -> p c k", k=TAPS)[:, :, k]

        def dve_prep_forms(dve, l):
            v = nc.vector
            dve.wait_ge(*cond_loaded(l))
            for n, (conv, div) in enumerate(((1, 4.0), (3, 8.0))):
                v.tensor_scalar(scaled[:, n], w_nat[:, conv, :].rearrange("p (c k) -> p k c", k=TAPS), 1.0 / div, None, ALU.mult)
            for k in range(TAPS):
                v.tensor_copy(first_mov[0:C, k, :], tap(w_nat, 0, k)[0:C])
                v.tensor_copy(first_mov[C:P, k + 1, :], tap(w_nat, 0, k)[C:P])
            lo_r, hi_r = slice(0, C), slice(C, P)
            for r, t, c0, k in ((lo_r, 0, C, 0), (lo_r, 1, 0, 1), (lo_r, 1, C, 2),
                                (hi_r, 1, 0, 0), (hi_r, 1, C, 1), (hi_r, 2, 0, 2)):
                v.tensor_copy(mid_nat[r, t, c0:c0 + C], tap(w_nat, 2, k)[r])
            link(dve, v.tensor_tensor(wsq_tmp[:], w_nat[0:C], w_nat[0:C], ALU.mult))
            v.tensor_reduce(wsq_nat[:].rearrange("p i c -> p (i c)"),
                            wsq_tmp[:].rearrange("p i (c k) -> p (i c) k", k=TAPS), AX_X, ALU.add)
            link(dve, v.tensor_tensor(pair_sum[:], scaled[:, :, 0:2, :], scaled[:, :, 1:3, :], ALU.add))
            for n in range(2):
                q = scaled[:, n]
                for t, h, x0, x1 in ((0, 0, q[:, 2], q[:, 1]), (2, 1, q[:, 0], q[:, 1]),
                                     (1, 0, pair_sum[:, n, 0], q[:, 2]), (1, 1, pair_sum[:, n, 1], q[:, 0])):
                    dst = up_st[:, t, h] if n == 0 else down_nat[:, 2 - t, h]
                    v.scalar_tensor_tensor(dst, x0, 3.0, x1, ALU.mult, ALU.add)
                for t, h, x0 in ((0, 1, q[:, 2]), (2, 0, q[:, 0])):
                    dst = up_st[:, t, h] if n == 0 else down_nat[:, 2 - t, h]
                    last = v.tensor_copy(dst, x0)
            link(dve, last)
            up = up_st[:].rearrange("p t h c -> p t (h c)")
            for r, t, d in ((lo_r, 0, 0), (hi_r, 1, 0), (lo_r, 2, 1)):
                last = v.tensor_copy(up_hi[r, d], up[r, t])
            link(dve, last)
            for r, t, d in ((lo_r, 0, 0), (hi_r, 1, 0), (lo_r, 2, 1)):
                last = v.tensor_tensor(up_lo[r, d], up[r, t], f(up_hi[r, d]), ALU.subtract)
            last.then_inc(s["conv_forms"], 1)

        def dve_prep_transposed(dve, l):
            v = nc.vector
            dve.wait_ge(s["forms_T"], l + 1)
            for h in range(2):
                v.tensor_copy(mod_w_T[:, :, h, :], ps[:, 2, 0:4 * C].rearrange("p (i c) -> p i c", c=C))
                v.tensor_copy(wsq_T[:, :, h, :], ps[0:C, 3, 3 * C:7 * C].rearrange("p (i c) -> p i c", c=C))
            if l == 0:
                v.tensor_copy(style_T[:], ps[:, 2, 4 * C:4 * C + B])
            for h in range(2):
                v.tensor_copy(first_T[:, :, h, :], ps[0:C, 3, 0:3 * C].rearrange("p (k c) -> p k c", c=C))
            v.tensor_copy(down_T[:], ps[:, 4, 0:3 * C].rearrange("p (k c) -> p k c", c=C))
            v.tensor_copy(mid_T[:], ps[:, 5, 0:3 * P].rearrange("p (k c) -> p k c", c=P)).then_inc(s["forms_out"], 1)

        def dve_prep_s(dve, l):
            v = nc.vector
            dve.wait_ge(s["s_pe"], l + 1)
            for c in range(4):
                last = v.tensor_scalar(s_all[:, c], ps[:, 2, B * c:B * c + B], mod_b_col[:, c:c + 1], None, ALU.add)
            link(dve, last)
            v.tensor_tensor(s_sq[:], s_all[:], s_all[:], ALU.mult).then_inc(s["sq_ready"], 1)

        def dve_prep_var(dve, l):
            v = nc.vector
            dve.wait_ge(s["d_pe"], l + 1)
            v.tensor_scalar(var[:], ps[:, 4, 0:4 * B].rearrange("p (c b) -> p c b", b=B), CONV_SCALE ** 2, DEMOD_EPS,
                            ALU.mult, ALU.add).then_inc(s["var_ready"], 1)

        def dve_prep_mods(dve, l):
            v = nc.vector
            dve.wait_ge(s["std_ready"], l + 1)
            link(dve, v.reciprocal(d_all[:], std[:]))
            link(dve, v.tensor_tensor(newton[:], d_all[:], d_all[:], ALU.mult))
            link(dve, v.tensor_tensor(newton[:], newton[:], var[:], ALU.mult))
            link(dve, v.tensor_scalar(newton[:], newton[:], -0.5, 1.5, ALU.mult, ALU.add))
            link(dve, v.tensor_tensor(d_all[:], d_all[:], newton[:], ALU.mult))
            v.tensor_copy(mods[:, S0], s_all[:, 0])
            for m, x0, x1 in ((G1, d_all[:, 0], d_all[:, 1]), (G2, s_all[:, 1], s_all[:, 2]), (G3, d_all[:, 2], s_all[:, 3])):
                v.scalar_tensor_tensor(mods[:, m], x0, CONV_SCALE, x1, ALU.mult, ALU.mult)
            v.tensor_scalar(mods[:, DS], d_all[:, 3], CONV_SCALE, None, ALU.mult)
            v.tensor_scalar(mods[:, BT1], d_all[:, 1], bias_col[:, 0:1], None, ALU.mult)
            v.tensor_scalar(mods[:, BT2], s_all[:, 2], bias_col[:, 1:2], 2.0, ALU.mult, ALU.mult)
            link(dve, v.tensor_scalar(mods[:, BT3], s_all[:, 3], bias_col[:, 2:3], None, ALU.mult))
            link(dve, v.tensor_copy(up_bias[:], mods[:, BT2].unsqueeze(2).to_broadcast([P, B, 12])))
            v.tensor_scalar(up_bias[0:C, :, 0:1], up_bias[0:C, :, 0:1], 7.0 / 8.0, None, ALU.mult)
            link(dve, v.tensor_scalar(up_bias[C:P, :, 11:12], up_bias[C:P, :, 11:12], 7.0 / 8.0, None, ALU.mult))
            v.tensor_copy(bias_v[:, 0], mods[:, BT1]).then_inc(s["bias_in"], 1)

        def dve_prep_bias(dve, l, step):
            v = nc.vector
            m, b = ((G2, BT2), (G3, BT3))[step]
            dve.wait_ge(s["bias_pe"], 3 * l + step + 1)
            link(dve, v.tensor_tensor(bias_v[:, 1 - step], ps[:, 2 + 2 * step, 0:B], mods[:, m], ALU.mult))
            v.tensor_tensor(bias_v[:, 1 - step], bias_v[:, 1 - step], mods[:, b], ALU.add).then_inc(s["bias_in"], 1)

        def dve_prep_bias_out(dve, l):
            v = nc.vector
            dve.wait_ge(s["bias_pe"], 3 * l + 3)
            link(dve, v.tensor_tensor(mods[:, CB], ps[:, 2, 0:B], mods[:, DS], ALU.mult))
            link(dve, v.tensor_scalar(mods[:, CB], mods[:, CB], bias_col[:, 3:4], None, ALU.add))
            for q in range(2):
                last = v.memset(fa[q][:, 0:7:6], 0.0)
            last.then_inc(s["mods_ready"], 1)

        DVE_PREP = (dve_prep_forms, dve_prep_transposed, dve_prep_s, dve_prep_var, dve_prep_mods,
                    lambda dve, l: dve_prep_bias(dve, l, 0), lambda dve, l: dve_prep_bias(dve, l, 1), dve_prep_bias_out)

        def dve_mods_pair(dve, l, k, par):
            if l > 0 or not isinstance(k, int):
                dve.wait_ge(s["act_y"], smp(l, k - 2, 1))
            nc.vector.tensor_copy(mods_pair[:, par], mods[:, :, ds(2 * k, 2)]).then_inc(s["dve_mp"], 1)
            dve.wait_ge(s["dve_mp"], pid(l, k) + 1)

        def dve_filter_in(dve, l, k, par):
            for q in range(2):
                dve.wait_ge(s["act_g"], smp(l, k, q))
                nc.vector.scalar_tensor_tensor(gw[q][1][:], first_mov[:], mods_pair[:, par, G1, q:q + 1], f(gw[q][0][:]),
                                               ALU.mult, ALU.subtract).then_inc(s["dve_g"], 1)

        def dve_filter_halves(dve, l, k, q, par):
            dve.wait_ge(s["pe_ab"], smp(l, k, q))
            nc.vector.tensor_copy(fb[q][:], ps[:, 3 + 2 * q, 0:5 * C].rearrange("p (t c) -> p t c", c=C)).then_inc(s["dve_ab"], 1)

        def dve_split_x(dve, l, k):
            dve.wait_ge(s["act_x"], pid(l, k) + 1)
            for (dst, src), (hi, _) in zip(x_parts(l, x_lo), x_parts(l, x_hi)):
                last = nc.vector.tensor_tensor(dst, src, f(hi), ALU.subtract)
            last.then_inc(s["dve_x"], 1)

        def dve_filter(dve, l, k, par):
            for q in range(2):
                dve.wait_ge(s["act_k"], smp(l, k, q))
                nc.vector.scalar_tensor_tensor(filt[q][:, :, 1, 0, :], ps[:, 2 + 2 * q, 0:5 * C].rearrange("p (t c) -> p t c", c=C),
                                               mods_pair[:, par, S0, q:q + 1], f(filt[q][:, :, 0, 0, :]),
                                               ALU.mult, ALU.subtract).then_inc(s["dve_k"], 1)

        def dve_y(dve, l, g, k, q, par):
            dve.wait_ge(s["act_y"], smp(l, k, q))
            dve.wait_ge(s["dve_e"], edge_count(l, g, EDGE_OPS))
            ends = y_nat[q][:].rearrange("p (a b) -> p a b", b=2)[:, 0:M // 2:M // 2 - 1, :]
            nc.vector.tensor_copy(ends, e_y[:, 2 * par + q]).then_inc(s["dve_y"], 1)

        def dve_edge(dve, l, g, stage_no):
            v = nc.vector

            def mod(m, rows, width):
                return mods[rows, m, ds(4 * g, 4)].unsqueeze(2).to_broadcast([rows.stop - rows.start, 4, width])

            def done(ins, step, wait=True):
                ins.then_inc(s["dve_e"], 1)
                if wait:
                    dve.wait_ge(s["dve_e"], edge_count(l, g, step))
            lo_r, all_r = slice(0, C), slice(0, P)
            if stage_no == 0:
                dve.wait_ge(s["e_loaded"], edge_loads(l, g))
                if not (l == 0 and is_zero(g)):
                    dve.wait_ge(s["pe_e"], 4 * (GROUPS * l + g))
                m = mods[lo_r, S0, ds(4 * g, 4)].unsqueeze(2).unsqueeze(3).to_broadcast([C, 4, 2, 4])
                if l == 0:
                    dst = e_x[:, :, 1:17].rearrange("p b (e w) -> p b e w", e=2)
                    for side in range(2):
                        done(v.tensor_tensor(dst[:, :, side], e_in_nat[:, :, side],
                                             mod(S0, lo_r, 8), ALU.mult), side + 1, False)
                    return
                for h in range(2):
                    dst = e_x[:, :, 1:17].rearrange("p b (e m h) -> p b e m h", e=2, h=2)[:, :, :, :, h]
                    done(v.tensor_tensor(dst, e_in[:, h], m, ALU.mult), h + 1, False)
                return
            bank, rows, src_w, dst, mul, add = {
                1: (2, lo_r, 14, e_h[:, :, 1:15], G1, BT1),
                2: (4, all_r, 12, e_z[:, :, 1:13], G2, None),
                3: (7, all_r, 10, e_z2[:, :, 1:11], G3, BT3),
                4: (7, all_r, 4, e_y[:].rearrange("p b e m -> p b (e m)"), DS, None)}[stage_no]
            dve.wait_ge(s["pe_e"], 4 * (GROUPS * l + g) + stage_no)
            src = ps[rows, bank, 0:4 * src_w].rearrange("p (b w) -> p b w", w=src_w)
            first = 2 * stage_no + 1
            done(v.tensor_tensor(dst, src, mod(mul, rows, src_w), ALU.mult), first)
            if add is not None:
                done(v.tensor_tensor(dst, dst, mod(add, rows, src_w), ALU.add), first + 1)
            elif stage_no == 2:
                done(v.tensor_tensor(dst, dst, up_bias[:, ds(4 * g, 4), :], ALU.add), first + 1)
            else:
                done(v.tensor_scalar(dst, dst, bias_col[:, 3:4], None, ALU.add), first + 1)

        def dve_step(dve, l, i, j, more, one_more):
            n = 2 * i + j
            edges = more and j == 0
            nxt = not more and l + 1 < LAYERS
            g_y = i if j == 0 else i + 1
            if more:
                dve_mods_pair(dve, l, n + 2, j)
            if edges:
                dve_edge(dve, l, i + 1, 0)
            for q in range(2 if l > 0 else 0):
                c = slice(C * q, C * q + C)
                dve.wait_ge(s["act_t"], smp(l - 1, n, q))
                if l == 2:
                    src = ps[:, 3 + 2 * q, :].rearrange("p (b c) -> p b c", c=C)
                else:
                    dve.wait_ge(s["act_f"], whole_y(l, n, q))
                    src = y_f[:, :, c]
                nc.vector.tensor_tensor(y_lo[:, :, c], src, f(y_hi[:, :, c]), ALU.subtract).then_inc(s["dve_t"], 1)
            if l == 0 and j == 0 and nxt:
                split_kernel_dve(dve, i)
                dve.wait_ge(s["kernel_dve"], 9)
            if nxt:
                (dve_prep_forms, dve_prep_mods)[j](dve, l + 1)
            if more:
                dve_filter_in(dve, l, n + 2, j)
            if one_more:
                dve_y(dve, l, g_y, n + 1, 0, 1 - j)
            if edges:
                dve_edge(dve, l, i + 1, 1)
            if one_more:
                dve_y(dve, l, g_y, n + 1, 1, 1 - j)
            if edges:
                dve_edge(dve, l, i + 1, 2)
            if l == 0 and j == 0 and not nxt:
                split_kernel_dve(dve, i)
            if l == 1 and j == 0:
                split_mixed_dve(dve, i)
            if more:
                dve_filter_halves(dve, l, n + 2, 0, j)
            if edges:
                dve_edge(dve, l, i + 1, 3)
            if more:
                dve_filter_halves(dve, l, n + 2, 1, j)
            if edges:
                dve_edge(dve, l, i + 1, 4)
            if more:
                dve_split_x(dve, l, n + 2)
            if nxt and j == 0:
                dve_prep_transposed(dve, l + 1)
            ffn_dve(dve, l, i, j)
            if more:
                dve_filter(dve, l, n + 2, j)
            if nxt and j == 0:
                dve_prep_s(dve, l + 1)
                dve_prep_var(dve, l + 1)
            if nxt and j == 1:
                for step in range(2):
                    dve_prep_bias(dve, l + 1, step)
            dve.wait_ge(s["pe_o"], pid(l, n) + 1)
            dve.wait_ge(res_loaded[j], 16 * (i + GROUPS * l + 1))
            ffn_dve_out(dve, l, i, j)
            if l == 0:
                dst, res = x_out[:, j, :], x_res[:, j, :].rearrange("p (m h) -> p h m", h=2)
            else:
                dst, res = x_res[:, j, :], x_res[:, j, :].rearrange("p (h m) -> p h m", h=2)
            nc.vector.tensor_tensor(dst.rearrange("p (h m) -> p h m", h=2), ps[:, 0:2, :], res, ALU.add).then_inc(s["dve_o"], 1)
            if nxt and j == 1:
                dve_prep_bias_out(dve, l + 1)


        def mm3(out, st, mv, first, last, **kw):
            for t, (x0, x1) in enumerate(((0, 0), (1, 0), (0, 1))):
                ins = nc.tensor.matmul(out, st[x0], mv[x1], start=first and t == 0, stop=last and t == 2, **kw)
            return ins

        def pe_prep_forms(pe, l):
            tr = nc.tensor.transpose
            if l == 0:
                pe.wait_ge(s["ident_ready"], 2)
                pe.wait_ge(s["style_loaded"], 16)
            pe.wait_ge(*cond_loaded(l))
            pe.wait_ge(s["conv_forms"], l + 1)
            idc = ident[0:C, 0:C]
            for c in range(4):
                tr(ps[:, 2, C * c:C * c + C], mod_w_nat[:, c, :], idc)
                tr(ps[0:C, 3, C * (3 + c):C * (4 + c)], wsq_nat[:, c, :], idc)
            if l == 0:
                tr(ps[:, 2, 4 * C:4 * C + B], style_nat[:], ident[0:B, 0:B])
            for k in range(TAPS):
                tr(ps[0:C, 3, C * k:C * k + C], tap(w_nat, 0, k)[0:C], idc)
                tr(ps[:, 4, C * k:C * k + C], down_nat[0:C, k].rearrange("p h c -> p (h c)"), idc)
                last = tr(ps[:, 5, P * k:P * k + P], mid_nat[:, k, :], ident[:])
            last.then_inc(s["forms_T"], 1)

        def pe_prep_s(pe, l):
            pe.wait_ge(s["forms_out"], l + 1)
            for c in range(4):
                last = nc.tensor.matmul(ps[:, 2, B * c:B * c + B], mod_w_T[:, c].rearrange("p h c -> p (h c)"), style_T[:],
                                        start=True, stop=True)
            last.then_inc(s["s_pe"], 1)

        def pe_prep_norms(pe, l):
            pe.wait_ge(s["sq_ready"], l + 1)
            for c in range(4):
                last = nc.tensor.matmul(ps[:, 4, B * c:B * c + B], wsq_T[:, c].rearrange("p h c -> p (h c)"), s_sq[0:C, c],
                                        start=True, stop=True)
            last.then_inc(s["d_pe"], 1)

        def pe_prep_bias(pe, l, step):
            mm = nc.tensor.matmul
            pe.wait_ge(s["bias_in"], 3 * l + step + 1)
            if step == 0:
                for k in range(TAPS):
                    last = mm(ps[:, 2, 0:B], up_st[0:C, k].rearrange("p h c -> p (h c)"), bias_v[0:C, 0], start=k == 0, stop=k == 2)
            elif step == 1:
                for k in range(TAPS):
                    last = mm(ps[:, 4, 0:B], mid_T[:, k], bias_v[:, 1], start=k == 0, stop=k == 2)
            else:
                for h in range(2):
                    for k in range(TAPS):
                        last = mm(ps[C * h:C * h + C, 2, 0:B], down_T[:, k], bias_v[:, 0], start=k == 0, stop=k == 2)
            last.then_inc(s["bias_pe"], 1)

        PE_PREP = (pe_prep_forms, pe_prep_s, pe_prep_norms) + tuple(
            lambda pe, l, step=step: pe_prep_bias(pe, l, step) for step in range(3))

        def pe_edge(pe, l, g, stage_no):
            mm = nc.tensor.matmul
            pe.wait_ge(s["dve_e"], edge_count(l, g, 2 * stage_no))
            if stage_no == 4:
                for h in range(2):
                    for k in range(TAPS):
                        rhs = e_z2[:].rearrange("p b (e w) -> p b e w", e=2)[:, :, :, k + h:k + h + 3:2]
                        last = mm(ps[C * h:C * h + C, 7, 0:16].rearrange("p (b e w) -> p b e w", b=4, e=2),
                                  down_T[:, k], rhs, start=k == 0, stop=k == 2)
            else:
                bank, rows, st, src, width = {
                    1: (2, P, [first_T[:, k].rearrange("p h c -> p (h c)") for k in range(3)], e_x, 7),
                    2: (4, P, [up_st[0:C, k].rearrange("p h c -> p (h c)") for k in range(3)], e_h, 6),
                    3: (7, P, [mid_T[:, k] for k in range(3)], e_z, 5)}[stage_no]
                for k in range(TAPS):
                    rhs = src[:].rearrange("p b (e w) -> p b e w", e=2)[:, :, :, k:k + width]
                    last = mm(ps[0:rows, bank, 0:8 * width].rearrange("p (b e w) -> p b e w", b=4, e=2),
                              st[k], rhs, start=k == 0, stop=k == 2)
            last.then_inc(s["pe_e"], 1)

        def pe_filter_halves(pe, l, k, q):
            pe.wait_ge(s["dve_g"], smp(l, k, q))
            up = [t for t in (up_hi, up_lo)]
            o = ps[:, 2 + 2 * q]
            mm3(o[:, 0:4 * C], [t[:, 0] for t in up], [t[:].rearrange("p t c -> p (t c)") for t in gw[q]],
                True, True, skip_group_check=True)
            mm3(o[:, 2 * C:5 * C], [t[:, 1] for t in up], [t[:, 0:3].rearrange("p t c -> p (t c)") for t in gw[q]],
                False, True, skip_group_check=True)
            o = ps[:, 3 + 2 * q]
            for t in range(TAPS):
                last = nc.tensor.matmul(o[:, C * t:C * (t + 3)], mid_nat[:, t], gu[q][:].rearrange("p t c -> p (t c)"),
                                        start=t == 0, stop=True, skip_group_check=True)
            last.then_inc(s["pe_ab"], 1)

        def pe_filter(pe, l, k, samples=(0, 1)):
            for q in samples:
                pe.wait_ge(s["act_ab"], smp(l, k, q))
                pe.wait_ge(s["dve_ab"], smp(l, k, q))
                o = ps[:, 2 + 2 * q]
                for n, j in enumerate((-2, -3, -1, 0, 1, 2)):
                    u = [x for x in (-4, -2, 0, 2, 4) if -2 <= x - j <= 2]
                    b0 = u[0] - j + 2
                    c0 = (u[0] + 4) // 2
                    last = nc.tensor.matmul(o[:, C * c0:C * (c0 + len(u))].rearrange("p (t c) -> p t c", c=C),
                                            fa[q][:, j + 3:j + 5].rearrange("p t c -> p (t c)"),
                                            fb[q][:, b0:b0 + 2 * len(u) - 1:2], start=n == 0, stop=True, skip_group_check=True)
                last.then_inc(s["pe_k"], 1)

        def pe_conv(pe, l, k, q):
            if q == 0:
                pe.wait_ge(s["dve_x"], pid(l, k) + 1)
            pe.wait_ge(filt_shifted[q], 32 * (pid(l, k) + 1))
            for t in range(5):
                st = [filt[q][:, t, r].rearrange("p h c -> p (h c)") for r in range(2)]
                mv = [x[:, q, t:t + M] for x in (x_hi, x_lo)]
                last = mm3(ps[:, 6 + q, :], st, mv, t == 0, t == 4)
            last.then_inc(s["pe_y"], 1)

        def pe_transpose_y(pe, l, k):
            for q in range(2):
                pe.wait_ge(s["dve_y"], smp(l, k, q))
                for t in range(4):
                    last = nc.tensor.transpose(ps[:, 3 + 2 * q, P * t:P * t + P], y_nat[q][:, P * t:P * t + P], ident[:])
                last.then_inc(s["pe_t"], 1)

        def pe_step(pe, l, i, j, more, one_more):
            n = 2 * i + j
            edges = more and j == 0
            pe_transpose_y(pe, l, n)
            if one_more:
                pe_conv(pe, l, n + 1, 0)
            if edges:
                pe_edge(pe, l, i + 1, 1)
            if one_more:
                pe_conv(pe, l, n + 1, 1)
            if edges:
                pe_edge(pe, l, i + 1, 2)
            if l > 0:
                pe.wait_ge(s["dve_t"], smp(l - 1, n, 1))
            if l != 2:
                pe.wait_ge(s["act_f"], whole_y(l, n, 1))
            if more:
                pe_filter_halves(pe, l, n + 2, 0)
            if one_more:
                pe.wait_ge(s["act_y"], smp(l, n + 1, 1))
            if edges:
                pe_edge(pe, l, i + 1, 3)
            if more:
                pe_filter_halves(pe, l, n + 2, 1)
            if edges:
                pe_edge(pe, l, i + 1, 4)
            nxt = not more and l + 1 < LAYERS
            if nxt and j == 0:
                pe_prep_forms(pe, l + 1)
            pe_project(pe, l, i, j)
            pe.wait_ge(s["dve_o"], pid(l, n) + 1)
            if edges:
                pe.wait_ge(s["dve_e"], edge_count(l, i + 1, EDGE_OPS))
            pe_ffn(pe, l, n, 0)
            if nxt and j == 0:
                pe_prep_s(pe, l + 1)
            if nxt and j == 1:
                pe_prep_bias(pe, l + 1, 0)
            if more:
                pe_filter(pe, l, n + 2, (0, 1) if l == 0 else (0,))
            pe_project_T(pe, l, i, j)
            if more and l > 0:
                pe_filter(pe, l, n + 2, (1,))
            pe_ffn(pe, l, n, 1)
            if nxt and j == 0:
                pe_prep_norms(pe, l + 1)
            if nxt and j == 1:
                pe_prep_bias(pe, l + 1, 1)
            pe_tail(pe, l, i, j)
            if nxt and j == 1:
                pe_prep_bias(pe, l + 1, 2)

        def kb_cols(t, kb):
            return t[:, (kb // 2) * 2 * P + kb % 2:(kb // 2 + 1) * 2 * P:2]

        def natural(t):
            return t.rearrange("p (h m) -> p m h", h=2)

        def raw_count(l, t):
            return 16 * (2 * (l - 2) + t // 4 + 1)

        def ffn_load(act, l):
            def small(dst, src):
                act.dma_start(dst, src).then_inc(s["small_loaded"], 16)
            if l == 0:
                small(raw[:, 2], w(0, "ffn_A").rearrange("h r d -> (h r) d"))
                small(tail_raw[0:8], w(0, "ffn_Wr"))
                for ob in range(8):
                    small(nat_b[:, ob, 0:P].rearrange("p (h r) -> p h r", h=8),
                          w(0, "ffn_B")[:, P * ob:P * ob + P, :].rearrange("h o r -> o h r"))
                small(router_b[:], w(0, "ffn_br").partition_broadcast(P))
            if l == 1:
                small(shared_a, w(1, "ffn_lora_A_shared"))
                small(shared_b[:, :, 32:64], w(1, "ffn_lora_B_shared").rearrange("(ob p) r -> p ob r", p=P))
                small(tail_raw[64:65, :], w(1, "ffn_bias").rearrange("(a n) -> a n", a=1))
            if l == 2:
                small(tail_raw[0:28], w(2, "ffn_gate_W"))
                la = w(2, "ffn_lora_A").rearrange("e r d -> (e r) d")
                small(raw[:, 2], la[0:P])
                small(raw[0:96, 3], la[P:224])
                for ob in range(8):
                    small(nat_b[:, ob, :].rearrange("p (e r) -> p e r", r=8),
                          w(2, "ffn_lora_B")[:, P * ob:P * ob + P, :].rearrange("e o r -> o e r"))
            if l == 3:
                for mb in range(4):
                    small(proj_raw[:, 2 * mb:2 * mb + 2, 0:32],
                          w(3, "ffn_A")[2 * P * mb:2 * P * (mb + 1), :].rearrange("(p h) r -> p h r", h=2))
                small(tail_raw[64:65, :], w(3, "ffn_b").rearrange("(a n) -> a n", a=1))
                small(tail_raw[0:32, :], w(3, "ffn_Bmat"))
                small(limes[:], w(3, "ffn_LiMEs"))
            if l >= 2:
                for ob in range(2 if l == 2 else 4):
                    load_wide(act, l, ob)

        SMALL_LOADS = (11, 3, 11, 7)
        shared_a = nat_b[0:32].rearrange("p o c -> p (o c)")[:, 768:768 + L]
        shared_b = nat_b[:].rearrange("p o c -> p (o c)")[:, 0:512].rearrange("p (o c) -> p o c", c=C)

        def small_count(l):
            return 16 * sum(SMALL_LOADS[:l + 1])

        def load_wide(eng, l, t):
            eng.dma_start(raw[:, t % 4, :], w(l, "ffn_base_W" if l == 2 else "ffn_W")[P * t:P * t + P, :]) \
                .then_inc(raw_loaded[t % 4], 16)

        def load_kernel(sp, e):
            sp.wait_ge(s["kernel_dve"], e + 1)
            for h in range(2):
                sp.dma_start(kernel_in[:, h:KB:2], kernel_cols[h, e]).then_inc(s["kernel_loaded"], 16)

        def kernel_eighth(t, e):
            return t[:].rearrange("p k (h m) -> p k m h", h=2)[:, :, ds(C * e, C), :]

        def split_kernel_act(act, e):
            act.wait_ge(s["kernel_loaded"], 32 * e + 32)
            act.wait_ge(s["mix_stored"], 3 * 16)
            nc.scalar.activation(kernel_eighth(w_hi, e), kernel_in.rearrange("p k (m h) -> p k m h", h=2),
                                 ACT.Copy).then_inc(s["kernel_act"], 1)

        def split_kernel_dve(dve, e):
            dve.wait_ge(s["kernel_act"], e + 1)
            nc.vector.tensor_tensor(kernel_eighth(w_lo, e), kernel_in.rearrange("p k (m h) -> p k m h", h=2),
                                    f(kernel_eighth(w_hi, e)), ALU.subtract).then_inc(s["kernel_dve"], 1)

        NARROW_PARTS = (5, 0, 8, 1)
        WIDE_PARTS = (0, 0, 16, 16)

        def part_count(l, n):
            return sum(NARROW_PARTS[:l]) + sum(WIDE_PARTS[:l]) + n + 1

        def narrow_parts(l):
            parts = []
            if l == 0:
                for b, k0 in enumerate(range(0, KB, 3)):
                    kn = min(3, KB - k0)
                    parts.append((proj_0[:, k0:k0 + kn, :], None,
                                  ps[:, 2 + b, 0:PROJ_W[0] * kn].rearrange("p (k w) -> p k w", w=PROJ_W[0])))
            if l == 2:
                width = PROJ_W[l]
                per = 512 // width
                for b, k0 in enumerate(range(0, KB, per)):
                    kn = min(per, KB - k0)
                    parts.append((proj_hi[:, k0:k0 + kn, 0:width], proj_lo[:, k0:k0 + kn, 0:width],
                                  ps[:, 2 + b, 0:width * kn].rearrange("p (k w) -> p k w", w=width)))
            if l in (0, 2):
                for blk, rows in ((0, P),) if l == 0 else ((0, P), (1, 96)):
                    for half in range(2):
                        hi, lo = (natural(t[0:rows, blk])[:, 256 * half:256 * half + 256] for t in (tail_hi, tail_lo))
                        bank = (5 + half) if l == 0 else 2 + 2 * blk + half
                        parts.append((hi, lo, ps[0:rows, bank, :].rearrange("p (m h) -> p m h", h=2)))
            if l == 3:
                parts.append((natural(tail_hi[64:65, 0]), natural(tail_lo[64:65, 0]),
                              tail_raw[64:65, :].rearrange("p (m h) -> p m h", h=2)))
            return parts

        WIDE_BANKS = (0, 1, 3, 5)

        def wide_part(l, n):
            ob, half = n // 2, n % 2
            hi, lo = (t[:, 4 * half:4 * half + 4, :].rearrange("p k (h m) -> p k m h", h=2)[:, :, C * ob:C * ob + C, :] for t in (w_hi, w_lo))
            return hi, lo, ps[:, WIDE_BANKS[n % 4], :].rearrange("p (k m h) -> p k m h", k=4, h=2)

        def ffn_act_prep(act, l):
            def split(part):
                nc.scalar.activation(part[0], part[2], ACT.Copy).then_inc(s["raw_act"], 1)
            if l > 0:
                act.wait_ge(s["pe_o"], pid(l, 0))
            for n, part in enumerate(narrow_parts(l)):
                if l == 3:
                    act.wait_ge(s["small_loaded"], small_count(3))
                elif n == 0:
                    act.wait_ge(s["narrow_pe"], (1, 0, 3)[l])
                elif l == 2 and n == 4:
                    act.wait_ge(s["narrow_pe"], 4)
                    for ob in (2, 3):
                        load_wide(act, 2, ob)
                split(part)
            for n in range(WIDE_PARTS[l]):
                act.wait_ge(s["wide_pe"], 16 * (l - 2) + n + 1)
                split(wide_part(l, n))
                if n % 2 == 1 and n // 2 < 4:
                    load_wide(act, l, n // 2 + 4)
            if l == 1:
                act.wait_ge(s["small_loaded"], small_count(1))
                act.wait_ge(s["shared_ready"], 2)

        def ffn_dve_prep(dve, l):
            v = nc.vector
            base = part_count(l, -1)
            if l == 1:
                v.memset(f(zt_hi[C:C + 1, 0]), 1.0)
                v.memset(f(zt_lo[C:C + 1, 0]), 0.0)
                v.memset(shared_b[:, :, 0:32], 0.0).then_inc(s["shared_ready"], 1)
                dve.wait_ge(s["narrow_pe"], 2)
                v.tensor_copy(proj_raw[:, :, 32:64], ps[:, 2, 0:256].rearrange("p (k r) -> p k r", r=32))
                for half in range(2):
                    last = v.tensor_copy(tail_raw[32:64, 512 * half:512 * half + 512], ps[32:64, 3 + half, :])
                last.then_inc(s["shared_ready"], 1)
            for n, part in enumerate(narrow_parts(l)):
                dve.wait_ge(s["raw_act"], base + n + 1)
                if part[1] is None:
                    dve.sem_inc(s["raw_dve"], 1)
                    continue
                v.tensor_tensor(part[1], part[2], f(part[0]), ALU.subtract).then_inc(s["raw_dve"], 1)

        def dve_wide(dve, l, quarter):
            for n in range(WIDE_PARTS[l] // 4 * quarter, WIDE_PARTS[l] // 4 * (quarter + 1)):
                part = wide_part(l, n)
                dve.wait_ge(s["raw_act"], part_count(l, NARROW_PARTS[l] + n))
                nc.vector.tensor_tensor(part[1], part[2], f(part[0]), ALU.subtract).then_inc(s["raw_dve"], 1)

        def ffn_pe_prep(pe, l):
            tr = nc.tensor.transpose
            if l < 3:
                pe.wait_ge(s["small_loaded"], small_count(l))
            if l == 0:
                for kb in range(KB):
                    b, c = 2 + kb // 3, 136 * (kb % 3)
                    tr(ps[:, b, c:c + P], kb_cols(raw[:, 2], kb), ident[:])
                    tr(ps[:, b, c + P:c + P + 8], kb_cols(tail_raw[0:8], kb), ident[0:8, 0:8])
                for ob in range(8):
                    last = tr(ps[:, 5 + ob // 4, P * (ob % 4):P * (ob % 4) + P], nat_b[:, ob, 0:P], ident[:])
                last.then_inc(s["narrow_pe"], 1)
                pe.wait_ge(s["raw_dve"], part_count(0, 4))
            if l == 1:
                for kb in range(KB):
                    tr(ps[:, 2, 32 * kb:32 * kb + 32], kb_cols(shared_a, kb), ident[0:32, 0:32])
                pe.wait_ge(s["shared_ready"], 1)
                for ob in range(8):
                    last = tr(ps[0:C, 3 + ob // 4, P * (ob % 4):P * (ob % 4) + P], shared_b[:, ob], ident[:])
                last.then_inc(s["narrow_pe"], 1)
                pe.wait_ge(s["shared_ready"], 2)
                pe.wait_ge(s["kernel_dve"], 9)
            if l == 2:
                for kb in range(KB):
                    b, c = 2 + kb // 2, 252 * (kb % 2)
                    tr(ps[:, b, c:c + 28], kb_cols(tail_raw[0:28], kb), ident[0:28, 0:28])
                    tr(ps[:, b, c + 28:c + 28 + P], kb_cols(raw[:, 2], kb), ident[:])
                    last = tr(ps[:, b, c + 28 + P:c + 252], kb_cols(raw[0:96, 3], kb), ident[0:96, 0:96])
                last.then_inc(s["narrow_pe"], 1)
                pe.wait_ge(s["raw_dve"], part_count(2, 3))
                for ob in range(8):
                    c = P * (ob % 4)
                    tr(ps[:, 2 + ob // 4, c:c + P], nat_b[:, ob, 0:P], ident[:])
                    last = tr(ps[0:96, 4 + ob // 4, c:c + P], nat_b[:, ob, P:224], ident[:])
                last.then_inc(s["narrow_pe"], 1)
            if l >= 2:
                pe.wait_ge(s["raw_dve"], part_count(l, NARROW_PARTS[l] - 1))
                pe.wait_ge(s["dve_o"], pid(l, 0) + 1)

        def pe_wide(pe, l, quarter):
            if l < 2:
                return
            for ob in (2 * quarter, 2 * quarter + 1):
                pe.wait_ge(raw_loaded[ob % 4], raw_count(l, ob))
                for half in range(2):
                    n = 2 * ob + half
                    if n >= 4:
                        pe.wait_ge(s["raw_dve"], part_count(l, NARROW_PARTS[l] + n - 4))
                    for k in range(4):
                        last = nc.tensor.transpose(ps[:, WIDE_BANKS[n % 4], P * k:P * k + P],
                                                   kb_cols(raw[:, ob % 4], 4 * half + k), ident[:])
                    last.then_inc(s["wide_pe"], 1)
            if quarter == 3:
                pe.wait_ge(s["raw_dve"], part_count(l, NARROW_PARTS[l] + 15))

        def mix_loads(act):
            for g in range(4):
                act.dma_start(mix_a[:, g], w(1, "ffn_lora_A")[4 * g:4 * g + 4].rearrange("n r d -> (n r) d")).then_inc(s["mix_loaded"], 16)
                act.dma_start(gate_col[32 * g:32 * g + 32], w(1, "ffn_gate").rearrange("b (g n) -> n (b g)", n=4)[g]
                              .partition_broadcast(32), allow_slow_non_contiguous=True).then_inc(s["mix_loaded"], 16)
            for ob in range(8):
                act.dma_start(mix_b[:, ob], w(1, "ffn_lora_B")[:, P * ob:P * ob + P, :].rearrange("n o r -> o n r")).then_inc(s["mix_loaded"], 16)

        MIX_LOADS = 16 * 16

        def mix_dve(dve):
            v = nc.vector
            dve.wait_ge(s["mix_loaded"], MIX_LOADS)
            dve.wait_ge(s["ident_ready"], 2)
            link(dve, v.tensor_reduce(same_rank[:], ident[:].rearrange("p (n r) -> p r n", n=4), AX_X, ALU.add))
            for g in range(4):
                last = v.tensor_tensor(gate_mat[:, g], gate_col[:].rearrange("p (b g) -> p g b", g=4)[:, g].unsqueeze(2).to_broadcast([P, 8, 32]),
                                       same_rank[:].unsqueeze(1).to_broadcast([P, 8, 32]), ALU.mult)
            last.then_inc(s["mix_dve"], 1)
            for half in range(2):
                for g in range(4):
                    dve.wait_ge(s["mix_pe"], 4 * half + g + 1)
                    v.tensor_copy(mix_bt[:, g, 512 * half:512 * half + 512], ps[:, 2 + g, :]).then_inc(s["mix_dve"], 1)
            for t in range(4):
                dve.wait_ge(s["mix_pe"], 8 + t + 1)
                v.tensor_copy(mixed_a[:, :, 2 * t:2 * t + 2, :],
                              ps[:, 2 + t, :].rearrange("p (k b r) -> p b k r", k=2, b=8)).then_inc(s["mix_dve"], 1)
            for t in range(4):
                dve.wait_ge(s["mix_pe"], 12 + t + 1)
                v.tensor_copy(mixed_b[:, t // 2, 512 * (t % 2):512 * (t % 2) + 512], ps[:, 2 + t, :]).then_inc(s["mix_dve"], 1)

        def mix_pe(pe):
            mm, tr = nc.tensor.matmul, nc.tensor.transpose
            pe.wait_ge(s["mix_loaded"], MIX_LOADS)
            pe.wait_ge(s["mix_dve"], 1)
            for half in range(2):
                for g in range(4):
                    if half:
                        pe.wait_ge(s["mix_dve"], 1 + g + 1)
                    for ob in range(4):
                        last = tr(ps[:, 2 + g, P * ob:P * ob + P],
                                  mix_b[:, 4 * half + ob, 4 * g:4 * g + 4, :].rearrange("p n r -> p (n r)"), ident[:])
                    last.then_inc(s["mix_pe"], 1)
            for t in range(4):
                pe.wait_ge(s["mix_dve"], 1 + 4 + t + 1)
                for k in range(2):
                    for g in range(4):
                        last = mm(ps[:, 2 + t, 256 * k:256 * k + 256], kb_cols(mix_a[:, g], 2 * t + k),
                                  gate_mat[:, g].rearrange("p b r -> p (b r)"), start=g == 0, stop=g == 3)
                last.then_inc(s["mix_pe"], 1)
            for t in range(4):
                pe.wait_ge(s["mix_dve"], 9 + t + 1)
                for g in range(4):
                    last = mm(ps[:, 2 + t, :], gate_mat[:, g, 4 * (t // 2):4 * (t // 2) + 4].rearrange("p b r -> p (b r)"),
                              mix_bt[:, g, 512 * (t % 2):512 * (t % 2) + 512], start=g == 0, stop=g == 3)
                last.then_inc(s["mix_pe"], 1)
            pe.wait_ge(s["mix_dve"], 17)

        def mix_store(sp):
            sp.wait_ge(s["mix_dve"], 13)
            sp.dma_start(mixed_a_dram.rearrange("b p w -> p b w"), mixed_a[:].rearrange("p b k r -> p b (k r)")).then_inc(s["mix_stored"], 16)
            sp.wait_ge(s["mix_dve"], 17)
            for t in range(2):
                sp.dma_start(mixed_b_dram[4 * t:4 * t + 4].rearrange("b r n -> (b r) n"), mixed_b[:, t]).then_inc(s["mix_stored"], 16)

        def load_mixed(sp, g):
            if not is_zero(g):
                sp.wait_ge(s["mixed_dve"], g)
                sp.wait_ge(s["pe_z"], pid(1, 2 * g))
            sp.dma_start(proj_raw[:, :, 0:32], mixed_a_dram[g].rearrange("p (k r) -> p k r", r=32)).then_inc(s["mixed_loaded"], 16)
            sp.dma_start(tail_raw[0:32, :], mixed_b_dram[g]).then_inc(s["mixed_loaded"], 16)

        def split_mixed_act(act, g):
            act.wait_ge(s["mixed_loaded"], 32 * g + 32)
            act.wait_ge(s["pe_o"], pid(1, 2 * g))
            nc.scalar.activation(natural(tail_hi[0:65, 0]), tail_raw[0:65, :].rearrange("p (m h) -> p m h", h=2),
                                 ACT.Copy).then_inc(s["mixed_act"], 1)

        def split_mixed_dve(dve, g):
            dve.wait_ge(s["mixed_act"], g + 1)
            nc.vector.tensor_tensor(natural(tail_lo[0:65, 0]), tail_raw[0:65, :].rearrange("p (m h) -> p m h", h=2),
                                    f(natural(tail_hi[0:65, 0])), ALU.subtract).then_inc(s["mixed_dve"], 1)

        def zc(l, n, step):
            return sum(PAIRS * x for x in Z_OPS[:l]) + Z_OPS[l] * n + step

        ZT_ROWS = ((P,), (64,), (P, 96), (32,))

        def ffn_act(act, l, i, j):
            n = 2 * i + j
            if l == 0:
                act.wait_ge(s["dve_z"], zc(l, n, 2))
                nc.scalar.activation(z_small[:, 16:24], z_small[:, 0:8], ACT.Exp, bias=z_small[:, 8:9],
                                     accum_out=z_small[:, 9:10]).then_inc(s["act_z"], 1)
            if l == 2:
                act.wait_ge(s["dve_z"], zc(l, n, 3))
                nc.scalar.activation(z_small[:, 41:42], z_small[:, 40:41], ACT.Exp).then_inc(s["act_z"], 1)
            if l == 3:
                return
            act.wait_ge(s["pe_zt"], pid(l, n) + 1)
            for b, rows in enumerate(ZT_ROWS[l]):
                last = nc.scalar.activation(zt_hi[0:rows, b, :], ps[0:rows, 7, P * b:P * b + P], ACT.Copy)
            last.then_inc(s["act_zt"], 1)

        def ffn_dve(dve, l, i, j):
            n = 2 * i + j
            v = nc.vector

            def done(ins, step):
                ins.then_inc(s["dve_z"], 1)
                dve.wait_ge(s["dve_z"], zc(l, n, step))

            dve.wait_ge(s["pe_z"], pid(l, n) + 1)
            if l == 0:
                done(v.tensor_tensor(z_small[:, 0:8], ps[:, 6, P:P + 8], router_b[:], ALU.add), 1)
                done(v.tensor_reduce(z_small[:, 8:9], z_small[:, 0:8], AX_X, ALU.max, negate=True), 2)
                dve.wait_ge(s["act_z"], n + 1)
                done(v.reciprocal(z_small[:, 10:11], z_small[:, 9:10]), 3)
                done(v.tensor_scalar(z_small[:, 11:12], z_small[:, 10:11], 16.0, None, ALU.mult), 4)
                done(v.scalar_tensor_tensor(z_sb[:, 0:P].rearrange("p (h r) -> p h r", h=8),
                                            ps[:, 6, 0:P].rearrange("p (h r) -> p h r", h=8), z_small[:, 11:12],
                                            z_small[:, 16:24].unsqueeze(2).to_broadcast([P, 8, 16]), ALU.mult, ALU.mult), 5)
            if l in (1, 3):
                done(v.tensor_copy(z_sb[:, 0:PROJ_W[l]], ps[:, 6, 0:PROJ_W[l]]), 1)
            if l == 2:
                lg, first, second = z_small[:, 0:28], z_small[:, 32:33], z_small[:, 33:34]
                diff, e2, den, p1, p2, apart = (z_small[:, c:c + 1] for c in range(40, 46))
                above, equal, seen, keep = (z_small[:, c:c + 28] for c in (48, 76, 104, 132))
                v.tensor_copy(lg, ps[:, 6, 0:28]).then_inc(s["dve_z"], 1)
                done(v.max(z_small[:, 32:40], ps[:, 6, 0:28]), 2)
                done(v.tensor_tensor(diff, second, first, ALU.subtract), 3)
                done(v.tensor_scalar(above, lg, second, None, ALU.is_gt), 4)
                done(v.tensor_scalar(equal, lg, second, None, ALU.is_equal), 5)
                done(v.tensor_tensor_scan(seen, ones[:, 0:28], equal, 0.0, ALU.mult, ALU.add), 6)
                done(v.tensor_tensor(apart, first, second, ALU.is_gt), 7)
                done(v.tensor_scalar(keep, seen, apart, 2.0, ALU.add, ALU.is_le), 8)
                done(v.tensor_tensor(keep, keep, equal, ALU.mult), 9)
                dve.wait_ge(s["act_z"], PAIRS + n + 1)
                done(v.tensor_scalar(den, e2, 1.0, None, ALU.add), 10)
                done(v.reciprocal(den, den), 11)
                done(v.tensor_scalar(p1, den, 2.0, None, ALU.mult), 12)
                done(v.tensor_tensor(p2, e2, p1, ALU.mult), 13)
                done(v.tensor_scalar(above, above, p1, None, ALU.mult), 14)
                done(v.scalar_tensor_tensor(above, keep, p2, above, ALU.mult, ALU.add), 15)
                done(v.tensor_tensor(z_sb[:, 0:224].rearrange("p (e r) -> p e r", r=8),
                                     ps[:, 6, 28:252].rearrange("p (e r) -> p e r", r=8),
                                     above.unsqueeze(2).to_broadcast([P, 28, 8]), ALU.mult), 16)
            if l == 3:
                dve.wait_ge(s["pe_zt"], pid(l, n) + 1)
                v.tensor_copy(zt_nat[:, ds(P * n, P)], ps[0:32, 7, 0:P]).then_inc(s["dve_zt"], 1)
                return
            dve.wait_ge(s["act_zt"], pid(l, n) + 1)
            for b, rows in enumerate(ZT_ROWS[l]):
                last = v.tensor_tensor(zt_lo[0:rows, b, :], ps[0:rows, 7, P * b:P * b + P], f(zt_hi[0:rows, b, :]), ALU.subtract)
            last.then_inc(s["dve_zt"], 1)

        def ffn_dve_out(dve, l, i, j):
            if l == 3:
                n = 2 * i + j
                nc.vector.tensor_copy(h_slice[:, ds(n, 1), :].rearrange("p a (m h) -> p (a h) m", h=2), ps[:, 0:2, 0:4])

        def pe_project(pe, l, i, j):
            n = 2 * i + j
            if l == 1 and j == 0:
                pe.wait_ge(s["mixed_loaded"], 32 * i + 32)
                pe.wait_ge(s["mixed_dve"], i + 1)
            if l != 2:
                proj = proj_0 if l == 0 else proj_raw
                for kb in range(KB):
                    last = nc.tensor.matmul(ps[:, 6, 0:PROJ_W[l]], y_f[:, kb], proj[:, kb, 0:PROJ_W[l]],
                                            start=kb == 0, stop=kb == KB - 1)
                last.then_inc(s["pe_z"], 1)
                return
            for kb in range(KB):
                last = mm3(ps[:, 6, 0:PROJ_W[l]], [t[:, kb] for t in (y_hi, y_lo)],
                           [t[:, kb, 0:PROJ_W[l]] for t in (proj_hi, proj_lo)], kb == 0, kb == KB - 1)
            last.then_inc(s["pe_z"], 1)

        def pe_ffn(pe, l, n, h):
            if l == 0:
                return
            for kb in range(KB):
                mm3(ps[:, h, :], [t[:, kb] for t in (y_hi, y_lo)], [t[:, kb, M * h:M * h + M] for t in (w_hi, w_lo)],
                    kb == 0, False)

        def pe_project_T(pe, l, i, j):
            n = 2 * i + j
            pe.wait_ge(s["dve_z"], zc(l, n, Z_OPS[l]))
            for b in range(len(ZT_ROWS[l])):
                last = nc.tensor.transpose(ps[:, 7, P * b:P * b + P], z_sb[:, P * b:P * b + P], ident[:])
            last.then_inc(s["pe_zt"], 1)

        def pe_tail(pe, l, i, j):
            n = 2 * i + j
            pe.wait_ge(s["dve_zt"], pid(l, n) + 1)
            if l == 3:
                pe.wait_ge(s["bias_row"], 16)
            for h in range(2):
                cols = slice(M * h, M * h + M)
                if l == 3:
                    last = nc.tensor.matmul(ps[:, h, :], two_ones[64:66], tail_hi[64:66, 0, cols], start=False, stop=True)
                    continue
                rows = (P,) if l == 0 else (65,) if l == 1 else (P, 96)
                for b, r in enumerate(rows):
                    last = mm3(ps[:, h, :], [t[0:r, b] for t in (zt_hi, zt_lo)], [t[0:r, b, cols] for t in (tail_hi, tail_lo)],
                               l == 0, b == len(rows) - 1)
            last.then_inc(s["pe_o"], 1)

        def join_bias(sp):
            sp.wait_ge(s["raw_dve"], part_count(3, 0))
            sp.dma_start(f(tail_hi[65:66, 0, :]), f(tail_lo[64:65, 0, :])).then_inc(s["bias_row"], 16)

        def final_dve(dve):
            v = nc.vector
            hs = h_slice[:].rearrange("p n e -> p (n e)")
            dve.wait_ge(s["limes_pe"], 1)
            v.tensor_copy(limes_T[:], ps[0:32, 3, 0:8]).then_inc(s["limes_ready"], 1)
            v.tensor_copy(to_anchor[:].rearrange("p (a t) -> p a t", t=2), ident[:, 1:P:2].unsqueeze(2).to_broadcast([P, C, 2]))
            v.tensor_reduce(odd[:], ident[:, 1:P:2], AX_X, ALU.add)
            dve.wait_ge(s["bm_act"], 1)
            v.scalar_tensor_tensor(natural(bm_lo[:]), tail_raw[0:32].rearrange("p (m h) -> p m h", h=2), 0.5,
                                   f(natural(bm_hi[:])), ALU.mult, ALU.subtract).then_inc(s["bm_ready"], 1)
            dve.wait_ge(s["fin_pe"], 1)
            link(dve, v.tensor_copy(d_slice[:].rearrange("p n e -> p (n e)"), ps[:, 2, 0:P]))
            link(dve, v.tensor_reduce(maxes[:, 0:1], hs, AX_X, ALU.max, apply_absolute_value=True))
            link(dve, v.tensor_reduce(maxes[:, 1:2], d_slice[:].rearrange("p n e -> p (n e)"), AX_X, ALU.max, apply_absolute_value=True))
            v.tensor_scalar(maxes[:, 2:4], maxes[:, 0:2], odd[:], None, ALU.mult).then_inc(s["fin_dve"], 1)
            dve.wait_ge(s["fin_pool"], 1)
            link(dve, v.tensor_scalar(maxes[:, 6:8], maxes[:, 4:6], 1e-6, None, ALU.max))
            link(dve, v.reciprocal(maxes[:, 6:8], maxes[:, 6:8]))
            link(dve, v.tensor_scalar(maxes[:, 6:8], maxes[:, 6:8], 0.5, None, ALU.mult))
            link(dve, v.tensor_scalar(hs, hs, maxes[:, 6:7], None, ALU.mult))
            lgs = route[:, 0]
            link(dve, v.scalar_tensor_tensor(lgs, d_slice[:].rearrange("p n e -> p (n e)"), maxes[:, 7:8], hs, ALU.mult, ALU.add))

            def per(t):
                return t.rearrange("p (n e) -> p n e", e=8)

            def bc(c):
                return col[:, c].unsqueeze(2).to_broadcast([P, PAIRS, 8])
            link(dve, v.tensor_reduce(col[:, 0], per(lgs), AX_X, ALU.max))
            v.tensor_tensor(per(route[:, 1]), per(lgs), bc(0), ALU.subtract).then_inc(s["fin_dve"], 1)
            dve.wait_ge(s["fin_act"], 1)
            link(dve, v.tensor_reduce(col[:, 1], per(route[:, 2]), AX_X, ALU.add))
            link(dve, v.reciprocal(col[:, 1], col[:, 1]))
            link(dve, v.tensor_tensor(per(route[:, 3]), per(route[:, 2]), bc(1), ALU.mult))
            for n in range(PAIRS):
                last = v.max(per(route[:, 4])[:, n], per(route[:, 3])[:, n])
            link(dve, last)
            link(dve, v.tensor_copy(col[:, 2], per(route[:, 4])[:, :, 1]))
            v.tensor_tensor(per(route[:, 5]), per(route[:, 3]), bc(2), ALU.subtract).then_inc(s["fin_dve"], 1)
            dve.wait_ge(s["fin_act"], 2)
            link(dve, v.tensor_scalar(route[:, 6], route[:, 6], 1.0, None, ALU.add))
            link(dve, v.reciprocal(route[:, 6], route[:, 6]))
            link(dve, v.tensor_tensor(route[:, 7], route[:, 3], route[:, 6], ALU.mult))
            link(dve, v.tensor_reduce(col[:, 3], per(route[:, 7]), AX_X, ALU.add))
            link(dve, v.tensor_scalar(col[:, 3], col[:, 3], 1e-9, None, ALU.add))
            link(dve, v.reciprocal(col[:, 3], col[:, 3]))
            v.tensor_tensor(per(route[:, 8]), per(route[:, 7]), bc(3), ALU.mult).then_inc(s["fin_dve"], 1)
            for t in range(4):
                dve.wait_ge(s["fin_pe"], 2 + t)
                v.tensor_copy(w_T[:, 512 * t:512 * t + 512], ps[0:8, 2 + t, :]).then_inc(s["fin_dve"], 1)
            for t in range(4):
                c = slice(512 * t, 512 * t + 512)
                dve.wait_ge(s["fin_pe"], 6 + t)
                link(dve, v.tensor_tensor(zt_nat[:, c], zt_nat[:, c], ps[0:32, 2 + t, :], ALU.mult))
                link(dve, v.tensor_copy(zp_hi[:, c], zt_nat[:, c]))
                v.tensor_tensor(zp_lo[:, c], zt_nat[:, c], f(zp_hi[:, c]), ALU.subtract).then_inc(s["fin_dve"], 1)
            for n in range(PAIRS):
                dve.wait_ge(s["fin_o"], n + 1)
                dve.wait_ge(fin_loaded[n % X_LAST], 16 * (n // X_LAST + 1))
                if n >= 2:
                    dve.wait_ge(fin_stored[n % 2], 16 * (n // 2))
                b = 2 * (n % 2)
                v.tensor_tensor(stage[:, n % 2].rearrange("p (m h) -> p h m", h=2), ps[:, b:b + 2, :],
                                x_last[:, n % X_LAST].rearrange("p (h m) -> p h m", h=2), ALU.add).then_inc(s["fin_x"], 1)

        def final_act(act):
            act.wait_ge(s["pe_o"], pid(LAYERS, 0))
            nc.scalar.activation(natural(bm_hi[:]), tail_raw[0:32].rearrange("p (m h) -> p m h", h=2), ACT.Copy,
                                 scale=0.5).then_inc(s["bm_act"], 1)
            act.wait_ge(s["fin_dve"], 2)
            nc.scalar.activation(route[:, 2], route[:, 1], ACT.Exp).then_inc(s["fin_act"], 1)
            act.wait_ge(s["fin_dve"], 3)
            nc.scalar.activation(route[:, 6], route[:, 5], ACT.Exp, scale=-2.0).then_inc(s["fin_act"], 1)

        def final_pool(gp):
            gp.wait_ge(s["fin_dve"], 1)
            gp.partition_all_reduce(maxes[:, 4:6], maxes[:, 2:4], P, RMAX).then_inc(s["fin_pool"], 1)

        def final_pe(pe):
            mm = nc.tensor.matmul
            pe.wait_ge(s["dve_zt"], pid(LAYERS, 0))
            nc.tensor.transpose(ps[0:32, 3, 0:8], limes[:], ident[0:8, 0:8]).then_inc(s["limes_pe"], 1)
            pe.wait_ge(s["limes_ready"], 1)
            for n in range(PAIRS):
                last = mm(ps[:, 2, 8 * n:8 * n + 8], zt_nat[:, P * n:P * n + P], limes_T[:], start=True, stop=True)
            last.then_inc(s["fin_pe"], 1)
            pe.wait_ge(s["fin_dve"], 4)
            for t in range(4):
                for n in range(4 * t, 4 * t + 4):
                    last = mm(ps[0:8, 2 + t, P * (n % 4):P * (n % 4) + P], route[:, 8, 8 * n:8 * n + 8], to_anchor[:], start=True, stop=True)
                last.then_inc(s["fin_pe"], 1)
            for t in range(4):
                pe.wait_ge(s["fin_dve"], 5 + t)
                mm(ps[0:32, 2 + t, :], limes[:], w_T[:, 512 * t:512 * t + 512], start=True, stop=True).then_inc(s["fin_pe"], 1)
            for n in range(PAIRS):
                pe.wait_ge(s["fin_dve"], 9 + n // 4)
                if n >= 2:
                    pe.wait_ge(s["fin_x"], n - 1)
                else:
                    pe.wait_ge(s["dve_o"], pid(LAYERS, 0) + 1)
                    pe.wait_ge(s["bm_ready"], 1)
                    pe.wait_ge(s["fin_dve"], 12)
                for h in range(2):
                    last = mm3(ps[:, 2 * (n % 2) + h, :], [t[:, P * n:P * n + P] for t in (zp_hi, zp_lo)],
                               [t[:, M * h:M * h + M] for t in (bm_hi, bm_lo)], True, True)
                last.then_inc(s["fin_o"], 1)

        def final_sp(sp):
            for n in range(X_LAST):
                final_load(sp, n)
            for n in range(PAIRS):
                sp.wait_ge(s["fin_x"], n + 1)
                sp.dma_start(out_rows[n], stage[:, n % 2]).then_inc(fin_stored[n % 2], 16)
                if n + X_LAST < PAIRS:
                    final_load(sp, n + X_LAST)
            for q in range(2):
                sp.wait_ge(fin_stored[q], 16 * (PAIRS // 2))

        def final_load(sp, n):
            sp.dma_start(x_last[:, n % X_LAST], xs_rows[n]).then_inc(fin_loaded[n % X_LAST], 16)

        @block.sync
        def _(sp):
            load_cond_weights(sp, 0)
            load_cond_rest(sp, 0)
            mix_store(sp)
            for l in range(LAYERS):
                sp_load_x(sp, l, 0)
                sp_shift_filter(sp, l, 0)
                sp_load_x(sp, l, 1)
                sp_shift_filter(sp, l, 1)
                if l == 1:
                    load_mixed(sp, 0)
                if l == 3:
                    join_bias(sp)
                with sp.Fori(0, GROUPS - 1) as i:
                    for j in range(2):
                        sp_step(sp, l, i, j, True)
                for j in range(2):
                    sp_step(sp, l, GROUPS - 1, j, False)
            for q in range(2):
                sp.wait_ge(stored[q], 16 * (GROUPS * LAYERS + 1))
            final_sp(sp)

        @block.gpsimd
        def _(gp):
            gp.memset(ident[:], 0.0).then_inc(s["ident_ready"], 1)
            gp.wait_ge(s["ident_ready"], 1)
            gp.affine_select(out=ident[:], in_=ident[:], compare_op=ALU.not_equal, fill=1.0, base=0,
                             pattern=[[-1, P]], channel_multiplier=1).then_inc(s["ident_ready"], 1)
            for l in range(LAYERS):
                pool_load_edge(gp, l, 0)
                if l + 1 < LAYERS:
                    load_cond_weights(gp, l + 1)
                with gp.Fori(0, GROUPS - 1) as i:
                    pool_load_edge(gp, l, i + 1)
                if l + 1 < LAYERS:
                    load_cond_rest(gp, l + 1)
            final_pool(gp)

        @block.scalar
        def _(act):
            act.dma_start(style_nat[:], a["cond_512"]).then_inc(s["style_loaded"], 16)
            ffn_load(act, 0)
            mix_loads(act)
            for q in range(2):
                act.sem_inc(stored[q], 16)
            for l in range(LAYERS):
                if l == 0:
                    act_root(act, l)
                ffn_act_prep(act, l)
                act_filter_in(act, l, 0, 0)
                act_filter_halves(act, l, 0, 0)
                act_split_x(act, l, 0)
                act_filter(act, l, 0, 0)
                act_filter_in(act, l, 1, 1)
                act_y(act, l, 0, 0)
                act_filter_halves(act, l, 1, 1)
                act_split_x(act, l, 1)
                act_filter(act, l, 1, 1)
                with act.Fori(0, GROUPS - 1) as i:
                    for j in range(2):
                        act_step(act, l, i, j, True, True)
                for j in range(2):
                    act_step(act, l, GROUPS - 1, j, False, j == 0)
            final_act(act)

        @block.vector
        def _(dve):
            dve.sem_inc(s["dve_o"], 1)
            dve.sem_inc(s["kernel_dve"], 1)
            for t in (x_hi, x_lo):
                nc.vector.memset(f(t[:]), 0.0)
            for q in range(2):
                nc.vector.memset(f(filt[q][:]), 0.0)
            for t in (fa[0], fa[1], e_x, e_h, e_z, e_z2, first_mov, mid_nat):
                nc.vector.memset(t[:], 0.0)
            for t in (up_hi, up_lo):
                nc.vector.memset(f(t[:]), 0.0)
            for t in (ones, two_ones):
                nc.vector.memset(f(t[:]), 1.0)
            link(dve, nc.vector.memset(z_sb[:], 0.0))
            for l in range(LAYERS):
                if l == 0:
                    for part in DVE_PREP:
                        part(dve, 0)
                ffn_dve_prep(dve, l)
                if l == 0:
                    mix_dve(dve)
                dve_mods_pair(dve, l, 0, 0)
                dve_edge(dve, l, 0, 0)
                for stage_no in range(1, 5):
                    dve_edge(dve, l, 0, stage_no)
                    dve_wide(dve, l, stage_no - 1)
                dve_filter_in(dve, l, 0, 0)
                dve_filter_halves(dve, l, 0, 0, 0)
                dve_filter_halves(dve, l, 0, 1, 0)
                dve_split_x(dve, l, 0)
                dve_filter(dve, l, 0, 0)
                dve_mods_pair(dve, l, 1, 1)
                dve_filter_in(dve, l, 1, 1)
                dve_y(dve, l, 0, 0, 0, 0)
                dve_y(dve, l, 0, 0, 1, 0)
                dve_filter_halves(dve, l, 1, 0, 1)
                dve_filter_halves(dve, l, 1, 1, 1)
                dve_split_x(dve, l, 1)
                dve_filter(dve, l, 1, 1)
                with dve.Fori(0, GROUPS - 1) as i:
                    for j in range(2):
                        dve_step(dve, l, i, j, True, True)
                for j in range(2):
                    dve_step(dve, l, GROUPS - 1, j, False, j == 0)
            final_dve(dve)

        @block.tensor
        def _(pe):
            for l in range(LAYERS):
                if l == 0:
                    for part in PE_PREP:
                        part(pe, 0)
                pe.wait_ge(s["mods_ready"], l + 1)
                ffn_pe_prep(pe, l)
                if l == 0:
                    mix_pe(pe)
                for stage_no in range(1, 5):
                    pe_edge(pe, l, 0, stage_no)
                    pe_wide(pe, l, stage_no - 1)
                pe_filter_halves(pe, l, 0, 0)
                pe_filter_halves(pe, l, 0, 1)
                pe_filter(pe, l, 0)
                pe_conv(pe, l, 0, 0)
                pe_conv(pe, l, 0, 1)
                pe_filter_halves(pe, l, 1, 0)
                pe_filter_halves(pe, l, 1, 1)
                pe_filter(pe, l, 1)
                with pe.Fori(0, GROUPS - 1) as i:
                    for j in range(2):
                        pe_step(pe, l, i, j, True, True)
                for j in range(2):
                    pe_step(pe, l, GROUPS - 1, j, False, j == 0)
            final_pe(pe)


def kernel(**inputs):
    import numpy as np
    import concourse.bacc as bacc
    from concourse.bass_utils import run_bass_kernel_spmd

    nc = bacc.Bacc("TRN2", target_bir_lowering=False, num_devices=1)
    arrays, args = {}, {}
    for name in inputs:
        arr = np.ascontiguousarray(inputs[name])
        arrays["in_" + name] = arr
        args[name] = nc.dram_tensor("in_" + name, arr.shape, mybir.dt.from_np(arr.dtype), kind="ExternalInput").ap()
    out = nc.dram_tensor("out_x", (B, C, L), F32, kind="ExternalOutput").ap()
    build(nc, args, out)
    r = run_bass_kernel_spmd(nc, [arrays], core_ids=[0])
    return r.results[0]["out_x"]
```
